# Optimizing a Trainium2 kernel written in Bass

```python
import numpy as np
import jax
import jax.numpy as jnp

def _softmax(x, axis=-1):
    return jax.nn.softmax(x, axis=axis)

def _gelu(x):
    return jax.nn.gelu(x, approximate=True)

def _silu(x):
    return jax.nn.silu(x)

def _sigmoid(x):
    return jax.nn.sigmoid(x)

def _layernorm(x, axis=-1, eps=1e-05):
    m = jnp.mean(x, axis=axis, keepdims=True)
    v = jnp.var(x, axis=axis, keepdims=True)
    return (x - m) / jnp.sqrt(v + eps)

def _scatter_add(tgt, idx, src, axis=0):
    return tgt.at[idx].add(src)

def _segment_sum(src, seg, n):
    return jax.ops.segment_sum(src, seg, n)
kernel_name = 'mk_flamingo_gated_d1_seqx_r4_3bbf6c'

def setup_inputs(seed: int=0):
    np.random.seed(seed)
    _w = jnp.asarray

    def _rec_inputs():
        import jax
        import jax.numpy as jnp
        _rk = jax.random.key(seed)
        x = -0.0002928 + 1 * jax.random.normal(jax.random.fold_in(_rk, 1), (16, 256, 256), jnp.float32)
        _lenS = 256 - jax.random.randint(jax.random.fold_in(_rk, 7), (16,), 0, max(1, 256 // 4) + 1, jnp.int32)
        _lenS2 = 256 - jax.random.randint(jax.random.fold_in(_rk, 8), (16,), 0, max(1, 256 // 4) + 1, jnp.int32)
        _ctx_1024P = jax.random.normal(jax.random.fold_in(_rk, 11), (16, 16, 256), jnp.float32)
        _ctx_1024c = jax.random.dirichlet(jax.random.fold_in(_rk, 511), 0.3 * jnp.ones((16,), jnp.float32), (16, 256))
        _ctx_1024t = jnp.einsum('bsk,bkd->bsd', _ctx_1024c, _ctx_1024P)
        _ctx_1024t = _ctx_1024t * jax.lax.rsqrt(jnp.mean(jnp.square(_ctx_1024t)) + 1e-12) * 0.953939
        ctx_1024 = -1.39393e-06 + 0.999914 * (_ctx_1024t + 0.3 * jax.random.normal(jax.random.fold_in(_rk, 611), (16, 256, 256), jnp.float32))
        _g = jax.random.normal(jax.random.fold_in(_rk, 9001), (2, 1), jnp.float32)
        _g = jnp.sign(_g) * jnp.maximum(jnp.abs(_g), 1.0) + (_g == 0) * 1.0
        g_xattn = _g[0]
        g_ffn = _g[1]
        return (x, ctx_1024, g_xattn, g_ffn)
    x, ctx_1024, g_xattn, g_ffn = _rec_inputs()

    def _L0_xattn_setup():
        import math
        import jax, jax.numpy as jnp
        import numpy as np
        EMBED = 256
        HEADS = 16
        HDIM = EMBED // HEADS
        key = jax.random.key(seed)
        ks = jax.random.split(key, 11)
        N, L, E = (2, 512, EMBED)
        s = 1.0 / math.sqrt(E)
        return {'q': jax.random.normal(ks[0], (N, L, E), jnp.float32), 'k': jax.random.normal(ks[1], (N, L, E), jnp.float32), 'v': jax.random.normal(ks[2], (N, L, E), jnp.float32), 'Wq': jax.random.normal(ks[3], (E, E), jnp.float32) * s, 'bq': jnp.zeros((E,), jnp.float32), 'Wk': jax.random.normal(ks[4], (E, E), jnp.float32) * s, 'bk': jnp.zeros((E,), jnp.float32), 'Wv': jax.random.normal(ks[5], (E, E), jnp.float32) * s, 'bv': jnp.zeros((E,), jnp.float32), 'Wo': jax.random.normal(ks[6], (E, E), jnp.float32) * s, 'bo': jnp.zeros((E,), jnp.float32)}
    _L0_xattn_all = _L0_xattn_setup()
    _L0_xattn_in = {k: v for k, v in _L0_xattn_all.items() if k in ('Wq', 'bq', 'Wk', 'bk', 'Wv', 'bv', 'Wo', 'bo')}
    del _L0_xattn_all

    def _L0_ffn_setup():
        import jax, jax.numpy as jnp
        import numpy as np
        D_MODEL = 256
        NUM_EXPERTS = 8
        HIDDEN = 512
        TOP_K = 2
        SHARED_HIDDEN = 512
        BATCH, SEQ = (4, 512)
        key = jax.random.key(seed)
        ks = jax.random.split(key, 8)
        s = 1.0 / np.sqrt(D_MODEL)
        sh = 1.0 / np.sqrt(HIDDEN)
        return {'x': jax.random.normal(ks[0], (BATCH, SEQ, D_MODEL), dtype=jnp.float32), 'w_router': jax.random.normal(ks[1], (D_MODEL, NUM_EXPERTS), dtype=jnp.float32) * s, 'w1': jax.random.normal(ks[2], (NUM_EXPERTS, D_MODEL, HIDDEN), dtype=jnp.float32) * s, 'w3': jax.random.normal(ks[3], (NUM_EXPERTS, D_MODEL, HIDDEN), dtype=jnp.float32) * s, 'w2': jax.random.normal(ks[4], (NUM_EXPERTS, HIDDEN, D_MODEL), dtype=jnp.float32) * sh, 'ws1': jax.random.normal(ks[5], (D_MODEL, SHARED_HIDDEN), dtype=jnp.float32) * s, 'ws3': jax.random.normal(ks[6], (D_MODEL, SHARED_HIDDEN), dtype=jnp.float32) * s, 'ws2': jax.random.normal(ks[7], (SHARED_HIDDEN, D_MODEL), dtype=jnp.float32) * sh}
    _L0_ffn_all = _L0_ffn_setup()
    _L0_ffn_in = {k: v for k, v in _L0_ffn_all.items() if k in ('w_router', 'w1', 'w3', 'w2', 'ws1', 'ws3', 'ws2')}
    del _L0_ffn_all
    return {'x': x, 'ctx_1024': ctx_1024, 'g_xattn': g_xattn, 'g_ffn': g_ffn, 'L0_xattn_Wq': _L0_xattn_in['Wq'], 'L0_xattn_bq': _L0_xattn_in['bq'], 'L0_xattn_Wk': _L0_xattn_in['Wk'], 'L0_xattn_bk': _L0_xattn_in['bk'], 'L0_xattn_Wv': _L0_xattn_in['Wv'], 'L0_xattn_bv': _L0_xattn_in['bv'], 'L0_xattn_Wo': _L0_xattn_in['Wo'], 'L0_xattn_bo': _L0_xattn_in['bo'], 'L0_ffn_w_router': _L0_ffn_in['w_router'], 'L0_ffn_w1': _L0_ffn_in['w1'], 'L0_ffn_w3': _L0_ffn_in['w3'], 'L0_ffn_w2': _L0_ffn_in['w2'], 'L0_ffn_ws1': _L0_ffn_in['ws1'], 'L0_ffn_ws3': _L0_ffn_in['ws3'], 'L0_ffn_ws2': _L0_ffn_in['ws2']}

def reference(x, ctx_1024, g_xattn, g_ffn, L0_xattn_Wq, L0_xattn_bq, L0_xattn_Wk, L0_xattn_bk, L0_xattn_Wv, L0_xattn_bv, L0_xattn_Wo, L0_xattn_bo, L0_ffn_w_router, L0_ffn_w1, L0_ffn_w3, L0_ffn_w2, L0_ffn_ws1, L0_ffn_ws3, L0_ffn_ws2):
    import jax
    import jax.numpy as jnp

    def _L0_xattn_ref(q, k, v, Wq, bq, Wk, bk, Wv, bv, Wo, bo):
        import math
        import jax, jax.numpy as jnp
        import numpy as np
        EMBED = 256
        HEADS = 16
        HDIM = EMBED // HEADS
        N, L, E = q.shape
        h, d = (HEADS, HDIM)
        qh = (q @ Wq.T + bq).reshape(N, L, h, d)
        kh = (k @ Wk.T + bk).reshape(N, L, h, d)
        vh = (v @ Wv.T + bv).reshape(N, L, h, d)
        energy = jnp.einsum('nqhd,nkhd->nhqk', qh, kh)
        attn = jax.nn.softmax(energy / math.sqrt(d), axis=-1)
        out = jnp.einsum('nhql,nlhd->nhqd', attn, vh)
        out = out.transpose(0, 2, 1, 3).reshape(N, L, E)
        return out @ Wo.T + bo

    def _L0_ffn_ref(x, w_router, w1, w3, w2, ws1, ws3, ws2):
        import jax, jax.numpy as jnp
        import numpy as np
        D_MODEL = 256
        NUM_EXPERTS = 8
        HIDDEN = 512
        TOP_K = 2
        SHARED_HIDDEN = 512
        BATCH, SEQ = (4, 512)
        orig_shape = x.shape
        xf = x.reshape(-1, D_MODEL)
        T = xf.shape[0]
        logits = xf @ w_router
        scores = jax.nn.softmax(logits, axis=-1)
        expert_weights, expert_indices = jax.lax.top_k(scores, TOP_K)
        cw = jnp.zeros((T, NUM_EXPERTS), dtype=xf.dtype)
        cw = cw.at[jnp.arange(T)[:, None], expert_indices].add(expert_weights)
        h = jax.nn.silu(jnp.einsum('td,edh->teh', xf, w1)) * jnp.einsum('td,edh->teh', xf, w3)
        y = jnp.einsum('teh,ehd->ted', h, w2)
        moe_out = jnp.einsum('te,ted->td', cw, y)
        shared = jax.nn.silu(xf @ ws1) * (xf @ ws3) @ ws2
        out = shared / (TOP_K + 1) + moe_out * (TOP_K / (TOP_K + 1))
        return out.reshape(orig_shape)
    x = x + jnp.tanh(g_xattn[0]) * _L0_xattn_ref(_layernorm(x, axis=-1), ctx_1024, ctx_1024, L0_xattn_Wq, L0_xattn_bq, L0_xattn_Wk, L0_xattn_bk, L0_xattn_Wv, L0_xattn_bv, L0_xattn_Wo, L0_xattn_bo)
    x = x + jnp.tanh(g_ffn[0]) * _L0_ffn_ref(_layernorm(x, axis=-1), L0_ffn_w_router, L0_ffn_w1, L0_ffn_w3, L0_ffn_w2, L0_ffn_ws1, L0_ffn_ws3, L0_ffn_ws2)
    return x

_drawn_inputs = setup_inputs


def setup_inputs(seed=0):
    import zlib

    import numpy as np

    out = dict(_drawn_inputs(seed))
    spreads = {'L0_xattn_bq': (0.0, 0.39),
     'L0_xattn_bk': (0.0, 0.8),
     'L0_xattn_bv': (0.0, 0.1),
     'L0_xattn_bo': (0.0, 0.1)}
    factors = {}
    for name, (base, spread) in spreads.items():
        noise = np.random.default_rng([zlib.crc32(name.encode()), seed]).standard_normal(out[name].shape)
        drawn = base * np.exp(spread * noise) if base else spread * noise
        out[name] = jnp.asarray(drawn.astype(out[name].dtype))
    for name, factor in factors.items():
        out[name] = (out[name] * factor).astype(out[name].dtype)
    return out
```

```python
from contextlib import ExitStack

import numpy as np
import concourse.bass as bass
from concourse import mybir

F32 = mybir.dt.float32
F32R = mybir.dt.float32r
I32 = mybir.dt.int32
U32 = mybir.dt.uint32
ALU = mybir.AluOpType
ACT = mybir.ActivationFunctionType
AX = mybir.AxisListType.X

P = 128
NB, L, E = 16, 256, 256
H, D = 16, 16
NX, HID = 8, 512
TC = L // P
EC = E // P
FC = HID // P
NTOK = NB * L
R = 3
LOOP0, TRIPS = 2, 3
PVW = 32
REG = NTOK + 2 * P
NT = (2 * NTOK) // P + 2 * NX
WSZ = 2 * EC * HID + FC * E
W3O, W2O = EC * HID, 2 * EC * HID
NST = NTOK // P

C_ID, C_UP, C_ONE, C_MROW = 0, P, 2 * P, 3 * P
C_EB = C_MROW + H
C_TRI = C_EB + NX
C_THR = C_TRI + NX * NX
NTHR = NTOK // P + 1
C_TI = C_THR + NTHR
C_MH = C_TI + NT
CW = C_MH + 1

T_ROW, T_B, T_E, T_Z = 0, NT, NT + NX, NT + 2 * NX
T_P = T_Z + NX
T_L3, T_L1 = T_P + NX, T_P + NX + 1
TW = T_L1 + 1


def constants():
    c = np.zeros((P, CW), np.float32)
    c[:, C_ID:C_ID + P] = np.eye(P)
    c[:, C_UP:C_UP + P] = np.triu(np.ones((P, P)), 1)
    c[:, C_ONE:C_ONE + P] = 1.0
    c[P - 2, C_MROW:C_MROW + H:2] = 1.0
    c[P - 1, C_MROW + 1:C_MROW + H:2] = 1.0
    c[:, C_EB:C_EB + NX] = np.arange(NX) * REG
    c[:, C_TRI:C_TRI + NX * NX] = np.tril(np.ones((NX, NX)), -1).reshape(-1)
    c[:, C_THR:C_THR + NTHR] = np.arange(NTHR) * P
    c[:, C_TI:C_TI + NT] = np.arange(NT)
    c[:, C_MH] = -0.5
    return c


def moved(e, sem, value):
    if isinstance(value, int) and value <= 0:
        return
    e.wait_ge(sem, value)


class Batch:

    def __init__(self, j, c):
        self.b = R * j + c
        self.slot = c % R
        self.turn = j + c // R

    def n(self, per=1, k=0):
        return self.b * per + k


def build(nc, x, ctxT, gates, wT, bqk, bvo, wr, wall, cst, out):
    with ExitStack() as keep:
        def sem(name):
            return keep.enter_context(nc.semaphore(name))

        def sb(stack, name, shape, dt=F32):
            return stack.enter_context(nc.sbuf_tensor(name, shape, dt))

        qk_d = nc.dram_tensor("qk_d", (R, 8, P, L), F32, kind="Internal").ap()
        xs_d = nc.dram_tensor("xs_d", (NX * REG, E), F32, kind="Internal").ap()
        ys_d = nc.dram_tensor("ys_d", (NT * P, E), F32, kind="Internal").ap()
        xn2_d = nc.dram_tensor("xn2_d", (NTOK, E), F32, kind="Internal").ap()
        x2_d = nc.dram_tensor("x2_d", (NTOK, E), F32, kind="Internal").ap()

        K = sb(keep, "consts", [P, CW])
        ident = K[:, C_ID:C_ID + P]
        gt = sb(keep, "gates_sb", [P, 2])
        gate = sb(keep, "gate_tanh", [P, 2])
        gsc = sb(keep, "gate_scaled", [P, 2])
        acc = sb(keep, "mask_total", [P, NX])
        wraw = sb(keep, "w_raw", [P, WSZ])
        w_h0 = sb(keep, "w_h0", [P, WSZ], F32R)
        w_l0 = sb(keep, "w_l0", [P, WSZ], F32R)
        tab = sb(keep, "table", [1, TW], I32)
        spare_v = sb(keep, "spare_v", [P, 1])
        spare_p = sb(keep, "spare_p", [P, 2])
        zero = sb(keep, "zero_rows", [P, E])
        slots = sb(keep, "slots_all", [P, NST, 2])
        wts = sb(keep, "router_wts", [P, NST, 2])

        with ExitStack() as a:
            wt_raw = sb(a, "wt_raw", [P, EC, E])
            wt_h = sb(a, "wt_h", [P, 4, EC, E], F32R)
            wt_l = sb(a, "wt_l", [P, 4, EC, E], F32R)
            bqk_s = sb(a, "bqk_s", [P, 4])
            bv_s = sb(a, "bv_s", [P, E])
            gbo = sb(a, "gated_bo", [P, E])
            wr_s = sb(a, "wr_s", [P, EC, NX])
            x_s = sb(a, "x_s", [P, TC, E])
            xr_s = sb(a, "x_residual", [P, TC, E])
            c_s = sb(a, "c_s", [P, EC, L])
            xn_s = sb(a, "xn_s", [P, TC, E])
            bst = sb(a, "bn_st", [P, TC, 6])
            bmv = sb(a, "bn_mv", [P, TC, 2])
            rstd = sb(a, "rstd", [P, TC])
            bst2 = sb(a, "bn_st2", [P, TC, 6])
            bmv2 = sb(a, "bn_mv2", [P, TC, 2])
            rstd2 = sb(a, "rstd2", [P, TC])
            xnT_h = sb(a, "xnT_h", [P, EC, L], F32R)
            xnT_l = sb(a, "xnT_l", [P, EC, L], F32R)
            c_h = sb(a, "c_h", [P, EC, L], F32R)
            c_l = sb(a, "c_l", [P, EC, L], F32R)
            qk_s = sb(a, "qk_s", [P, 8, L], F32R)
            q4 = [sb(a, f"q4_{i}", [P, H // 2, L], F32R) for i in range(R)]
            k4 = [sb(a, f"k4_{i}", [P, H, L], F32R) for i in range(R)]
            v_s = [sb(a, f"v_{i}", [P, TC, H, PVW]) for i in range(R)]
            mx = sb(a, "row_max", [P, TC, H])
            mT = sb(a, "minus_max_T", [H, L], F32R)
            pT = sb(a, "probs_T", [P, 8, TC * L])
            oT_s = sb(a, "oT_s", [P, 4, L])
            rsum = sb(a, "rsum", [P, TC, H])
            o_s = sb(a, "o_s", [P, TC, E])
            oT_h = sb(a, "oT_h", [P, EC, L], F32R)
            oT_l = sb(a, "oT_l", [P, EC, L], F32R)
            x2_s = sb(a, "x2_s", [P, TC, E])
            xn2_s = sb(a, "xn2_s", [P, TC, E])
            xn2T = sb(a, "xn2T", [P, EC, L])
            lg = sb(a, "logits", [P, TC, NX])
            lgd = sb(a, "logits_less_max", [P, TC, NX])
            lmx = sb(a, "logit_max", [P, TC])
            ex = sb(a, "router_exp", [P, TC, NX])
            gtm = sb(a, "count_greater", [P, TC, NX, NX])
            eqm = sb(a, "count_equal", [P, TC, NX, NX])
            rk = sb(a, "rank_in_row", [P, TC, NX])
            oh = sb(a, "one_hot", [P, 2, TC, NX])
            msk = sb(a, "mask", [P, TC, NX])
            pr = sb(a, "products", [P, 2, TC, NX])
            ssum = sb(a, "score_sum", [P, TC])
            rec = sb(a, "score_rec", [P, TC])
            s2 = sb(a, "score_second", [P, TC])
            ex2 = sb(a, "exp_second", [P, TC, NX])
            pos = sb(a, "list_pos", [P, TC, NX])
            slot = sb(a, "slot_f", [P, 2, TC])
            slot_i = sb(a, "slot_i", [P, TC, 2], I32)
        with ExitStack() as m:
            w_h = [w_h0, sb(m, "w_h1", [P, WSZ], F32R)]
            w_l = [w_l0, sb(m, "w_l1", [P, WSZ], F32R)]
            xg = sb(m, "xg", [P, E])
            xg_h = sb(m, "xg_h", [P, EC, P], F32R)
            xg_l = sb(m, "xg_l", [P, EC, P], F32R)
            sg = sb(m, "sg", [P, HID])
            gg = sb(m, "gg", [P, HID])
            gT_h = sb(m, "gT_h", [P, FC, P], F32R)
            gT_l = sb(m, "gT_l", [P, FC, P], F32R)
            y_s = sb(m, "y_s", [P, E])
            ysh = [sb(m, f"ysh_{i}", [P, E]) for i in range(2)]
            yga = [sb(m, f"yga_{i}", [P, E]) for i in range(2)]
            ygb = [sb(m, f"ygb_{i}", [P, E]) for i in range(2)]
            x2g = [sb(m, f"x2g_{i}", [P, E]) for i in range(2)]
            wg = [sb(m, f"wg_{i}", [P, 2]) for i in range(2)]
            ig = [sb(m, f"ig_{i}", [P, 2], I32) for i in range(2)]
            gidx = sb(m, "gather_rows", [P, NST, 2], I32)
            gf = sb(m, "gather_f", [P, NST * 2])
            gge = sb(m, "gather_ge", [P, NST * 2, NX])
            dlt = sb(m, "list_shift", [P, NX])
            o_o = [sb(m, f"oo_{i}", [P, E]) for i in range(2)]
            cnt = sb(m, "cnt", [P, NX])
            tge = sb(m, "tge", [P, NX, NTHR])
            ntl = sb(m, "ntl", [P, NX])
            tend = sb(m, "tend", [P, NX])
            tgt = sb(m, "tgt", [P, NT, NX])
            tpr = sb(m, "tpr", [P, NT, NX])
            te_n = sb(m, "te_n", [P, NT])
            tb_n = sb(m, "tb_n", [P, NT])
            tabf = sb(m, "tabf", [P, TW])

        bank = [keep.enter_context(nc.psum_tensor(f"bank{i}", [P, 512], F32)) for i in range(8)]
        SS, SM, OT, T0, T1 = bank[0:2], bank[2:4], bank[4:6], bank[6], bank[7]
        psX, psG, psY, psH1, psH3 = bank[0], bank[1], bank[2], bank[3], bank[4]

        k_in = sem("k_in"); wt_in = sem("wt_in"); wt_ok = sem("wt_ok"); wt_used = sem("wt_used")
        cinit = sem("cinit"); gate_ok = sem("gate_ok"); gbo_ok = sem("gbo_ok")
        x_in = sem("x_in"); xr_in = sem("xr_in"); c_in = sem("c_in")
        var1_ok = sem("var1_ok"); rstd1_ok = sem("rstd1_ok"); var2_ok = sem("var2_ok"); rstd2_ok = sem("rstd2_ok")
        xn_ok = sem("xn_ok"); xnT_ps = sem("xnT_ps"); xnTh_ok = sem("xnTh_ok"); xnTl_ok = sem("xnTl_ok")
        ch_ok = sem("ch_ok"); cl_ok = sem("cl_ok")
        q_ps = sem("q_ps"); qh_ok = sem("qh_ok"); ql_ok = sem("ql_ok")
        k_ps = sem("k_ps"); kh_ok = sem("kh_ok"); kl_ok = sem("kl_ok")
        v_ps = sem("v_ps"); v_ok = sem("v_ok")
        qk_st = sem("qk_st"); stk = [sem(f"stk{i}") for i in range(R)]
        sm_ps = sem("sm_ps"); mx_ok = sem("mx_ok"); mT_ps = sem("mT_ps"); mT_ok = sem("mT_ok")
        mrow = sem("mrow")
        ss_ps = sem("ss_ps"); exp_ok = sem("exp_ok"); pv_ps = sem("pv_ps"); ot_ok = sem("ot_ok")
        oq_ps = sem("oq_ps"); o_ok = sem("o_ok"); oT_ps = sem("oT_ps"); oTh_ok = sem("oTh_ok")
        oTl_ok = sem("oTl_ok"); op_ps = sem("op_ps"); xb_ok = sem("xb_ok")
        x2_ok = sem("x2_ok"); xn2_ok = sem("xn2_ok"); row_st = sem("row_st")
        xn2T_ps = sem("xn2T_ps"); xn2T_ok = sem("xn2T_ok"); lg_ps = sem("lg_ps"); lgd_ok = sem("lgd_ok")
        ex_ok = sem("ex_ok"); oh_ok = sem("oh_ok"); rk_ps = sem("rk_ps"); slot_ok = sem("slot_ok")
        sc_done = sem("sc_done"); acc_ok = sem("acc_ok")
        chain = sem("chain")
        cnt_ps = sem("cnt_ps"); tab_ok = sem("tab_ok"); z_done = sem("z_done"); ys_zero = sem("ys_zero"); idx_ok = sem("idx_ok"); ig_ok = sem("ig_ok")
        w_in = sem("w_in"); w_used = sem("w_used"); w_ok = sem("w_ok")
        xg_in = sem("xg_in"); xt_ps = sem("xt_ps"); xh_ok = sem("xh_ok"); xl_ok = sem("xl_ok")
        h1_ps = sem("h1_ps"); h3_ps = sem("h3_ps"); sg_ok = sem("sg_ok"); g_ok = sem("g_ok")
        gT_ps = sem("gT_ps"); gh_ok = sem("gh_ok"); gl_ok = sem("gl_ok"); w2_ps = sem("w2_ps")
        y_ok = sem("y_ok"); y_st = sem("y_st")
        mg_in = [sem(f"mg_in{i}") for i in range(2)]; yg_in = [sem(f"yg_in{i}") for i in range(2)]
        spare_ok = sem("spare_ok"); cmb_ok = sem("cmb_ok"); o_st = [sem(f"o_st{i}") for i in range(2)]

        block = keep.enter_context(nc.Block())

        def iterations(e, one):
            for i in range(-R, LOOP0):
                one(0, i)
            with e.Fori(0, TRIPS) as j:
                for c in range(LOOP0, LOOP0 + R):
                    one(j, c)
            for i in range(LOOP0 + R * TRIPS, NB + 1):
                one(0, i)

        def stage(j, c, ahead):
            if isinstance(j, int) and not 0 <= R * j + c + ahead < NB:
                return None
            return Batch(j, c + ahead)

        @block.sync
        def _(sp):
            sp.dma_start(K[:, :], cst).then_inc(k_in, 16)
            sp.dma_start(gt[:, :], gates).then_inc(k_in, 16)
            sp.dma_start(bqk_s[:, :], bqk).then_inc(k_in, 16)
            sp.dma_start(bv_s[:, :], bvo[0]).then_inc(k_in, 16)
            sp.dma_start(gbo[:, :], bvo[1]).then_inc(k_in, 16)
            sp.dma_start(wr_s[:, :, :], wr).then_inc(k_in, 16)

            sp.wait_ge(cinit, 1)

            def load_x(n):
                moved(sp, xn_ok, n.n())
                sp.dma_start(x_s[:, :, :], x[bass.ds(n.b, 1)].rearrange("b (t p) d -> p (b t) d", p=P)).then_inc(x_in, 16)

            for w in range(4):
                moved(sp, wt_used, w)
                sp.dma_start(wt_raw[:, :, :], wT[w]).then_inc(wt_in, 16)

            def one(j, c):
                A, B, C, X, S = (stage(j, c, k) for k in (2, 1, 0, 3, -1))
                if X:
                    load_x(X)
                if A:
                    moved(sp, ch_ok, A.n())
                    moved(sp, cl_ok, A.n())
                    sp.dma_start(c_s[:, :, :], ctxT[bass.ds(A.b, 1)].rearrange("b (c p) t -> p (b c) t", p=P)).then_inc(c_in, 16)
                if S:
                    sp.wait_ge(x2_ok, S.n(1, 1))
                    sp.dma_start(x2_d[bass.ds(S.n(L), L), :].rearrange("(t p) d -> p t d", p=P), x2_s[:, :, :]).then_inc(row_st, 16)
                if C:
                    moved(sp, x2_ok, C.n())
                    sp.dma_start(xr_s[:, :, :], x[bass.ds(C.b, 1)].rearrange("b (t p) d -> p (b t) d", p=P)).then_inc(xr_in, 16)
                if S:
                    sp.wait_ge(xn2_ok, S.n(1, 1))
                    sp.dma_start(xn2_d[bass.ds(S.n(L), L), :].rearrange("(t p) d -> p t d", p=P), xn2_s[:, :, :]).then_inc(row_st, 16)
                if A:
                    moved(sp, ss_ps, A.n(H, -(R - 1) * H))
                    for s in (qh_ok, ql_ok, kh_ok, kl_ok):
                        sp.wait_ge(s, A.n(1, 1))
                    sp.dma_start(qk_d[A.slot].rearrange("c p t -> p c t"), qk_s[:, :, :].bitcast(F32)).then_inc(qk_st, 16)
                    sp.wait_ge(qk_st, A.n(16, 16))
                    for side, terms in ((0, (0, 1, 0)), (1, (0, 0, 1))):
                        for par in range(2):
                            for term, half in enumerate(terms):
                                c8 = 4 * side + 2 * half
                                rows = qk_d[A.slot, c8:c8 + 2].rearrange("c p t -> (c p) t")
                                rows = rows.rearrange("(s q d) t -> q d s t", q=2, d=D)[par]
                                r0 = 64 * par + D * term
                                dst = (q4[A.slot][r0:r0 + D, :, :] if side == 0
                                       else k4[A.slot][r0:r0 + D, par:H:2, :])
                                sp.dma_start(dst.bitcast(F32), rows).then_inc(stk[A.slot], 16)
                if C:
                    sp.dma_start(ys_d[bass.ds(C.n(NT * P // NB), NT * P // NB), :].rearrange("(t p) d -> p t d", p=P), zero[:, :].unsqueeze(1).to_broadcast([P, NT // NB, E])).then_inc(ys_zero, 16)
                if B:
                    sp.wait_ge(mT_ok, B.n(1, 1))
                    for par in range(2):
                        sp.dma_start(q4[B.slot][P - 2 + par:P - 1 + par, :, :].bitcast(F32), mT[8 * par:8 * par + 8, :].bitcast(F32)).then_inc(mrow, 16)

            iterations(sp, one)

            sp.wait_ge(tab_ok, 1)
            sp.wait_ge(sc_done, NB * 64)
            for k in range(NX):
                z = sp.value_load(tab[0:1, T_Z + k:T_Z + k + 1], min_val=0, max_val=NX * REG - 2 * P)
                sp.dma_start(xs_d[bass.ds(z, 2 * P), :].rearrange("(t p) d -> p t d", p=P), zero[:, :].unsqueeze(1).to_broadcast([P, 2, E])).then_inc(z_done, 16)
            sp.wait_ge(z_done, 16 * NX)
            sp.wait_ge(ys_zero, NB * 16)
            total = sp.value_load(tab[0:1, T_E + NX - 1:T_E + NX], min_val=2 * NX, max_val=NT)

            def tile_row(u):
                return sp.value_load(tab[0:1, bass.ds(u, 1)], min_val=0, max_val=NX * REG - P)

            def load_routed(u):
                r = tile_row(u)
                moved(sp, xt_ps, u)
                sp.dma_start(xg[:, :], xs_d[bass.ds(r, P), :]).then_inc(xg_in, 16)

            def load_shared(k):
                sp.wait_ge(xt_ps, total + k)
                sp.dma_start(xg[:, :], xn2_d[bass.ds(k * P, P), :]).then_inc(xg_in, 16)

            def store_y(u):
                sp.wait_ge(y_ok, u + 2)
                sp.dma_start(ys_d[bass.ds(u * P, P), :], y_s[:, :]).then_inc(y_st, 16)

            for u in range(3):
                load_routed(u)
            with sp.Fori(3, total) as u:
                load_routed(u)
                store_y(u - 3)
            sp.wait_ge(row_st, NB * 32)
            last3 = sp.value_load(tab[0:1, T_L3:T_L3 + 1], min_val=2 * NX - 3, max_val=NT - 3)

            def load_x2(k, p):
                moved(sp, cmb_ok, k - 1)
                sp.dma_start(x2g[p][:, :], x2_d[bass.ds(k * P, P), :]).then_inc(mg_in[p], 16)

            def store_out(k, p):
                sp.wait_ge(cmb_ok, k + 1)
                sp.dma_start(out[bass.ds(k * P, P), :], o_o[p][:, :]).then_inc(o_st[p], 16)

            def shared(k, p):
                load_shared(k)
                load_x2(k - 2, p)
                store_out(k - 4, p)

            for k in range(4):
                load_shared(k)
                if k < 3:
                    store_y(last3 + k)
                if k >= 2:
                    load_x2(k - 2, k % 2)
            with sp.Fori(2, NST // 2) as jj:
                shared(2 * jj, 0)
                shared(2 * jj + 1, 1)
            for k in range(NST, NST + 4):
                if k < NST + 2:
                    load_x2(k - 2, k % 2)
                store_out(k - 4, k % 2)
            sp.wait_ge(o_st[0], 16 * (NST // 2))
            sp.wait_ge(o_st[1], 16 * (NST // 2))

        @block.tensor
        def _(pe):
            def three(out, lhs, rhs, n, first=True, last=True):
                r = None
                for k in range(n):
                    (ah, al), (bh, bl) = lhs(k), rhs(k)
                    pe.matmul(out, ah, bh, start=first and k == 0, stop=False)
                    pe.matmul(out, al, bh, start=False, stop=False)
                    r = pe.matmul(out, ah, bl, start=False, stop=last and k == n - 1)
                return r

            pe.wait_ge(k_in, 96)
            pe.wait_ge(wt_ok, 8)
            pe.wait_ge(cinit, 1)

            def one(j, c):
                A, B, C, S = (stage(j, c, k) for k in (2, 1, 0, -1))

                def scores(h):
                    if C:
                        if h == 0:
                            pe.wait_ge(mrow, C.n(32, 32))
                        moved(pe, exp_ok, C.n(H, h - 1))
                        for kc in range(TC):
                            r = pe.matmul(SS[h % 2][:, kc * L:(kc + 1) * L],
                                          k4[C.slot][:, h, kc * P:(kc + 1) * P], q4[C.slot][:, h // 2, :],
                                          start=True, stop=True)
                        r.then_inc(ss_ps, 1)
                    if B:
                        if h == 0:
                            pe.wait_ge(stk[B.slot], B.turn * 192 + 192)
                        moved(pe, mx_ok, B.n(H, h - 1))
                        for qc in range(TC):
                            r = pe.matmul(SM[h % 2][:, qc * L:(qc + 1) * L],
                                          q4[B.slot][0:112, h // 2, qc * P:(qc + 1) * P], k4[B.slot][0:112, h, :],
                                          start=True, stop=True)
                        r.then_inc(sm_ps, 1)

                def values(g):
                    if C:
                        pe.wait_ge(exp_ok, C.n(H, 4 * g + 4))
                        moved(pe, ot_ok, C.n(4, g - 1))
                        for kc in range(TC):
                            for i in range(4):
                                h = 4 * g + i
                                r = pe.matmul(OT[g % 2][PVW * i:PVW * (i + 1), 0:L], v_s[C.slot][:, kc, h, :],
                                              pT[:, h % 8, kc * L:(kc + 1) * L], start=kc == 0, stop=kc == TC - 1)
                        r.then_inc(pv_ps, 1)

                def transposes(bnk, src, done):
                    for ic in range(EC):
                        for t in range(TC):
                            r = pe.transpose(bnk[:, ic * L + t * P:ic * L + (t + 1) * P],
                                             src[:, t, ic * P:(ic + 1) * P], ident)
                    r.then_inc(done, 1)

                def project(bnk, w, src_h, src_l, done):
                    for oc in range(EC):
                        r = three(bnk[:, oc * L:(oc + 1) * L],
                                  lambda k: (wt_h[:, w, k, oc * P:(oc + 1) * P], wt_l[:, w, k, oc * P:(oc + 1) * P]),
                                  lambda k: (src_h[:, k, :], src_l[:, k, :]), EC)
                    r.then_inc(done, 1)

                def project_rows(bnk, w, src_h, src_l, done):
                    for t in range(TC):
                        r = three(bnk[:, t * E:(t + 1) * E],
                                  lambda k: (src_h[:, k, t * P:(t + 1) * P], src_l[:, k, t * P:(t + 1) * P]),
                                  lambda k: (wt_h[:, w, k, :], wt_l[:, w, k, :]), EC)
                    r.then_inc(done, 1)

                for h in range(H):
                    scores(h)
                    if h in (5, 9, 13):
                        values((h - 5) // 4)
                    if h == 1 and A:
                        pe.wait_ge(xn_ok, A.n(1, 1))
                        moved(pe, oTl_ok, A.n(1, -2))
                        transposes(T0, xn_s, xnT_ps)
                    if h == 3 and S:
                        pe.wait_ge(xn2_ok, S.n(1, 1))
                        transposes(T1, xn2_s, xn2T_ps)
                    if h == 5 and A:
                        pe.wait_ge(xnTl_ok, A.n(1, 1))
                        project(T0, 0, xnT_h, xnT_l, q_ps)
                    if h == 7 and A:
                        pe.wait_ge(cl_ok, A.n(1, 1))
                        moved(pe, xn2T_ok, A.n(1, -2))
                        project(T1, 1, c_h, c_l, k_ps)
                    if h == 9 and S:
                        pe.wait_ge(xn2T_ok, S.n(1, 1))
                        moved(pe, ql_ok, S.n(1, 4) if A else NB)
                        for t in range(TC):
                            for k in range(EC):
                                r = pe.matmul(T0[:, t * NX:(t + 1) * NX], xn2T[:, k, t * P:(t + 1) * P],
                                              wr_s[:, k, :], start=k == 0, stop=k == EC - 1)
                        r.then_inc(lg_ps, 1)
                    if h == 11 and A:
                        pe.wait_ge(kl_ok, A.n(1, 1))
                        project_rows(T1, 2, c_h, c_l, v_ps)
                    if h == 13 and S:
                        pe.wait_ge(oh_ok, S.n(1, 1))
                        moved(pe, acc_ok, S.n(1, 0))
                        ones, up = K[:, C_ONE:C_ONE + P], K[:, C_UP:C_UP + P]
                        for t in range(TC):
                            o = T0[:, 64 + t * NX:64 + (t + 1) * NX]
                            pe.matmul(o, ones, acc[:, :], start=True, stop=False)
                            for s in range(t):
                                pe.matmul(o, ones, msk[:, s, :], start=False, stop=False)
                            r = pe.matmul(o, up, msk[:, t, :], start=False, stop=True)
                        r.then_inc(rk_ps, 1)
                if B:
                    pe.wait_ge(mx_ok, B.n(H, H))
                    moved(pe, v_ok, B.n(1, 2) if A else NB)
                    for qc in range(TC):
                        r = pe.transpose(T1[0:H, qc * P:(qc + 1) * P], mx[:, qc, :], ident)
                    r.then_inc(mT_ps, 1)
                values(3)
                if C:
                    pe.wait_ge(ot_ok, C.n(4, 4))
                    for qc, (bnk, free, cnt_) in enumerate(((T0, slot_ok, S.n(1, 1) if S else 0),
                                                           (T1, mT_ok, B.n(1, 1) if B else NB))):
                        moved(pe, free, cnt_)
                        for g in range(4):
                            r = pe.transpose(bnk[:, g * P:(g + 1) * P], oT_s[:, g, qc * P:(qc + 1) * P], ident)
                        r.then_inc(oq_ps, 1)
                    pe.wait_ge(o_ok, C.n(2, 2))
                    transposes(T0, o_s, oT_ps)
                    pe.wait_ge(oTl_ok, C.n(1, 1))
                    project_rows(T1, 3, oT_h, oT_l, op_ps)

            iterations(pe, one)

            pe.wait_ge(acc_ok, NB)
            pe.matmul(T1[:, 0:NX], K[:, C_ONE:C_ONE + P], acc[:, :], start=True, stop=True).then_inc(cnt_ps, 1)
            pe.wait_ge(tab_ok, 1)

            def transpose_x(u):
                pe.wait_ge(xg_in, u * 16 + 16)
                moved(pe, xl_ok, u)
                for k in range(EC):
                    r = pe.transpose(psX[:, k * P:(k + 1) * P], xg[:, k * P:(k + 1) * P], ident)
                r.then_inc(xt_ps, 1)

            def up(u, p):
                pe.wait_ge(xl_ok, u + 1)
                moved(pe, g_ok, u)
                for ps, off, done in ((psH1, 0, h1_ps), (psH3, W3O, h3_ps)):
                    three(ps[:, :], lambda k: (xg_h[:, k, :], xg_l[:, k, :]),
                          lambda k: (w_h[p][:, off + k * HID:off + (k + 1) * HID],
                                     w_l[p][:, off + k * HID:off + (k + 1) * HID]), EC).then_inc(done, 1)

            def down(done, p):
                pe.wait_ge(gl_ok, done)
                pe.wait_ge(y_ok, done)
                three(psY[:, 0:E], lambda k: (gT_h[:, k, :], gT_l[:, k, :]),
                      lambda k: (w_h[p][:, W2O + k * E:W2O + (k + 1) * E],
                                 w_l[p][:, W2O + k * E:W2O + (k + 1) * E]), FC).then_inc(w2_ps, 1)

            def transpose_g(u):
                pe.wait_ge(g_ok, u + 1)
                moved(pe, gl_ok, u)
                for k in range(FC):
                    r = pe.transpose(psG[:, k * P:(k + 1) * P], gg[:, k * P:(k + 1) * P], ident)
                r.then_inc(gT_ps, 1)

            def tile(u, p, before, after=True):
                up(u, p)
                if before is not None:
                    down(u, before)
                transpose_g(u)
                if after:
                    transpose_x(u + 2)

            def value(column, k, least, most):
                return pe.value_load(tab[0:1, bass.ds(k + column, 1)], min_val=least, max_val=most)

            def expert(k, p, before, tb, ends):
                pe.wait_ge(w_ok, k + 1)
                tile(tb, p, before)
                te = ends if isinstance(ends, list) else [value(T_E, k + i, 2, NT) for i in range(ends)]
                with pe.Fori(tb + 1, te[0]) as u:
                    tile(u, p, p)
                return te[1:]

            transpose_x(0)
            transpose_x(1)
            expert(0, 0, None, 0, 1)
            with pe.Fori(0, (NX - 2) // 2) as kk:
                k = 2 * kk + 1
                te = [value(T_E, k + i, 2, NT) for i in range(2)]
                expert(k, 1, 0, value(T_B, k, 2, NT - 2), te)
                expert(k + 1, 0, 1, te[0], te[1:])
            total = value(T_E, NX - 1, 2 * NX, NT)
            expert(NX - 1, 1, 0, value(T_B, NX - 1, 2, NT - 2), [total])
            pe.wait_ge(w_ok, NX + 1)
            tile(total, 0, 1)
            with pe.Fori(1, NST - 2) as k:
                tile(total + k, 0, 0)
            tile(total + (NST - 2), 0, 0, after=False)
            tile(total + (NST - 1), 0, 0, after=False)
            down(total + NST, 0)

        @block.scalar
        def _(act):
            act.wait_ge(k_in, 96)
            act.sem_inc(y_ok, 1)
            act.activation(gate[:, :], gt[:, :], ACT.Tanh).then_inc(gate_ok, 1)
            for w in range(4):
                act.wait_ge(wt_in, 16 * (w + 1))
                act.activation(wt_h[:, w, :, :], wt_raw[:, :, :], ACT.Copy).then_inc(wt_ok, 1)

            def one(j, c):
                A, B, C, S = (stage(j, c, k) for k in (2, 1, 0, -1))

                def probs(h):
                    if C:
                        act.wait_ge(ss_ps, C.n(H, h + 1))
                        moved(act, pv_ps, C.n(4, h // 4 - 1))
                        act.activation(pT[:, h % 8, :], SS[h % 2][:, :], ACT.Exp, scale=D ** -0.5).then_inc(exp_ok, 1)

                def head_out(g):
                    if C:
                        act.wait_ge(pv_ps, C.n(4, g + 1))
                        moved(act, oq_ps, C.n(2, 0))
                        act.activation(oT_s[:, g, :], OT[g % 2][:, 0:L], ACT.Copy).then_inc(ot_ok, 1)

                for h in range(H):
                    probs(h)
                    if h in (6, 10, 14):
                        head_out((h - 6) // 4)
                    if h == 2 and A:
                        act.wait_ge(xnT_ps, A.n(1, 1))
                        moved(act, q_ps, A.n())
                        act.activation(xnT_h[:, :, :], T0[:, :].rearrange("p (c t) -> p c t", c=EC), ACT.Copy).then_inc(xnTh_ok, 1)
                    if h == 3 and A:
                        act.wait_ge(c_in, A.n(16, 16))
                        moved(act, v_ps, A.n())
                        act.activation(c_h[:, :, :], c_s[:, :, :], ACT.Copy).then_inc(ch_ok, 1)
                    if h == 4 and S:
                        act.wait_ge(xn2T_ps, S.n(1, 1))
                        moved(act, lg_ps, S.n())
                        act.activation(xn2T[:, :, :], T1[:, :].rearrange("p (c t) -> p c t", c=EC), ACT.Copy).then_inc(xn2T_ok, 1)
                    if h in (6, 8) and A:
                        ps, done, ok, bnk, side = ((q_ps, None, qh_ok, T0, 0), (k_ps, None, kh_ok, T1, 1))[h == 8]
                        act.wait_ge(ps, A.n(1, 1))
                        moved(act, qk_st, A.n(16))
                        for oc in range(EC):
                            r = act.activation(qk_s[:, 4 * side + oc, :], bnk[:, oc * L:(oc + 1) * L], ACT.Identity,
                                               bias=bqk_s[:, 2 * side + oc:2 * side + oc + 1])
                        r.then_inc(ok, 1)
                    if h == 11 and S:
                        act.wait_ge(lgd_ok, S.n(1, 1))
                        act.activation(ex[:, :, :], lgd[:, :, :], ACT.Exp).then_inc(ex_ok, 1)
                if B:
                    act.wait_ge(mT_ps, B.n(1, 1))
                    moved(act, mrow, B.n(32))
                    act.activation(mT[:, :], T1[0:H, 0:L], ACT.Copy, scale=-1.0).then_inc(mT_ok, 1)
                head_out(3)
                if C:
                    act.wait_ge(oT_ps, C.n(1, 1))
                    moved(act, op_ps, C.n())
                    act.activation(oT_h[:, :, :], T0[:, :].rearrange("p (c t) -> p c t", c=EC), ACT.Copy).then_inc(oTh_ok, 1)

            iterations(act, one)

            act.wait_ge(tab_ok, 1)
            total = act.value_load(tab[0:1, T_E + NX - 1:T_E + NX], min_val=2 * NX, max_val=NT)

            def x_high(u):
                act.wait_ge(xt_ps, u + 1)
                moved(act, h3_ps, u)
                act.activation(xg_h[:, :, :], psX[:, 0:E].rearrange("p (c t) -> p c t", c=EC), ACT.Copy).then_inc(xh_ok, 1)

            def silu(u):
                act.wait_ge(h1_ps, u + 1)
                moved(act, g_ok, u)
                act.activation(sg[:, :], psH1[:, :], ACT.Silu).then_inc(sg_ok, 1)

            def g_high(u):
                act.wait_ge(gT_ps, u + 1)
                moved(act, w2_ps, u)
                act.activation(gT_h[:, :, :], psG[:, :].rearrange("p (c t) -> p c t", c=FC), ACT.Copy).then_inc(gh_ok, 1)

            def y_routed(u):
                act.wait_ge(w2_ps, u + 1)
                moved(act, y_st, u * 16)
                act.activation(y_s[:, :], psY[:, 0:E], ACT.Copy).then_inc(y_ok, 1)

            def y_shared(k, p):
                act.wait_ge(w2_ps, total + k + 1)
                moved(act, cmb_ok, k - 1)
                act.activation(ysh[p][:, :], psY[:, 0:E], ACT.Copy).then_inc(y_ok, 1)

            x_high(0)
            silu(0)
            x_high(1)
            g_high(0)
            def routed(u):
                silu(u)
                x_high(u + 1)
                y_routed(u - 1)
                g_high(u)

            routed(1)
            with act.Fori(2, total) as u:
                routed(u)
            silu(total)
            x_high(total + 1)
            y_routed(act.value_load(tab[0:1, T_L1:T_L1 + 1], min_val=2 * NX - 1, max_val=NT - 1))
            g_high(total)

            def shared(k, p, after=True):
                u = total + k
                silu(u)
                if after:
                    x_high(u + 1)
                y_shared(k - 1, 1 - p)
                g_high(u)

            shared(1, 1)
            shared(2, 0)
            with act.Fori(1, (NST - 2) // 2) as jj:
                shared(2 * jj + 1, 1)
                shared(2 * jj + 2, 0)
            shared(NST - 1, 1, after=False)
            y_shared(NST - 1, 1)

        @block.vector
        def _(v):
            seen = {"base": 0, "k": 0, "j": None, "per": 0}

            def link(ins, apart=False):
                seen["k"] += 1
                ins.then_inc(chain, 1)
                at = seen["base"] + seen["k"]
                v.wait_ge(chain, at if seen["j"] is None else seen["j"] * seen["per"] + at)
                if apart:
                    v.memset(spare_v[:, :], 0.0)

            for i in range(R):
                v.memset(q4[i][:, :, :].bitcast(U32), 0)
                v.memset(k4[i][:, :, :].bitcast(U32), 0)
                link(v.memset(v_s[i][:, :, :, :], 0.0))
            v.memset(zero[:, :], 0.0)
            link(v.memset(acc[:, :], 0.0))
            v.wait_ge(k_in, 96)
            for i in range(R):
                v.memset(v_s[i][:, :, :, D:D + 1], 1.0)
                r = v.tensor_copy(k4[i][96:128, :, :], K[96:128, C_MROW:C_MROW + H].unsqueeze(2).to_broadcast([32, H, L]))
            r.then_inc(cinit, 1)
            v.wait_ge(gate_ok, 1)
            link(v.tensor_scalar(gsc[:, 0:1], gate[:, 1:2], 1.0 / 3.0, None, ALU.mult))
            link(v.tensor_scalar(gsc[:, 1:2], gate[:, 1:2], 2.0 / 3.0, None, ALU.mult))
            v.tensor_scalar(gbo[:, :], gbo[:, :], gate[:, 0:1], None, ALU.mult).then_inc(gbo_ok, 1)
            for w in range(4):
                v.wait_ge(wt_ok, 2 * w + 1)
                v.tensor_tensor(wt_l[:, w, :, :], wt_raw[:, :, :], wt_h[:, w, :, :].bitcast(F32), ALU.subtract).then_inc(wt_ok, 1)
                v.wait_ge(wt_ok, 2 * w + 2)
                v.engine_nop().then_inc(wt_used, 1)

            def moments(src, st, mv, done):
                for t in range(TC):
                    r = v.bn_stats(st[:, t, :], src[:, t, :])
                link(r, apart=True)
                for t in range(TC):
                    r = v.bn_aggr(mv[:, t, :], st[:, t, :])
                link(r)
                v.tensor_scalar(mv[:, :, 1], mv[:, :, 1], 1e-5, None, ALU.add).then_inc(done, 1)

            def normalise(src, dst, mv, rs, done):
                for t in range(TC):
                    r = v.tensor_scalar(dst[:, t, :], src[:, t, :], mv[:, t, 0:1], rs[:, t:t + 1], ALU.subtract, ALU.mult)
                r.then_inc(done, 1)

            def low(dst, ps, high):
                return v.tensor_tensor(dst, ps, high.bitcast(F32), ALU.subtract)

            def one(j, c):
                Eb, A, B, C, S = (stage(j, c, k) for k in (3, 2, 1, 0, -1))

                def maximum(h):
                    if B:
                        v.wait_ge(sm_ps, B.n(H, h + 1))
                        moved(v, mT_ps, B.n())
                        v.tensor_reduce(mx[:, :, 8 * (h % 2) + h // 2], SM[h % 2][:, :].rearrange("p (t k) -> p t k", t=TC),
                                        AX, ALU.max).then_inc(mx_ok, 1)

                if S:
                    v.wait_ge(op_ps, S.n(1, 1))
                    v.wait_ge(xb_ok, S.n(1, 1))
                    moved(v, row_st, S.n(32))
                    v.scalar_tensor_tensor(x2_s[:, :, :], T1[:, :].rearrange("p (t d) -> p t d", t=TC), gate[:, 0:1],
                                           xr_s[:, :, :], ALU.mult, ALU.add).then_inc(x2_ok, 1)
                    v.wait_ge(x2_ok, S.n(1, 1))
                    moments(x2_s, bst2, bmv2, var2_ok)
                for h in range(H):
                    maximum(h)
                    if h == 1 and S:
                        v.wait_ge(rstd2_ok, S.n(1, 1))
                        moved(v, sc_done, S.n(64))
                        moved(v, xn2T_ps, S.n())
                        normalise(x2_s, xn2_s, bmv2, rstd2, xn2_ok)
                    if h == 12 and Eb:
                        v.wait_ge(x_in, Eb.n(16, 16))
                        moments(x_s, bst, bmv, var1_ok)
                    if h == 3 and A:
                        v.wait_ge(xnTh_ok, A.n(1, 1))
                        low(xnT_l[:, :, :], T0[:, :].rearrange("p (c t) -> p c t", c=EC), xnT_h[:, :, :]).then_inc(xnTl_ok, 1)
                    if h in (7, 9) and A:
                        side = h == 9
                        bnk = (T0, T1)[side]
                        v.wait_ge((qh_ok, kh_ok)[side], A.n(1, 1))
                        for oc in range(EC):
                            r = v.scalar_tensor_tensor(qk_s[:, 4 * side + 2 + oc, :], bnk[:, oc * L:(oc + 1) * L],
                                                       bqk_s[:, 2 * side + oc:2 * side + oc + 1],
                                                       qk_s[:, 4 * side + oc, :].bitcast(F32), ALU.add, ALU.subtract)
                        r.then_inc((ql_ok, kl_ok)[side], 1)
                    if h == 10 and S:
                        v.wait_ge(lg_ps, S.n(1, 1))
                        moved(v, rk_ps, S.n())
                        link(v.tensor_copy(lg[:, :, :], T0[:, 0:TC * NX].rearrange("p (t e) -> p t e", t=TC)))
                        link(v.tensor_reduce(lmx[:, :], lg[:, :, :], AX, ALU.max))
                        v.tensor_tensor(lgd[:, :, :], lg[:, :, :], lmx[:, :].unsqueeze(2).to_broadcast([P, TC, NX]),
                                        ALU.subtract).then_inc(lgd_ok, 1)
                        other = [lg[:, t, :].unsqueeze(1).to_broadcast([P, NX, NX]) for t in range(TC)]
                        own = [lg[:, t, :].unsqueeze(2).to_broadcast([P, NX, NX]) for t in range(TC)]
                        for t in range(TC):
                            v.tensor_tensor(gtm[:, t], other[t], own[t], ALU.is_gt)
                            r = v.tensor_tensor(eqm[:, t], other[t], own[t], ALU.is_equal)
                        link(r)
                        tri = K[:, C_TRI:C_TRI + NX * NX].rearrange("p (e j) -> p e j", e=NX)
                        link(v.tensor_tensor(eqm[:, :], eqm[:, :], tri.unsqueeze(1).to_broadcast([P, TC, NX, NX]), ALU.mult))
                        link(v.tensor_tensor(gtm[:, :], gtm[:, :], eqm[:, :], ALU.add))
                        link(v.tensor_reduce(rk[:, :, :], gtm[:, :], AX, ALU.add))
                        v.tensor_scalar(oh[:, 0], rk[:, :, :], 0.0, None, ALU.is_equal)
                        link(v.tensor_scalar(oh[:, 1], rk[:, :, :], 1.0, None, ALU.is_equal))
                        v.tensor_tensor(msk[:, :, :], oh[:, 0], oh[:, 1], ALU.add).then_inc(oh_ok, 1)
                    if h == 12 and A:
                        v.wait_ge(v_ps, A.n(1, 1))
                        moved(v, pv_ps, A.n(4, -4 * (R - 1)))
                        v.tensor_tensor(v_s[A.slot][:, :, :, 0:D], T1[:, :].rearrange("p (t h d) -> p t h d", t=TC, h=H),
                                        bv_s[:, :].rearrange("p (h d) -> p h d", h=H).unsqueeze(1).to_broadcast([P, TC, H, D]),
                                        ALU.add).then_inc(v_ok, 1)
                    if h == 13 and S:
                        v.wait_ge(ex_ok, S.n(1, 1))
                        v.tensor_reduce(ssum[:, :], ex[:, :, :], AX, ALU.add)
                        link(v.tensor_tensor(ex2[:, :, :], ex[:, :, :], oh[:, 1], ALU.mult))
                        v.reciprocal(rec[:, :], ssum[:, :])
                        link(v.tensor_reduce(s2[:, :], ex2[:, :, :], AX, ALU.add))
                        v.tensor_scalar(wts[:, bass.ds(S.n(TC), TC), 0], rec[:, :], gsc[:, 1:2], None, ALU.mult)
                        link(v.tensor_tensor(s2[:, :], s2[:, :], rec[:, :], ALU.mult))
                        v.tensor_scalar(wts[:, bass.ds(S.n(TC), TC), 1], s2[:, :], gsc[:, 1:2], None, ALU.mult)
                    if h == 14 and S:
                        v.wait_ge(rk_ps, S.n(1, 1))
                        link(v.tensor_tensor(pos[:, :, :], T0[:, 64:64 + TC * NX].rearrange("p (t e) -> p t e", t=TC),
                                             K[:, C_EB:C_EB + NX].unsqueeze(1).to_broadcast([P, TC, NX]), ALU.add))
                        link(v.tensor_tensor(pr[:, :], oh[:, :], pos[:, :, :].unsqueeze(1).to_broadcast([P, 2, TC, NX]), ALU.mult))
                        link(v.tensor_reduce(slot[:, :, :], pr[:, :], AX, ALU.add))
                        moved(v, sc_done, S.n(64))
                        by_tile = slot[:, :, :].rearrange("p k t -> p t k")
                        v.tensor_copy(slots[:, bass.ds(S.n(TC), TC), :], by_tile)
                        v.tensor_copy(slot_i[:, :, :], by_tile).then_inc(slot_ok, 1)
                        link(v.tensor_tensor(acc[:, :], acc[:, :], msk[:, 0, :], ALU.add))
                        v.tensor_tensor(acc[:, :], acc[:, :], msk[:, 1, :], ALU.add).then_inc(acc_ok, 1)
                    if h == 15 and Eb:
                        v.wait_ge(rstd1_ok, Eb.n(1, 1))
                        moved(v, xnT_ps, Eb.n())
                        normalise(x_s, xn_s, bmv, rstd, xn_ok)
                if C:
                    for qc, bnk in enumerate((T0, T1)):
                        v.wait_ge(oq_ps, C.n(2, qc + 1))
                        moved(v, oT_ps, C.n())
                        heads = bnk[:, :].rearrange("p (h w) -> p h w", w=PVW)
                        link(v.reciprocal(rsum[:, qc, :], heads[:, :, D]))
                        v.tensor_tensor(o_s[:, qc, :].rearrange("p (h d) -> p h d", d=D), heads[:, :, 0:D],
                                        rsum[:, qc, :].unsqueeze(2).to_broadcast([P, H, D]), ALU.mult).then_inc(o_ok, 1)
                    v.wait_ge(oTh_ok, C.n(1, 1))
                    low(oT_l[:, :, :], T0[:, :].rearrange("p (c t) -> p c t", c=EC), oT_h[:, :, :]).then_inc(oTl_ok, 1)

            for i in range(-R, LOOP0):
                one(0, i)
            seen.update(base=seen["base"] + seen["k"], k=0, per=LINKS_PER_LOOP)
            with v.Fori(0, TRIPS) as j:
                seen["j"] = j
                for c in range(LOOP0, LOOP0 + R):
                    one(j, c)
            assert seen["k"] == LINKS_PER_LOOP, seen["k"]
            seen.update(base=seen["base"] + TRIPS * LINKS_PER_LOOP, k=0, j=None)
            for i in range(LOOP0 + R * TRIPS, NB + 1):
                one(0, i)

            v.wait_ge(cnt_ps, 1)
            link(v.tensor_copy(cnt[:, :], T1[:, 0:NX]))
            link(v.tensor_tensor(tge[:, :, :], cnt[:, :].unsqueeze(2).to_broadcast([P, NX, NTHR]),
                                 K[:, C_THR:C_THR + NTHR].unsqueeze(1).to_broadcast([P, NX, NTHR]), ALU.is_gt))
            link(v.tensor_reduce(ntl[:, :], tge[:, :, :], AX, ALU.add))
            link(v.tensor_scalar(ntl[:, :], ntl[:, :], 2.0, None, ALU.max))
            link(v.tensor_copy(tend[:, 0:1], ntl[:, 0:1]))
            for k in range(1, NX):
                link(v.tensor_tensor(tend[:, k:k + 1], tend[:, k - 1:k], ntl[:, k:k + 1], ALU.add))
            v.tensor_copy(tabf[:, T_E:T_E + NX], tend[:, :])
            v.tensor_tensor(tabf[:, T_B:T_B + NX], tend[:, :], ntl[:, :], ALU.subtract)
            v.tensor_tensor(tabf[:, T_Z:T_Z + NX], cnt[:, :], K[:, C_EB:C_EB + NX], ALU.add)
            link(v.tensor_tensor(tgt[:, :, :], tend[:, :].unsqueeze(1).to_broadcast([P, NT, NX]),
                                 K[:, C_TI:C_TI + NT].unsqueeze(2).to_broadcast([P, NT, NX]), ALU.is_le))
            v.tensor_reduce(te_n[:, :], tgt[:, :, :], AX, ALU.add)
            link(v.tensor_tensor(tpr[:, :, :], tgt[:, :, :], ntl[:, :].unsqueeze(1).to_broadcast([P, NT, NX]), ALU.mult))
            link(v.tensor_reduce(tb_n[:, :], tpr[:, :, :], AX, ALU.add))
            link(v.tensor_scalar(te_n[:, :], te_n[:, :], float(NX - 1), float(REG), ALU.min, ALU.mult))
            link(v.tensor_tensor(tb_n[:, :], K[:, C_TI:C_TI + NT], tb_n[:, :], ALU.subtract))
            link(v.scalar_tensor_tensor(tabf[:, T_ROW:T_ROW + NT], tb_n[:, :], float(P), te_n[:, :], ALU.mult, ALU.add))
            v.tensor_scalar(tabf[:, T_L3:T_L3 + 1], tend[:, NX - 1:NX], -3.0, None, ALU.add)
            v.tensor_scalar(tabf[:, T_L1:T_L1 + 1], tend[:, NX - 1:NX], -1.0, None, ALU.add)
            link(v.tensor_scalar(tabf[:, T_P:T_P + NX], tabf[:, T_B:T_B + NX], -1.0, 0.0, ALU.add, ALU.max))
            v.tensor_copy(tab[0:1, :], tabf[0:1, :]).then_inc(tab_ok, 1)
            link(v.scalar_tensor_tensor(dlt[:, :], tabf[:, T_B:T_B + NX], float(P), K[:, C_EB:C_EB + NX], ALU.mult, ALU.subtract))
            link(v.tensor_copy(cnt[:, :], dlt[:, :]))
            link(v.tensor_tensor(dlt[:, 1:NX], cnt[:, 1:NX], cnt[:, 0:NX - 1], ALU.subtract))
            flat = slots[:, :, :].rearrange("p t k -> p (t k)")
            link(v.tensor_tensor(gge[:, :, :], flat.unsqueeze(2).to_broadcast([P, NST * 2, NX]),
                                 K[:, C_EB:C_EB + NX].unsqueeze(1).to_broadcast([P, NST * 2, NX]), ALU.is_ge))
            link(v.tensor_tensor(gge[:, :, :], gge[:, :, :], dlt[:, :].unsqueeze(1).to_broadcast([P, NST * 2, NX]), ALU.mult))
            link(v.tensor_reduce(gf[:, :], gge[:, :, :], AX, ALU.add))
            v.tensor_tensor(gidx[:, :, :].rearrange("p t k -> p (t k)"), gf[:, :], flat, ALU.add).then_inc(idx_ok, 1)
            v.wait_ge(tab_ok, 1)
            total = v.value_load(tab[0:1, T_E + NX - 1:T_E + NX], min_val=2 * NX, max_val=NT)

            def x_low(u):
                v.wait_ge(xh_ok, u + 1)
                low(xg_l[:, :, :], psX[:, 0:E].rearrange("p (c t) -> p c t", c=EC), xg_h[:, :, :]).then_inc(xl_ok, 1)

            def gated(u):
                v.wait_ge(sg_ok, u + 1)
                v.wait_ge(h3_ps, u + 1)
                moved(v, gT_ps, u)
                v.tensor_tensor(gg[:, :], sg[:, :], psH3[:, :], ALU.mult).then_inc(g_ok, 1)

            def g_low(u):
                v.wait_ge(gh_ok, u + 1)
                low(gT_l[:, :, :], psG[:, :].rearrange("p (c t) -> p c t", c=FC), gT_h[:, :, :]).then_inc(gl_ok, 1)

            base = seen["base"] + seen["k"]

            def combine(k, p, turn):
                v.wait_ge(y_ok, total + k + 2)
                v.wait_ge(mg_in[p], turn * 16 + 16)
                v.wait_ge(ig_ok, k + 1)
                v.wait_ge(yg_in[p], turn * 32 + 32)
                moved(v, o_st[p], turn * 16)
                v.scalar_tensor_tensor(yga[p][:, :], yga[p][:, :], wg[p][:, 0:1], x2g[p][:, :], ALU.mult, ALU.add).then_inc(chain, 1)
                v.wait_ge(chain, base + 2 * k + 1)
                v.scalar_tensor_tensor(ygb[p][:, :], ygb[p][:, :], wg[p][:, 1:2], yga[p][:, :], ALU.mult, ALU.add).then_inc(chain, 1)
                v.wait_ge(chain, base + 2 * k + 2)
                v.scalar_tensor_tensor(o_o[p][:, :], ysh[p][:, :], gsc[:, 0:1], ygb[p][:, :], ALU.mult, ALU.add).then_inc(cmb_ok, 1)

            def take(k, p):
                moved(v, cmb_ok, k - 1)
                v.tensor_copy(wg[p][:, :], wts[:, bass.ds(k, 1), :].rearrange("p t k -> p (t k)"))
                v.tensor_copy(ig[p][:, :], gidx[:, bass.ds(k, 1), :].rearrange("p t k -> p (t k)")).then_inc(ig_ok, 1)

            v.wait_ge(idx_ok, 1)
            take(0, 0)
            take(1, 1)
            x_low(0)
            gated(0)
            x_low(1)
            g_low(0)
            with v.Fori(1, total + 1) as u:
                gated(u)
                x_low(u + 1)
                g_low(u)

            def shared(jj, p):
                k = 2 * jj + (2 - p)
                gated(total + k)
                x_low(total + k + 1)
                g_low(total + k)
                combine(k - 1, 1 - p, jj)
                take(k + 1, 1 - p)

            shared(0, 1)
            shared(0, 0)
            with v.Fori(1, (NST - 2) // 2) as jj:
                shared(jj, 1)
                shared(jj, 0)
            k = NST - 1
            gated(total + k)
            g_low(total + k)
            combine(k - 1, 0, (k - 1) // 2)
            combine(k, 1, k // 2)

        @block.gpsimd
        def _(po):
            def load_w(k):
                moved(po, w_ok, k)
                po.dma_start(wraw[:, :], wall[k]).then_inc(w_in, 16)

            def cut(k, p, tiles=None):
                po.wait_ge(w_in, 16 * (k + 1))
                if tiles is not None:
                    po.wait_ge(w2_ps, tiles)
                po.tensor_copy(w_h[p][:, :], wraw[:, :]).then_inc(w_used, 1)
                po.wait_ge(w_used, k + 1)
                po.tensor_tensor(w_l[p][:, :], wraw[:, :], w_h[p][:, :].bitcast(F32), ALU.subtract).then_inc(w_ok, 1)

            def carry(n):
                po.wait_ge(spare_ok, n + 1)
                po.tensor_tensor(spare_p[:, 1:2], spare_p[:, 0:1], spare_p[:, 0:1], ALU.add).then_inc(spare_ok, 1)

            po.memset(spare_p[:, :], 0.0).then_inc(spare_ok, 1)
            po.wait_ge(spare_ok, 1)
            load_w(0)
            po.wait_ge(gbo_ok, 1)

            def one(j, c):
                Eb, A, C, S = (stage(j, c, k) for k in (3, 2, 0, -1))

                def root(mv, rs, asked, b, done):
                    po.wait_ge(asked, b.n(1, 1))
                    po.tensor_tensor(rs[:, :], mv[:, :, 1], K[:, C_MH:C_MH + 1].to_broadcast([P, TC]), ALU.pow).then_inc(done, 1)

                if S:
                    root(bmv2, rstd2, var2_ok, S, rstd2_ok)
                if A:
                    po.wait_ge(ch_ok, A.n(1, 1))
                    moved(po, v_ps, A.n())
                    po.tensor_tensor(c_l[:, :, :], c_s[:, :, :], c_h[:, :, :].bitcast(F32), ALU.subtract).then_inc(cl_ok, 1)
                if C:
                    po.wait_ge(xr_in, C.n(16, 16))
                    po.tensor_tensor(xr_s[:, :, :], xr_s[:, :, :], gbo[:, :].unsqueeze(1).to_broadcast([P, TC, E]), ALU.add).then_inc(xb_ok, 1)
                if Eb:
                    root(bmv, rstd, var1_ok, Eb, rstd1_ok)
                if S:
                    po.wait_ge(slot_ok, S.n(1, 1))
                    carry(S.b)
                    for t in range(TC):
                        for k in range(2):
                            po.indirect_dma_start(
                                out=xs_d, out_offset=bass.IndirectOffsetOnAxis(ap=slot_i[:, t, k:k + 1].bitcast(U32), axis=0),
                                in_=xn2_s[:, t, :], in_offset=None).then_inc(sc_done, 16)
                if isinstance(j, int) and c == 0:
                    cut(0, 0)
                    load_w(1)

            iterations(po, one)

            po.wait_ge(tab_ok, 1)
            cut(1, 1)
            load_w(2)
            for k in range(2, NX + 1):
                te = po.value_load(tab[0:1, T_E + k - 2:T_E + k - 1], min_val=2, max_val=NT)
                cut(k, k % 2, te)
                if k < NX:
                    load_w(k + 1)
            total = po.value_load(tab[0:1, T_E + NX - 1:T_E + NX], min_val=2 * NX, max_val=NT)
            with po.Fori(0, NST // 2) as jj:
                for p in range(2):
                    po.wait_ge(y_st, total * 16)
                    po.wait_ge(ig_ok, 2 * jj + (1 + p))
                    carry(2 * jj + (NB + p))
                    for k, dst in enumerate((yga, ygb)):
                        po.indirect_dma_start(
                            out=dst[p][:, :], out_offset=None, in_=ys_d,
                            in_offset=bass.IndirectOffsetOnAxis(ap=ig[p][:, k:k + 1].bitcast(U32), axis=0)).then_inc(yg_in[p], 16)


LINKS_PER_LOOP = 3 * 20


def kernel(**inputs):
    import numpy as _np
    import concourse.bacc as _bacc
    from concourse import mybir as _mybir
    from concourse.bass_utils import run_bass_kernel_spmd as _run

    a = {k: _np.asarray(v) for k, v in inputs.items()}
    P_ = 128

    def chunks(w):
        return w.reshape(-1, P_, w.shape[-1]).transpose(1, 0, 2)

    def rows(v):
        return _np.broadcast_to(v[None, :], (P_, v.shape[0]))

    wT = _np.stack([chunks(a["L0_xattn_" + n].T) for n in ("Wq", "Wk", "Wv", "Wo")])
    experts = [(a["L0_ffn_w1"][e], a["L0_ffn_w3"][e], a["L0_ffn_w2"][e]) for e in range(8)]
    experts.append((a["L0_ffn_ws1"], a["L0_ffn_ws3"], a["L0_ffn_ws2"]))
    wall = _np.stack([_np.concatenate([chunks(m).reshape(P_, -1) for m in e], axis=1) for e in experts])
    arrays = {
        "x": a["x"],
        "ctxT": a["ctx_1024"].transpose(0, 2, 1),
        "gates": rows(_np.concatenate([a["g_xattn"], a["g_ffn"]])),
        "wT": wT,
        "bqk": _np.concatenate([a["L0_xattn_bq"].reshape(2, P_), a["L0_xattn_bk"].reshape(2, P_)]).T,
        "bvo": _np.stack([rows(a["L0_xattn_bv"]), rows(a["L0_xattn_bo"])]),
        "wr": chunks(a["L0_ffn_w_router"]),
        "wall": wall,
        "cst": constants(),
    }
    arrays = {k: _np.ascontiguousarray(v) for k, v in arrays.items()}
    nc = _bacc.Bacc("TRN2", target_bir_lowering=False, num_devices=1)
    args = [nc.dram_tensor(k, v.shape, _mybir.dt.from_np(v.dtype), kind="ExternalInput").ap() for k, v in arrays.items()]
    o = nc.dram_tensor("out", (NTOK, E), _mybir.dt.float32, kind="ExternalOutput").ap()
    build(nc, *args, o)
    r = _run(nc, [arrays], core_ids=[0])
    return r.results[0]["out"].reshape(16, 256, 256)
```

```python
from contextlib import ExitStack

import numpy as np
import concourse.bass as bass
from concourse import mybir

F32 = mybir.dt.float32
F32R = mybir.dt.float32r
I32 = mybir.dt.int32
U32 = mybir.dt.uint32
ALU = mybir.AluOpType
ACT = mybir.ActivationFunctionType
AX = mybir.AxisListType.X

P = 128
NB, L, E = 16, 256, 256
H, D = 16, 16
NX, HID = 8, 512
TC = L // P
EC = E // P
FC = HID // P
NTOK = NB * L
R = 3
LOOP0, TRIPS = 3, 3
W_ORDER = (1, 0, 2, 3)
LATE = 4
WP = 3
PVW = 32
REG = NTOK + 2 * P
NT = (2 * NTOK) // P + 2 * NX
WSZ = 2 * EC * HID + FC * E
W3O, W2O = EC * HID, 2 * EC * HID
NST = NTOK // P

C_ID, C_UP, C_ONE, C_MROW = 0, P, 2 * P, 3 * P
C_EB = C_MROW + H
C_TRI = C_EB + NX
C_THR = C_TRI + NX * NX
NTHR = NTOK // P + 1
C_TI = C_THR + NTHR
C_MH = C_TI + NT
CW = C_MH + 1

T_ROW, T_B, T_E, T_Z = 0, NT, NT + NX, NT + 2 * NX
T_P = T_Z + NX
T_L3, T_L1 = T_P + NX, T_P + NX + 1
TW = T_L1 + 1


def constants():
    c = np.zeros((P, CW), np.float32)
    c[:, C_ID:C_ID + P] = np.eye(P)
    c[:, C_UP:C_UP + P] = np.triu(np.ones((P, P)), 1)
    c[:, C_ONE:C_ONE + P] = 1.0
    c[P - 2, C_MROW:C_MROW + H:2] = 1.0
    c[P - 1, C_MROW + 1:C_MROW + H:2] = 1.0
    c[:, C_EB:C_EB + NX] = np.arange(NX) * REG
    c[:, C_TRI:C_TRI + NX * NX] = np.tril(np.ones((NX, NX)), -1).reshape(-1)
    c[:, C_THR:C_THR + NTHR] = np.arange(NTHR) * P
    c[:, C_TI:C_TI + NT] = np.arange(NT)
    c[:, C_MH] = -0.5
    return c


def moved(e, sem, value):
    if isinstance(value, int) and value <= 0:
        return
    e.wait_ge(sem, value)


class Batch:

    def __init__(self, j, c):
        self.b = R * j + c
        self.slot = c % R
        self.turn = j + c // R

    def n(self, per=1, k=0):
        return self.b * per + k


def build(nc, x, ctxT, gates, wT, bqk, bvo, wr, wall, cst, out):
    with ExitStack() as keep:
        def sem(name):
            return keep.enter_context(nc.semaphore(name))

        def sb(stack, name, shape, dt=F32):
            return stack.enter_context(nc.sbuf_tensor(name, shape, dt))

        qk_d = nc.dram_tensor("qk_d", (R, 8, P, L), F32, kind="Internal").ap()
        xs_d = nc.dram_tensor("xs_d", (NX * REG, E), F32, kind="Internal").ap()
        ys_d = nc.dram_tensor("ys_d", (NT * P, E), F32, kind="Internal").ap()
        xn2_d = nc.dram_tensor("xn2_d", (NTOK, E), F32, kind="Internal").ap()
        x2_d = nc.dram_tensor("x2_d", (NTOK, E), F32, kind="Internal").ap()

        K = sb(keep, "consts", [P, CW])
        ident = K[:, C_ID:C_ID + P]
        gt = sb(keep, "gates_sb", [P, 2])
        gate = sb(keep, "gate_tanh", [P, 2])
        gsc = sb(keep, "gate_scaled", [P, 2])
        acc = sb(keep, "mask_total", [P, TC, NX])
        wraw = sb(keep, "w_raw", [P, WSZ])
        w_h0 = sb(keep, "w_h0", [P, WSZ], F32R)
        w_l0 = sb(keep, "w_l0", [P, WSZ], F32R)
        tab = sb(keep, "table", [1, TW], I32)
        spare_v = sb(keep, "spare_v", [P, 1])
        spare_p = sb(keep, "spare_p", [P, 2])
        zero = sb(keep, "zero_rows", [P, E])
        slots = sb(keep, "slots_all", [P, NST, 2])
        wts = sb(keep, "router_wts", [P, NST, 2])

        with ExitStack() as a:
            wt_h = sb(a, "wt_h", [P, 4, EC, E], F32R)
            wt_l = sb(a, "wt_l", [P, 4, EC, E], F32R)
            bqk_s = sb(a, "bqk_s", [P, 4])
            bv_s = sb(a, "bv_s", [P, E])
            gbo = sb(a, "gated_bo", [P, E])
            wr_s = sb(a, "wr_s", [P, EC, NX])
            x_s = sb(a, "x_s", [P, TC, E])
            xr_s = sb(a, "x_residual", [P, TC, E])
            c_s = sb(a, "c_s", [P, EC, L])
            xn_s = sb(a, "xn_s", [P, TC, E])
            bst = sb(a, "bn_st", [P, TC, 6])
            bmv = sb(a, "bn_mv", [P, TC, 2])
            rstd = sb(a, "rstd", [P, TC])
            bst2 = sb(a, "bn_st2", [P, TC, 6])
            bmv2 = sb(a, "bn_mv2", [P, TC, 2])
            rstd2 = sb(a, "rstd2", [P, TC])
            xnT_h = sb(a, "xnT_h", [P, EC, L], F32R)
            xnT_l = sb(a, "xnT_l", [P, EC, L], F32R)
            c_h = sb(a, "c_h", [P, EC, L], F32R)
            c_l = sb(a, "c_l", [P, EC, L], F32R)
            qk_s = sb(a, "qk_s", [P, 8, L], F32R)
            q4 = [sb(a, f"q4_{i}", [P, H // 2, L], F32R) for i in range(R)]
            k4 = [sb(a, f"k4_{i}", [P, H, L], F32R) for i in range(R)]
            v_s = [sb(a, f"v_{i}", [P, TC, H, PVW]) for i in range(R)]
            mx = [sb(a, f"row_max_{i}", [P, TC, H]) for i in range(R)]
            mT = sb(a, "minus_max_T", [H, L], F32R)
            pT = sb(a, "probs_T", [P, 8, TC * L])
            wt_raw = pT[:, 0:4, :]
            oT_s = sb(a, "oT_s", [P, 4, L])
            rsum = sb(a, "rsum", [P, TC, H])
            o_s = sb(a, "o_s", [P, TC, E])
            oT_h = sb(a, "oT_h", [P, EC, L], F32R)
            oT_l = sb(a, "oT_l", [P, EC, L], F32R)
            x2_s = sb(a, "x2_s", [P, TC, E])
            xn2_s = [sb(a, f"xn2_{i}", [P, TC, E]) for i in range(R)]
            xn2T = sb(a, "xn2T", [P, EC, L])
            lg = sb(a, "logits", [P, TC, NX])
            lgd = sb(a, "logits_less_max", [P, TC, NX])
            lmx = sb(a, "logit_max", [P, TC])
            ex = sb(a, "router_exp", [P, TC, NX])
            gtm = sb(a, "count_greater", [P, TC, NX, NX])
            eqm = sb(a, "count_equal", [P, TC, NX, NX])
            rk = sb(a, "rank_in_row", [P, TC, NX])
            oh = sb(a, "one_hot", [P, 2, TC, NX])
            msk = sb(a, "mask", [P, TC, NX])
            pr = sb(a, "products", [P, 2, TC, NX])
            ssum = sb(a, "score_sum", [P, TC])
            rec = sb(a, "score_rec", [P, TC])
            s2 = sb(a, "score_second", [P, TC])
            ex2 = sb(a, "exp_second", [P, TC, NX])
            pos = sb(a, "list_pos", [P, TC, NX])
            slot = sb(a, "slot_f", [P, 2, TC])
            slot_i = sb(a, "slot_i", [P, TC, 2], I32)
        with ExitStack() as m:
            w_h = [w_h0, sb(m, "w_h1", [P, WSZ], F32R)]
            w_l = [w_l0, sb(m, "w_l1", [P, WSZ], F32R)]
            xg = sb(m, "xg", [P, E])
            xg_h = sb(m, "xg_h", [P, EC, P], F32R)
            xg_l = sb(m, "xg_l", [P, EC, P], F32R)
            sg = sb(m, "sg", [P, HID])
            gg = sb(m, "gg", [P, HID])
            gT_h = sb(m, "gT_h", [P, FC, P], F32R)
            gT_l = sb(m, "gT_l", [P, FC, P], F32R)
            y_s = sb(m, "y_s", [P, E])
            ysh = [sb(m, f"ysh_{i}", [P, E]) for i in range(2)]
            yga = [sb(m, f"yga_{i}", [P, E]) for i in range(2)]
            ygb = [sb(m, f"ygb_{i}", [P, E]) for i in range(2)]
            x2g = [sb(m, f"x2g_{i}", [P, E]) for i in range(2)]
            wg = [sb(m, f"wg_{i}", [P, 2]) for i in range(2)]
            ig = [sb(m, f"ig_{i}", [P, 2], I32) for i in range(2)]
            gidx = sb(m, "gather_rows", [P, NST, 2], I32)
            gf = sb(m, "gather_f", [P, NST * 2])
            gge = sb(m, "gather_ge", [P, NST * 2, NX])
            dlt = sb(m, "list_shift", [P, NX])
            o_o = [sb(m, f"oo_{i}", [P, E]) for i in range(2)]
            cnt = sb(m, "cnt", [P, NX])
            tge = sb(m, "tge", [P, NX, NTHR])
            ntl = sb(m, "ntl", [P, NX])
            tend = sb(m, "tend", [P, NX])
            tgt = sb(m, "tgt", [P, NT, NX])
            tpr = sb(m, "tpr", [P, NT, NX])
            tpe = sb(m, "tpe", [P, NX, NX])
            te_n = sb(m, "te_n", [P, NT])
            tb_n = sb(m, "tb_n", [P, NT])
            tabf = sb(m, "tabf", [P, TW])

        bank = [keep.enter_context(nc.psum_tensor(f"bank{i}", [P, 512], F32)) for i in range(8)]
        SS, SM, T2, T0, T1 = bank[0:2], bank[2:4], bank[5], bank[6], bank[7]
        OT = [bank[4][:, 0:L], bank[4][:, L:2 * L]]
        mT_p, lg_p, rk_p = bank[4][0:H, 0:L], T1[:, 0:TC * NX], T1[:, 0:TC * NX]
        psX, psG, psY, psH1, psH3 = bank[0], bank[1], bank[2], bank[3], bank[4]

        k_in = sem("k_in"); wt_in = [sem(f"wt_in{w}") for w in range(4)]; wth_ok = sem("wth_ok"); wtl_ok = sem("wtl_ok"); few_in = sem("few_in")
        zero_ok = sem("zero_ok"); q_zero = sem("q_zero"); k_init = sem("k_init"); gate_ok = sem("gate_ok"); gbo_ok = sem("gbo_ok")
        x_in = sem("x_in"); xr_in = sem("xr_in"); c_in = sem("c_in")
        var1_ok = sem("var1_ok"); rstd1_ok = sem("rstd1_ok"); var2_ok = sem("var2_ok"); rstd2_ok = sem("rstd2_ok")
        xn_ok = sem("xn_ok"); xc_ok = sem("xc_ok"); xnT_ps = sem("xnT_ps"); xnTh_ok = sem("xnTh_ok"); xnTl_ok = sem("xnTl_ok")
        ch_ok = sem("ch_ok"); cl_ok = sem("cl_ok")
        q_ps = sem("q_ps"); qh_ok = sem("qh_ok"); ql_ok = sem("ql_ok")
        k_ps = sem("k_ps"); kh_ok = sem("kh_ok"); kl_ok = sem("kl_ok")
        v_ps = sem("v_ps"); vr_ok = sem("vr_ok"); v_ok = sem("v_ok")
        qk_st = sem("qk_st"); stk = [sem(f"stk{i}") for i in range(R)]
        sm_ps = sem("sm_ps"); mx_ok = sem("mx_ok"); mT_ps = sem("mT_ps"); mT_ok = sem("mT_ok")
        mrow = sem("mrow")
        ss_ps = sem("ss_ps"); exp_ok = sem("exp_ok"); pv_ps = sem("pv_ps"); ot_ok = sem("ot_ok")
        oq_ps = sem("oq_ps"); o_ok = sem("o_ok"); oT_ps = sem("oT_ps"); oTh_ok = sem("oTh_ok")
        oTl_ok = sem("oTl_ok"); op_ps = sem("op_ps"); xb_ok = sem("xb_ok")
        x2_ok = sem("x2_ok"); xn2_ok = sem("xn2_ok"); x2_st = sem("x2_st"); xn2_st = sem("xn2_st")
        xn2T_ps = sem("xn2T_ps"); xn2T_ok = sem("xn2T_ok"); lg_ps = sem("lg_ps"); lgc_ok = sem("lgc_ok"); pos_ok = sem("pos_ok"); lgd_ok = sem("lgd_ok")
        ex_ok = sem("ex_ok"); oh_ok = sem("oh_ok"); rk_ps = sem("rk_ps"); slot_ok = sem("slot_ok")
        sc_done = sem("sc_done"); acc_ok = sem("acc_ok")
        chain = sem("chain")
        cnt_ps = sem("cnt_ps"); tab_ok = sem("tab_ok"); ends_ok = sem("ends_ok"); z_first = sem("z_first"); z_done = sem("z_done"); ys_zero = sem("ys_zero"); idx_ok = sem("idx_ok"); ig_ok = sem("ig_ok")
        w_in = [sem(f"w_in{i}") for i in range(WP)]; w_used = sem("w_used"); w_ok = sem("w_ok")
        xg_in = sem("xg_in"); xt_ps = sem("xt_ps"); xh_ok = sem("xh_ok"); xl_ok = sem("xl_ok")
        h1_ps = sem("h1_ps"); h3_ps = sem("h3_ps"); sg_ok = sem("sg_ok"); g_ok = sem("g_ok")
        gT_ps = sem("gT_ps"); gh_ok = sem("gh_ok"); gl_ok = sem("gl_ok"); w2_ps = sem("w2_ps")
        y_ok = sem("y_ok"); y_st = sem("y_st")
        mg_in = [sem(f"mg_in{i}") for i in range(2)]; yg_in = [sem(f"yg_in{i}") for i in range(2)]
        spare_ok = sem("spare_ok"); cmb_ok = sem("cmb_ok"); o_st = [sem(f"o_st{i}") for i in range(2)]

        block = keep.enter_context(nc.Block())

        def iterations(e, one):
            for i in range(-R, LOOP0):
                one(0, i)
            with e.Fori(0, TRIPS) as j:
                for c in range(LOOP0, LOOP0 + R):
                    one(j, c)
            for i in range(LOOP0 + R * TRIPS, NB + 3):
                one(0, i)

        def among_first(batch, n):
            return isinstance(batch.b, int) and batch.b < n

        def late_head(C, S, h):
            return (S, H - LATE + h) if h < LATE else (C, h - LATE)

        def clear_behind(e, lists, done):
            for k in lists:
                z = e.value_load(tab[0:1, T_Z + k:T_Z + k + 1], min_val=0, max_val=NX * REG - 2 * P)
                e.dma_start(xs_d[bass.ds(z, 2 * P), :].rearrange("(t p) d -> p t d", p=P),
                            zero[:, :].unsqueeze(1).to_broadcast([P, 2, E])).then_inc(done, 16)

        def part(i):
            return slice(i * WSZ // WP, (i + 1) * WSZ // WP)

        def stage(j, c, ahead):
            if isinstance(j, int) and not 0 <= R * j + c + ahead < NB:
                return None
            return Batch(j, c + ahead)

        @block.sync
        def _(sp):
            def load_x(n):
                moved(sp, xn_ok, n.n())
                sp.dma_start(x_s[:, :, :], x[bass.ds(n.b, 1)].rearrange("b (t p) d -> p (b t) d", p=P)).then_inc(x_in, 16)

            def load_c(n):
                sp.dma_start(c_s[:, :, :], ctxT[bass.ds(n.b, 1)].rearrange("b (c p) t -> p (b c) t", p=P)).then_inc(c_in, 16)

            sp.sem_inc(xn2_st, R * 16)
            load_x(Batch(0, 0))
            sp.dma_start(K[:, :], cst).then_inc(k_in, 16)
            load_c(Batch(0, 0))
            for w in W_ORDER:
                sp.dma_start(wt_raw[:, w, :], wT[w].rearrange("p c n -> p (c n)")).then_inc(wt_in[w], 16)
            sp.dma_start(gt[:, :], gates).then_inc(few_in, 16)
            sp.dma_start(bqk_s[:, :], bqk).then_inc(few_in, 16)
            sp.dma_start(bv_s[:, :], bvo[0]).then_inc(few_in, 16)
            sp.dma_start(gbo[:, :], bvo[1]).then_inc(few_in, 16)
            sp.dma_start(wr_s[:, :, :], wr).then_inc(few_in, 16)

            def halves_out(A, side):
                if side == 1:
                    moved(sp, ss_ps, A.n(H, -(R - 1) * H))
                if among_first(A, R):
                    sp.wait_ge((q_zero, k_init)[side], A.b + 1)
                for s in ((qh_ok, ql_ok), (kh_ok, kl_ok))[side]:
                    sp.wait_ge(s, A.n(1, 1))
                sp.dma_start(qk_d[A.slot, 4 * side:4 * side + 4].rearrange("c p t -> p c t"),
                             qk_s[:, 4 * side:4 * side + 4, :].bitcast(F32)).then_inc(qk_st, 16)
                sp.wait_ge(qk_st, A.n(32, 32 - 16 * side))
                for par in range(2):
                    for first, terms, half in (((0, 1, 1), (1, 2, 0)), ((0, 2, 0), (2, 1, 1)))[side]:
                        c8 = 4 * side + 2 * half
                        rows = qk_d[A.slot, c8:c8 + 2].rearrange("c p t -> (c p) t")
                        rows = rows.rearrange("(s q d) t -> q d s t", q=2, d=D)[par]
                        for term in range(first, first + terms):
                            r0 = 64 * par + D * term
                            dst = (q4[A.slot][r0:r0 + D, :, :] if side == 0
                                   else k4[A.slot][r0:r0 + D, par:H:2, :])
                            sp.dma_start(dst.bitcast(F32), rows).then_inc(stk[A.slot], 16)

            def one(j, c):
                X, Eb, A, C, S, S2 = (stage(j, c, k) for k in (4, 3, 2, 0, -1, -2))
                if C:
                    sp.wait_ge(mT_ok, C.n(1, 1))
                    for par in range(2):
                        sp.dma_start(q4[C.slot][P - 2 + par:P - 1 + par, :, :].bitcast(F32), mT[8 * par:8 * par + 8, :].bitcast(F32)).then_inc(mrow, 16)
                if Eb:
                    moved(sp, ch_ok, Eb.n())
                    moved(sp, cl_ok, Eb.n())
                    if not among_first(Eb, 1):
                        load_c(Eb)
                if C:
                    sp.dma_start(ys_d[bass.ds(C.n(NT * P // NB), NT * P // NB), :].rearrange("(t p) d -> p t d", p=P), zero[:, :].unsqueeze(1).to_broadcast([P, NT // NB, E])).then_inc(ys_zero, 16)
                if A:
                    halves_out(A, 1)
                if S2:
                    sp.wait_ge(x2_ok, S2.n(1, 1))
                    sp.dma_start(x2_d[bass.ds(S2.n(L), L), :].rearrange("(t p) d -> p t d", p=P), x2_s[:, :, :]).then_inc(x2_st, 16)
                if S:
                    sp.dma_start(xr_s[:, :, :], x[bass.ds(S.b, 1)].rearrange("b (t p) d -> p (b t) d", p=P)).then_inc(xr_in, 16)
                if S2:
                    sp.wait_ge(xn2_ok, S2.n(1, 1))
                    sp.dma_start(xn2_d[bass.ds(S2.n(L), L), :].rearrange("(t p) d -> p t d", p=P), xn2_s[S2.slot][:, :, :]).then_inc(xn2_st, 16)
                if A:
                    halves_out(A, 0)
                if X:
                    load_x(X)

            iterations(sp, one)

            sp.wait_ge(ends_ok, 1)
            clear_behind(sp, (0,), z_first)
            sp.wait_ge(sc_done, NB * 64)
            sp.wait_ge(z_first, 16)
            sp.dma_start(xg[:, :], xs_d[0:P, :]).then_inc(xg_in, 16)
            clear_behind(sp, (2, 4), z_done)
            sp.wait_ge(xt_ps, 1)
            sp.dma_start(xg[:, :], xs_d[P:2 * P, :]).then_inc(xg_in, 16)
            clear_behind(sp, (6,), z_done)
            sp.wait_ge(tab_ok, 1)
            total = sp.value_load(tab[0:1, T_E + NX - 1:T_E + NX], min_val=2 * NX, max_val=NT)
            sp.wait_ge(z_done, 16 * (NX - 1))
            sp.wait_ge(ys_zero, NB * 16)

            def tile_row(u):
                return sp.value_load(tab[0:1, bass.ds(u, 1)], min_val=0, max_val=NX * REG - P)

            def load_routed(u):
                r = tile_row(u)
                moved(sp, xt_ps, u)
                sp.dma_start(xg[:, :], xs_d[bass.ds(r, P), :]).then_inc(xg_in, 16)

            def load_shared(k):
                sp.wait_ge(xt_ps, total + k)
                sp.dma_start(xg[:, :], xn2_d[bass.ds(k * P, P), :]).then_inc(xg_in, 16)

            def store_y(u):
                sp.wait_ge(y_ok, u + 2)
                sp.dma_start(ys_d[bass.ds(u * P, P), :], y_s[:, :]).then_inc(y_st, 16)

            load_routed(2)
            with sp.Fori(3, total) as u:
                load_routed(u)
                store_y(u - 3)
            sp.wait_ge(xn2_st, (R + NB) * 16)
            sp.wait_ge(x2_st, NB * 16)
            last3 = sp.value_load(tab[0:1, T_L3:T_L3 + 1], min_val=2 * NX - 3, max_val=NT - 3)

            def load_x2(k, p):
                moved(sp, cmb_ok, k - 1)
                sp.dma_start(x2g[p][:, :], x2_d[bass.ds(k * P, P), :]).then_inc(mg_in[p], 16)

            def store_out(k, p):
                sp.wait_ge(cmb_ok, k + 1)
                sp.dma_start(out[bass.ds(k * P, P), :], o_o[p][:, :]).then_inc(o_st[p], 16)

            def shared(k, p):
                load_shared(k)
                load_x2(k - 2, p)
                store_out(k - 4, p)

            for k in range(4):
                load_shared(k)
                if k < 3:
                    store_y(last3 + k)
                if k >= 2:
                    load_x2(k - 2, k % 2)
            with sp.Fori(2, NST // 2) as jj:
                shared(2 * jj, 0)
                shared(2 * jj + 1, 1)
            for k in range(NST, NST + 4):
                if k < NST + 2:
                    load_x2(k - 2, k % 2)
                store_out(k - 4, k % 2)
            sp.wait_ge(o_st[0], 16 * (NST // 2))
            sp.wait_ge(o_st[1], 16 * (NST // 2))

        @block.tensor
        def _(pe):
            def three(out, lhs, rhs, n, first=True, last=True):
                r = None
                for k in range(n):
                    (ah, al), (bh, bl) = lhs(k), rhs(k)
                    pe.matmul(out, ah, bh, start=first and k == 0, stop=False)
                    pe.matmul(out, al, bh, start=False, stop=False)
                    r = pe.matmul(out, ah, bl, start=False, stop=last and k == n - 1)
                return r

            pe.wait_ge(k_in, 16)
            pe.wait_ge(zero_ok, 1)

            def weights(batch, w):
                if among_first(batch, 1):
                    pe.wait_ge(wtl_ok, W_ORDER.index(w) + 1)

            def one(j, c):
                A, B, C, S, S2, S3 = (stage(j, c, k) for k in (2, 1, 0, -1, -2, -3))

                def scores(h):
                    V, hv = late_head(C, S, h)
                    if V:
                        if hv == 0:
                            pe.wait_ge(mrow, V.n(32, 32))
                        moved(pe, exp_ok, V.n(H, hv - 1))
                        for kc in range(TC):
                            r = pe.matmul(SS[hv % 2][:, kc * L:(kc + 1) * L],
                                          k4[V.slot][:, hv, kc * P:(kc + 1) * P], q4[V.slot][:, hv // 2, :],
                                          start=True, stop=True)
                        r.then_inc(ss_ps, 1)
                    if B:
                        if h == 0:
                            pe.wait_ge(stk[B.slot], B.turn * 192 + 192)
                        moved(pe, mx_ok, B.n(H, h - 1))
                        for qc in range(TC):
                            r = pe.matmul(SM[h % 2][:, qc * L:(qc + 1) * L],
                                          q4[B.slot][0:112, h // 2, qc * P:(qc + 1) * P], k4[B.slot][0:112, h, :],
                                          start=True, stop=True)
                        r.then_inc(sm_ps, 1)

                def values(V, g, kc):
                    if V:
                        if g == 0 and kc == 0:
                            if among_first(V, R):
                                pe.wait_ge(k_init, V.b + 1)
                            pe.wait_ge(v_ok, V.n(1, 1))
                        if kc == 0:
                            pe.wait_ge(exp_ok, V.n(H, 4 * g + 4))
                            moved(pe, ot_ok, V.n(4, g))
                        for i in range(4):
                            h = 4 * g + i
                            r = pe.matmul(OT[g % 2][PVW * i:PVW * (i + 1), :], v_s[V.slot][:, kc, h, :],
                                          pT[:, h % 8, kc * L:(kc + 1) * L], start=kc == 0, stop=kc == TC - 1)
                        if kc == TC - 1:
                            r.then_inc(pv_ps, 1)

                def transposes(bnk, src, done):
                    for ic in range(EC):
                        for t in range(TC):
                            r = pe.transpose(bnk[:, ic * L + t * P:ic * L + (t + 1) * P],
                                             src[:, t, ic * P:(ic + 1) * P], ident)
                    r.then_inc(done, 1)

                def attention_rows(qc):
                    for g in range(4):
                        r = pe.transpose((T0, T1)[qc][:, g * P:(g + 1) * P], oT_s[:, g, qc * P:(qc + 1) * P], ident)
                    r.then_inc(oq_ps, 1)

                def project(bnk, w, oc, src_h, src_l, done):
                    three(bnk[:, oc * L:(oc + 1) * L],
                          lambda k: (wt_h[:, w, k, oc * P:(oc + 1) * P], wt_l[:, w, k, oc * P:(oc + 1) * P]),
                          lambda k: (src_h[:, k, :], src_l[:, k, :]), EC).then_inc(done, 1)

                def project_rows(bnk, w, t, src_h, src_l, done):
                    three(bnk[:, t * E:(t + 1) * E],
                          lambda k: (src_h[:, k, t * P:(t + 1) * P], src_l[:, k, t * P:(t + 1) * P]),
                          lambda k: (wt_h[:, w, k, :], wt_l[:, w, k, :]), EC).then_inc(done, 1)

                for h in range(H):
                    scores(h)
                    if h == 0 and C:
                        pe.wait_ge(mx_ok, C.n(H, H))
                        if S:
                            pe.wait_ge(ot_ok, S.n(4, 2))
                        for qc in range(TC):
                            r = pe.transpose(mT_p[:, qc * P:(qc + 1) * P], mx[C.slot][:, qc, :], ident)
                        r.then_inc(mT_ps, 1)
                    if h == 0 and S3:
                        pe.wait_ge(oh_ok, S3.n(1, 1))
                        moved(pe, acc_ok, S3.n())
                        if S2:
                            pe.wait_ge(o_ok, S2.n(1, 1))
                        ones, up = K[:, C_ONE:C_ONE + P], K[:, C_UP:C_UP + P]
                        pe.matmul(rk_p, ones, acc[:, :, :].rearrange("p t e -> p (t e)"), start=True, stop=False)
                        r = pe.matmul(rk_p, up, msk[:, :, :].rearrange("p t e -> p (t e)"), start=False, stop=True)
                        r.then_inc(rk_ps, 1)
                    if h in (0, 1) and A:
                        if h == 0:
                            pe.wait_ge(cl_ok, A.n(1, 1))
                            moved(pe, qh_ok, A.n())
                            weights(A, 1)
                        project(T2, 1, h, c_h, c_l, k_ps)
                    if h in (2, 3):
                        if h == 2 and C:
                            pe.wait_ge(mT_ok, C.n(1, 1))
                        values(S, 2, h - 2)
                    if h in (2, 3) and S2:
                        if h == 2:
                            weights(S2, 3)
                            pe.wait_ge(oTl_ok, S2.n(1, 1))
                            if S3:
                                pe.wait_ge(pos_ok, S3.n(1, 1))
                        project_rows(T1, 3, h - 2, oT_h, oT_l, op_ps)
                    if h == 2 and A:
                        pe.wait_ge(xn_ok, A.n(1, 1))
                        if S2:
                            pe.wait_ge(oTl_ok, S2.n(1, 1))
                        else:
                            moved(pe, vr_ok, A.n())
                        transposes(T0, xn_s, xnT_ps)
                    if h in (5, 6):
                        values(S, 3, h - 5)
                    if h in (5, 6) and A:
                        if h == 5:
                            pe.wait_ge(xnTl_ok, A.n(1, 1))
                            pe.wait_ge(kh_ok, A.n(1, 1))
                            weights(A, 0)
                        project(T2, 0, h - 5, xnT_h, xnT_l, q_ps)
                    if h in (7, 8) and A:
                        if h == 7:
                            weights(A, 2)
                        project_rows(T0, 2, h - 7, c_h, c_l, v_ps)
                    if h == 9 and S2:
                        pe.wait_ge(xn2_ok, S2.n(1, 1))
                        pe.wait_ge(x2_ok, S2.n(1, 1))
                        transposes(T1, xn2_s[S2.slot], xn2T_ps)
                    if h in (9, 10):
                        values(C, 0, h - 9)
                    if h == 10 and S:
                        pe.wait_ge(ot_ok, S.n(4, 4))
                        if A:
                            pe.wait_ge(vr_ok, A.n(1, 1))
                        elif S2:
                            pe.wait_ge(oTl_ok, S2.n(1, 1))
                        attention_rows(0)
                    if h == 11 and S2:
                        if among_first(S2, 1):
                            pe.wait_ge(few_in, 80)
                        pe.wait_ge(xn2T_ok, S2.n(1, 1))
                        for t in range(TC):
                            for k in range(EC):
                                r = pe.matmul(lg_p[:, t * NX:(t + 1) * NX], xn2T[:, k, t * P:(t + 1) * P],
                                              wr_s[:, k, :], start=k == 0, stop=k == EC - 1)
                        r.then_inc(lg_ps, 1)
                    if h == 13 and S:
                        if S2:
                            pe.wait_ge(lgc_ok, S2.n(1, 1))
                        attention_rows(1)
                    if h in (13, 14):
                        values(C, 1, h - 13)
                    if h == 15 and S:
                        pe.wait_ge(o_ok, S.n(1, 1))
                        transposes(T0, o_s, oT_ps)

            iterations(pe, one)

            pe.wait_ge(acc_ok, NB)
            pe.matmul(T0[:, 0:NX], K[:, C_ONE:C_ONE + P], acc[:, 0, :], start=True, stop=True).then_inc(cnt_ps, 1)

            def transpose_x(u):
                pe.wait_ge(xg_in, u * 16 + 16)
                moved(pe, xl_ok, u)
                for k in range(EC):
                    r = pe.transpose(psX[:, k * P:(k + 1) * P], xg[:, k * P:(k + 1) * P], ident)
                r.then_inc(xt_ps, 1)

            def up(u, p, after):
                pe.wait_ge(xl_ok, u + 1)
                moved(pe, g_ok, u)
                for ps, off, done in ((psH1, 0, h1_ps), (psH3, W3O, h3_ps)):
                    three(ps[:, :], lambda k: (xg_h[:, k, :], xg_l[:, k, :]),
                          lambda k: (w_h[p][:, off + k * HID:off + (k + 1) * HID],
                                     w_l[p][:, off + k * HID:off + (k + 1) * HID]), EC).then_inc(done, 1)
                    if after and done is h1_ps:
                        transpose_x(u + 1)

            def down(done, p):
                pe.wait_ge(gl_ok, done)
                pe.wait_ge(y_ok, done)
                three(psY[:, 0:E], lambda k: (gT_h[:, k, :], gT_l[:, k, :]),
                      lambda k: (w_h[p][:, W2O + k * E:W2O + (k + 1) * E],
                                 w_l[p][:, W2O + k * E:W2O + (k + 1) * E]), FC).then_inc(w2_ps, 1)

            def transpose_g(u):
                pe.wait_ge(g_ok, u + 1)
                moved(pe, gl_ok, u)
                for k in range(FC):
                    r = pe.transpose(psG[:, k * P:(k + 1) * P], gg[:, k * P:(k + 1) * P], ident)
                r.then_inc(gT_ps, 1)

            def tile(u, p, before, after=True):
                up(u, p, after)
                if before is not None:
                    down(u, before)
                transpose_g(u)

            def value(column, k, least, most):
                return pe.value_load(tab[0:1, bass.ds(k + column, 1)], min_val=least, max_val=most)

            def expert(k, p, before, tb, ends):
                pe.wait_ge(w_ok, k * WP + WP)
                tile(tb, p, before)
                te = ends if isinstance(ends, list) else [value(T_E, k + i, 2, NT) for i in range(ends)]
                with pe.Fori(tb + 1, te[0]) as u:
                    tile(u, p, p)
                return te

            transpose_x(0)
            pe.wait_ge(tab_ok, 1)
            expert(0, 0, None, 0, 1)
            with pe.Fori(0, (NX - 2) // 2) as kk:
                k = 2 * kk + 1
                ends = expert(k, 1, 0, value(T_B, k, 2, NT - 2), 2)
                expert(k + 1, 0, 1, ends[0], ends[1:])
            total, = expert(NX - 1, 1, 0, value(T_B, NX - 1, 2, NT - 2), 1)
            pe.wait_ge(w_ok, (NX + 1) * WP)
            tile(total, 0, 1)
            with pe.Fori(1, NST - 1) as k:
                tile(total + k, 0, 0)
            tile(total + (NST - 1), 0, 0, after=False)
            down(total + NST, 0)

        @block.scalar
        def _(act):
            act.sem_inc(y_ok, 1)

            def clear_q(i):
                act.activation(q4[i][:, :, :], zero[:, :].unsqueeze(1).to_broadcast([P, H // 2, L]), ACT.Copy).then_inc(q_zero, 1)

            act.wait_ge(zero_ok, 1)
            clear_q(0)
            for w in W_ORDER:
                act.wait_ge(wt_in[w], 16)
                act.activation(wt_h[:, w, :, :], wt_raw[:, w, :].rearrange("p (c n) -> p c n", c=EC), ACT.Copy).then_inc(wth_ok, 1)
            act.wait_ge(few_in, 80)
            act.activation(gate[:, :], gt[:, :], ACT.Tanh).then_inc(gate_ok, 1)

            def one(j, c):
                Eb, A, C, S, S2 = (stage(j, c, k) for k in (3, 2, 0, -1, -2))

                def probs(h):
                    V, hv = late_head(C, S, h)
                    if V:
                        if hv == 0 and among_first(V, 1):
                            act.wait_ge(wtl_ok, 4)
                        act.wait_ge(ss_ps, V.n(H, hv + 1))
                        moved(act, pv_ps, V.n(4, hv // 4 - 1))
                        act.activation(pT[:, hv % 8, :], SS[hv % 2][:, :], ACT.Exp, scale=D ** -0.5).then_inc(exp_ok, 1)

                def head_out(V, g):
                    if V:
                        act.wait_ge(pv_ps, V.n(4, g + 1))
                        moved(act, oq_ps, V.n(2))
                        act.activation(oT_s[:, g, :], OT[g % 2], ACT.Copy).then_inc(ot_ok, 1)

                def from_bank(dst, bnk, ps, b, used, count, done):
                    act.wait_ge(ps, b.n(1, 1))
                    moved(act, used, count)
                    act.activation(dst[:, :, :], bnk[:, :].rearrange("p (c t) -> p c t", c=EC), ACT.Copy).then_inc(done, 1)

                def q_or_k(side, bnk, ps, done):
                    act.wait_ge(ps, A.n(2, 2))
                    moved(act, qk_st, A.n(32, -16 * side))
                    for oc in range(EC):
                        for half in range(2):
                            dst = qk_s[:, 4 * side + 2 * half + oc, :]
                            r = act.activation(dst.bitcast(F32) if half else dst, bnk[:, oc * L:(oc + 1) * L], ACT.Identity,
                                               bias=bqk_s[:, 2 * side + oc:2 * side + oc + 1])
                    r.then_inc(done, 1)

                for h in range(H):
                    probs(h)
                    if h == 0 and S2:
                        from_bank(oT_h, T0, oT_ps, S2, op_ps, S2.n(2), oTh_ok)
                    if h == 0 and C:
                        act.wait_ge(mT_ps, C.n(1, 1))
                        moved(act, mrow, C.n(32))
                        act.activation(mT[:, :], mT_p, ACT.Copy, scale=-1.0).then_inc(mT_ok, 1)
                    if h == 2 and A:
                        q_or_k(1, T2, k_ps, kh_ok)
                    if h == 3 and A:
                        from_bank(xnT_h, T0, xnT_ps, A, q_ps, A.n(2), xnTh_ok)
                    if h == 4:
                        head_out(S, 2)
                    if h == 7:
                        head_out(S, 3)
                    if h == 7 and A:
                        q_or_k(0, T2, q_ps, qh_ok)
                    if h == 9 and A:
                        act.wait_ge(v_ps, A.n(2, 2))
                        moved(act, pv_ps, A.n(4, -4 * (R - 1)))
                        act.activation(v_s[A.slot][:, :, :, 0:D], T0[:, :].rearrange("p (t h d) -> p t h d", t=TC, h=H),
                                       ACT.Copy).then_inc(vr_ok, 1)
                    if h == 10 and Eb:
                        act.wait_ge(c_in, Eb.n(16, 16))
                        moved(act, v_ps, Eb.n(2))
                        act.activation(c_h[:, :, :], c_s[:, :, :], ACT.Copy).then_inc(ch_ok, 1)
                    if h == 10 and S2:
                        from_bank(xn2T, T1, xn2T_ps, S2, lg_ps, S2.n(), xn2T_ok)
                    if h == 11:
                        head_out(C, 0)
                    if h == 13 and S2:
                        act.wait_ge(lgd_ok, S2.n(1, 1))
                        act.activation(ex[:, :, :], lgd[:, :, :], ACT.Exp).then_inc(ex_ok, 1)
                    if h == 15:
                        head_out(C, 1)
                if Eb and among_first(Eb, R - 1):
                    clear_q(Eb.b + 1)
                if S and among_first(S, NB) and S.b == NB - 2:
                    for i in range(WP):
                        act.wait_ge(w_in[i], 16)
                        act.activation(w_h0[:, part(i)], wraw[:, part(i)], ACT.Copy).then_inc(w_used, 1)

            iterations(act, one)

            act.wait_ge(ends_ok, 1)
            clear_behind(act, (1, 3, 5, 7), z_done)

            def x_high(u):
                act.wait_ge(xt_ps, u + 1)
                moved(act, h3_ps, u)
                act.activation(xg_h[:, :, :], psX[:, 0:E].rearrange("p (c t) -> p c t", c=EC), ACT.Copy).then_inc(xh_ok, 1)

            def silu(u):
                act.wait_ge(h1_ps, u + 1)
                moved(act, g_ok, u)
                act.activation(sg[:, :], psH1[:, :], ACT.Silu).then_inc(sg_ok, 1)

            def g_high(u):
                act.wait_ge(gT_ps, u + 1)
                moved(act, w2_ps, u)
                act.activation(gT_h[:, :, :], psG[:, :].rearrange("p (c t) -> p c t", c=FC), ACT.Copy).then_inc(gh_ok, 1)

            def y_routed(u):
                act.wait_ge(w2_ps, u + 1)
                moved(act, y_st, u * 16)
                act.activation(y_s[:, :], psY[:, 0:E], ACT.Copy).then_inc(y_ok, 1)

            def y_shared(k, p):
                act.wait_ge(w2_ps, total + k + 1)
                moved(act, cmb_ok, k - 1)
                act.activation(ysh[p][:, :], psY[:, 0:E], ACT.Copy).then_inc(y_ok, 1)

            x_high(0)
            act.wait_ge(tab_ok, 1)
            total = act.value_load(tab[0:1, T_E + NX - 1:T_E + NX], min_val=2 * NX, max_val=NT)
            silu(0)
            x_high(1)
            g_high(0)
            def routed(u):
                silu(u)
                x_high(u + 1)
                y_routed(u - 1)
                g_high(u)

            routed(1)
            with act.Fori(2, total) as u:
                routed(u)
            silu(total)
            x_high(total + 1)
            y_routed(act.value_load(tab[0:1, T_L1:T_L1 + 1], min_val=2 * NX - 1, max_val=NT - 1))
            g_high(total)

            def shared(k, p, after=True):
                u = total + k
                silu(u)
                if after:
                    x_high(u + 1)
                y_shared(k - 1, 1 - p)
                g_high(u)

            shared(1, 1)
            shared(2, 0)
            with act.Fori(1, (NST - 2) // 2) as jj:
                shared(2 * jj + 1, 1)
                shared(2 * jj + 2, 0)
            shared(NST - 1, 1, after=False)
            y_shared(NST - 1, 1)

        @block.vector
        def _(v):
            seen = {"base": 0, "k": 0, "j": None, "per": 0}

            def mark(ins):
                seen["k"] += 1
                ins.then_inc(chain, 1)

            def settle(apart=False):
                at = seen["base"] + seen["k"]
                v.wait_ge(chain, at if seen["j"] is None else seen["j"] * seen["per"] + at)
                if apart:
                    v.memset(spare_v[:, :], 0.0)

            def link(ins):
                mark(ins)
                settle()

            v.memset(zero[:, :], 0.0)
            link(v.memset(acc[:, :, :], 0.0))
            v.tensor_copy(spare_v[:, :], acc[:, 0, 0:1]).then_inc(zero_ok, 1)
            v.wait_ge(k_in, 16)

            def clear_k(i):
                link(v.memset(k4[i][:, :, :].bitcast(U32), 0))
                v.memset(v_s[i][:, :, :, D:D + 1], 1.0)
                v.memset(v_s[i][:, :, :, D + 1:PVW], 0.0)
                v.tensor_copy(k4[i][96:128, :, :], K[96:128, C_MROW:C_MROW + H].unsqueeze(2).to_broadcast([32, H, L])).then_inc(k_init, 1)

            def weights_low():
                for n, w in enumerate(W_ORDER):
                    v.wait_ge(wth_ok, n + 1)
                    v.tensor_tensor(wt_l[:, w, :, :], wt_raw[:, w, :].rearrange("p (c n) -> p c n", c=EC),
                                    wt_h[:, w, :, :].bitcast(F32), ALU.subtract).then_inc(wtl_ok, 1)

            def scale_gates():
                v.wait_ge(gate_ok, 1)
                link(v.tensor_scalar(gsc[:, 0:1], gate[:, 1:2], 1.0 / 3.0, None, ALU.mult))
                link(v.tensor_scalar(gsc[:, 1:2], gate[:, 1:2], 2.0 / 3.0, None, ALU.mult))
                v.tensor_scalar(gbo[:, :], gbo[:, :], gate[:, 0:1], None, ALU.mult).then_inc(gbo_ok, 1)

            def bank_chunks(bnk):
                return bnk[:, :].rearrange("p (c t) -> p c t", c=EC)

            def low(dst, ps, high):
                return v.tensor_tensor(dst, ps, high.bitcast(F32), ALU.subtract)

            def stats(src, st):
                for t in range(TC):
                    r = v.bn_stats(st[:, t, :], src[:, t, :])
                mark(r)

            def mean_and_variance(st, mv):
                settle(apart=True)
                for t in range(TC):
                    r = v.bn_aggr(mv[:, t, :], st[:, t, :])
                mark(r)

            def add_eps(mv, done):
                settle()
                v.tensor_scalar(mv[:, :, 1], mv[:, :, 1], 1e-5, None, ALU.add).then_inc(done, 1)

            def one(j, c):
                Eb, A, B, S, S2, S3 = (stage(j, c, k) for k in (3, 2, 1, -1, -2, -3))
                spread = [P, TC, NX]

                def early(h):
                    if h == 0 and S3:
                        settle()
                        v.reciprocal(rec[:, :], ssum[:, :])
                        mark(v.tensor_reduce(s2[:, :], ex2[:, :, :], AX, ALU.add))
                    if h == 1 and S3:
                        v.wait_ge(pos_ok, S3.n(1, 1))
                        mark(v.tensor_tensor(pr[:, :], oh[:, :], pos[:, :, :].unsqueeze(1).to_broadcast([P, 2, TC, NX]), ALU.mult))
                    if h == 1 and S2:
                        v.wait_ge(oTh_ok, S2.n(1, 1))
                        low(oT_l[:, :, :], bank_chunks(T0), oT_h[:, :, :]).then_inc(oTl_ok, 1)
                    if h == 2 and S3:
                        settle()
                        moved(v, sc_done, S3.n(64))
                        by_tile = slot[:, :, :].rearrange("p k t -> p t k")
                        v.tensor_copy(slots[:, bass.ds(S3.n(TC), TC), :], by_tile)
                        v.tensor_copy(slot_i[:, :, :], by_tile).then_inc(slot_ok, 1)
                        v.tensor_scalar(wts[:, bass.ds(S3.n(TC), TC), 0], rec[:, :], gsc[:, 1:2], None, ALU.mult)
                        v.tensor_scalar(wts[:, bass.ds(S3.n(TC), TC), 1], s2[:, :], gsc[:, 1:2], None, ALU.mult)
                        v.tensor_tensor(acc[:, 0, :], acc[:, 1, :], msk[:, 1, :], ALU.add).then_inc(acc_ok, 1)
                    if h == 4 and A:
                        v.wait_ge(xnTh_ok, A.n(1, 1))
                        low(xnT_l[:, :, :], bank_chunks(T0), xnT_h[:, :, :]).then_inc(xnTl_ok, 1)
                    if h == 5 and S2:
                        mean_and_variance(bst2, bmv2)
                    if h == 7 and S2:
                        v.wait_ge(rstd2_ok, S2.n(1, 1))
                        if not among_first(S2, 1):
                            v.wait_ge(xn2_st, S2.n(16, 16))
                        for t in range(TC):
                            r = v.tensor_scalar(xn2_s[S2.slot][:, t, :], x2_s[:, t, :], bmv2[:, t, 0:1], rstd2[:, t:t + 1], ALU.subtract, ALU.mult)
                        r.then_inc(xn2_ok, 1)
                    if h == 9 and Eb:
                        moved(v, xn_ok, Eb.n())
                        mean_and_variance(bst, bmv)
                    if h == 12 and S2:
                        v.wait_ge(lgc_ok, S2.n(1, 1))
                        mark(v.tensor_reduce(lmx[:, :], lg[:, :, :], AX, ALU.max))
                    if h == 13 and S2:
                        settle()
                        tri = K[:, C_TRI:C_TRI + NX * NX].rearrange("p (e j) -> p e j", e=NX)
                        mark(v.tensor_tensor(eqm[:, :], eqm[:, :], tri.unsqueeze(1).to_broadcast([P, TC, NX, NX]), ALU.mult))
                    if h == 14 and (S or S2):
                        settle()
                    if h == 14 and S2:
                        mark(v.tensor_reduce(rk[:, :, :], gtm[:, :], AX, ALU.add))
                    if h == 14 and S:
                        for qc, bnk in enumerate((T0, T1)):
                            r = v.tensor_tensor(o_s[:, qc, :].rearrange("p (h d) -> p h d", d=D),
                                                bnk[:, :].rearrange("p (h w) -> p h w", w=PVW)[:, :, 0:D],
                                                rsum[:, qc, :].unsqueeze(2).to_broadcast([P, H, D]), ALU.mult)
                        r.then_inc(o_ok, 1)
                    if h == 15 and S2:
                        settle()
                        link(v.tensor_tensor(msk[:, :, :], oh[:, 0], oh[:, 1], ALU.add))
                        v.tensor_tensor(acc[:, 1, :], acc[:, 0, :], msk[:, 0, :], ALU.add).then_inc(oh_ok, 1)

                def late(h):
                    if h == 0 and S3:
                        settle()
                        mark(v.tensor_tensor(s2[:, :], s2[:, :], rec[:, :], ALU.mult))
                        v.wait_ge(rk_ps, S3.n(1, 1))
                        v.tensor_tensor(pos[:, :, :], rk_p.rearrange("p (t e) -> p t e", t=TC),
                                        K[:, C_EB:C_EB + NX].unsqueeze(1).to_broadcast(spread), ALU.add).then_inc(pos_ok, 1)
                    if h == 1 and S3:
                        settle()
                        mark(v.tensor_reduce(slot[:, :, :], pr[:, :], AX, ALU.add))
                    if h == 3 and S2:
                        v.wait_ge(op_ps, S2.n(2, 2))
                        v.wait_ge(xb_ok, S2.n(1, 1))
                        moved(v, x2_st, S2.n(16))
                        v.scalar_tensor_tensor(x2_s[:, :, :], T1[:, :].rearrange("p (t d) -> p t d", t=TC), gate[:, 0:1],
                                               xr_s[:, :, :], ALU.mult, ALU.add).then_inc(x2_ok, 1)
                    if h == 4 and S2:
                        v.wait_ge(x2_ok, S2.n(1, 1))
                        stats(x2_s, bst2)
                    if h == 5 and S2:
                        add_eps(bmv2, var2_ok)
                    if h == 8 and Eb:
                        v.wait_ge(x_in, Eb.n(16, 16))
                        stats(x_s, bst)
                    if h == 9 and Eb:
                        add_eps(bmv, var1_ok)
                    if h == 11 and S2:
                        v.wait_ge(lg_ps, S2.n(1, 1))
                        v.tensor_copy(lg[:, :, :], lg_p.rearrange("p (t e) -> p t e", t=TC)).then_inc(lgc_ok, 1)
                    if h == 12 and S2:
                        settle()
                        v.tensor_tensor(lgd[:, :, :], lg[:, :, :], lmx[:, :].unsqueeze(2).to_broadcast(spread), ALU.subtract).then_inc(lgd_ok, 1)
                        for t in range(TC):
                            other = lg[:, t, :].unsqueeze(1).to_broadcast([P, NX, NX])
                            own = lg[:, t, :].unsqueeze(2).to_broadcast([P, NX, NX])
                            v.tensor_tensor(gtm[:, t], other, own, ALU.is_gt)
                            r = v.tensor_tensor(eqm[:, t], other, own, ALU.is_equal)
                        mark(r)
                    if h == 13 and S2:
                        settle()
                        mark(v.tensor_tensor(gtm[:, :], gtm[:, :], eqm[:, :], ALU.add))
                    if h == 13 and S:
                        v.wait_ge(oq_ps, S.n(2, 2))
                        moved(v, oT_ps, S.n())
                        for qc, bnk in enumerate((T0, T1)):
                            r = v.reciprocal(rsum[:, qc, :], bnk[:, :].rearrange("p (h w) -> p h w", w=PVW)[:, :, D])
                        mark(r)
                    if h == 14 and S2:
                        settle()
                        v.tensor_scalar(oh[:, 0], rk[:, :, :], 0.0, None, ALU.is_equal)
                        mark(v.tensor_scalar(oh[:, 1], rk[:, :, :], 1.0, None, ALU.is_equal))
                    if h == 15 and S2:
                        v.wait_ge(ex_ok, S2.n(1, 1))
                        v.tensor_reduce(ssum[:, :], ex[:, :, :], AX, ALU.add)
                        mark(v.tensor_tensor(ex2[:, :, :], ex[:, :, :], oh[:, 1], ALU.mult))

                for h in range(H):
                    early(h)
                    if B:
                        v.wait_ge(sm_ps, B.n(H, h + 1))
                        if h == 0:
                            moved(v, mT_ps, B.n(1, 1 - R))
                        v.tensor_reduce(mx[B.slot][:, :, 8 * (h % 2) + h // 2], SM[h % 2][:, :].rearrange("p (t k) -> p t k", t=TC),
                                        AX, ALU.max).then_inc(mx_ok, 1)
                    late(h)
                if S and among_first(S, NB) and S.b == NB - 2:
                    for i in range(WP):
                        v.wait_ge(w_used, i + 1)
                        v.tensor_tensor(w_l0[:, part(i)], wraw[:, part(i)], w_h0[:, part(i)].bitcast(F32), ALU.subtract).then_inc(w_ok, 1)
                if Eb and among_first(Eb, R):
                    if Eb.b == 0:
                        weights_low()
                    clear_k(Eb.b)
                    if Eb.b == 0:
                        scale_gates()

            for i in range(-R, LOOP0):
                one(0, i)
            seen.update(base=seen["base"] + seen["k"], k=0, per=LINKS_PER_LOOP)
            with v.Fori(0, TRIPS) as j:
                seen["j"] = j
                for c in range(LOOP0, LOOP0 + R):
                    one(j, c)
            assert seen["k"] == LINKS_PER_LOOP, seen["k"]
            seen.update(base=seen["base"] + TRIPS * LINKS_PER_LOOP, k=0, j=None)
            for i in range(LOOP0 + R * TRIPS, NB + 3):
                one(0, i)

            v.wait_ge(cnt_ps, 1)
            link(v.tensor_copy(cnt[:, :], T0[:, 0:NX]))
            link(v.tensor_tensor(tabf[:, T_Z:T_Z + NX], cnt[:, :], K[:, C_EB:C_EB + NX], ALU.add))
            v.tensor_copy(tab[0:1, T_Z:T_Z + NX], tabf[0:1, T_Z:T_Z + NX]).then_inc(ends_ok, 1)
            link(v.tensor_tensor(tge[:, :, :], cnt[:, :].unsqueeze(2).to_broadcast([P, NX, NTHR]),
                                 K[:, C_THR:C_THR + NTHR].unsqueeze(1).to_broadcast([P, NX, NTHR]), ALU.is_gt))
            link(v.tensor_reduce(ntl[:, :], tge[:, :, :], AX, ALU.add))
            link(v.tensor_scalar(ntl[:, :], ntl[:, :], 2.0, None, ALU.max))
            before = K[:, C_TRI:C_TRI + NX * NX].rearrange("p (e j) -> p e j", e=NX)
            link(v.tensor_tensor(tpe[:, :, :], before, ntl[:, :].unsqueeze(1).to_broadcast([P, NX, NX]), ALU.mult))
            link(v.tensor_reduce(tend[:, :], tpe[:, :, :], AX, ALU.add))
            link(v.tensor_tensor(tend[:, :], tend[:, :], ntl[:, :], ALU.add))
            v.tensor_copy(tabf[:, T_E:T_E + NX], tend[:, :])
            v.tensor_tensor(tabf[:, T_B:T_B + NX], tend[:, :], ntl[:, :], ALU.subtract)
            link(v.tensor_tensor(tgt[:, :, :], tend[:, :].unsqueeze(1).to_broadcast([P, NT, NX]),
                                 K[:, C_TI:C_TI + NT].unsqueeze(2).to_broadcast([P, NT, NX]), ALU.is_le))
            v.tensor_reduce(te_n[:, :], tgt[:, :, :], AX, ALU.add)
            link(v.tensor_tensor(tpr[:, :, :], tgt[:, :, :], ntl[:, :].unsqueeze(1).to_broadcast([P, NT, NX]), ALU.mult))
            link(v.tensor_reduce(tb_n[:, :], tpr[:, :, :], AX, ALU.add))
            link(v.tensor_scalar(te_n[:, :], te_n[:, :], float(NX - 1), float(REG), ALU.min, ALU.mult))
            link(v.tensor_tensor(tb_n[:, :], K[:, C_TI:C_TI + NT], tb_n[:, :], ALU.subtract))
            link(v.scalar_tensor_tensor(tabf[:, T_ROW:T_ROW + NT], tb_n[:, :], float(P), te_n[:, :], ALU.mult, ALU.add))
            v.tensor_scalar(tabf[:, T_L3:T_L3 + 1], tend[:, NX - 1:NX], -3.0, None, ALU.add)
            v.tensor_scalar(tabf[:, T_L1:T_L1 + 1], tend[:, NX - 1:NX], -1.0, None, ALU.add)
            link(v.tensor_scalar(tabf[:, T_P:T_P + NX], tabf[:, T_B:T_B + NX], -1.0, 0.0, ALU.add, ALU.max))
            v.tensor_copy(tab[0:1, 0:T_Z], tabf[0:1, 0:T_Z])
            v.tensor_copy(tab[0:1, T_P:TW], tabf[0:1, T_P:TW]).then_inc(tab_ok, 1)
            v.wait_ge(tab_ok, 1)
            total = v.value_load(tab[0:1, T_E + NX - 1:T_E + NX], min_val=2 * NX, max_val=NT)

            def x_low(u):
                v.wait_ge(xh_ok, u + 1)
                low(xg_l[:, :, :], psX[:, 0:E].rearrange("p (c t) -> p c t", c=EC), xg_h[:, :, :]).then_inc(xl_ok, 1)

            def gated(u):
                v.wait_ge(sg_ok, u + 1)
                v.wait_ge(h3_ps, u + 1)
                moved(v, gT_ps, u)
                v.tensor_tensor(gg[:, :], sg[:, :], psH3[:, :], ALU.mult).then_inc(g_ok, 1)

            def g_low(u):
                v.wait_ge(gh_ok, u + 1)
                low(gT_l[:, :, :], psG[:, :].rearrange("p (c t) -> p c t", c=FC), gT_h[:, :, :]).then_inc(gl_ok, 1)

            x_low(0)
            link(v.scalar_tensor_tensor(dlt[:, :], tabf[:, T_B:T_B + NX], float(P), K[:, C_EB:C_EB + NX], ALU.mult, ALU.subtract))
            link(v.tensor_copy(cnt[:, :], dlt[:, :]))
            link(v.tensor_tensor(dlt[:, 1:NX], cnt[:, 1:NX], cnt[:, 0:NX - 1], ALU.subtract))
            flat = slots[:, :, :].rearrange("p t k -> p (t k)")
            link(v.tensor_tensor(gge[:, :, :], flat.unsqueeze(2).to_broadcast([P, NST * 2, NX]),
                                 K[:, C_EB:C_EB + NX].unsqueeze(1).to_broadcast([P, NST * 2, NX]), ALU.is_ge))
            link(v.tensor_tensor(gge[:, :, :], gge[:, :, :], dlt[:, :].unsqueeze(1).to_broadcast([P, NST * 2, NX]), ALU.mult))
            link(v.tensor_reduce(gf[:, :], gge[:, :, :], AX, ALU.add))
            v.tensor_tensor(gidx[:, :, :].rearrange("p t k -> p (t k)"), gf[:, :], flat, ALU.add).then_inc(idx_ok, 1)
            base = seen["base"] + seen["k"]

            def combine(k, p, turn):
                v.wait_ge(y_ok, total + k + 2)
                v.wait_ge(mg_in[p], turn * 16 + 16)
                v.wait_ge(ig_ok, k + 1)
                v.wait_ge(yg_in[p], turn * 32 + 32)
                moved(v, o_st[p], turn * 16)
                v.scalar_tensor_tensor(yga[p][:, :], yga[p][:, :], wg[p][:, 0:1], x2g[p][:, :], ALU.mult, ALU.add).then_inc(chain, 1)
                v.wait_ge(chain, base + 2 * k + 1)
                v.scalar_tensor_tensor(ygb[p][:, :], ygb[p][:, :], wg[p][:, 1:2], yga[p][:, :], ALU.mult, ALU.add).then_inc(chain, 1)
                v.wait_ge(chain, base + 2 * k + 2)
                v.scalar_tensor_tensor(o_o[p][:, :], ysh[p][:, :], gsc[:, 0:1], ygb[p][:, :], ALU.mult, ALU.add).then_inc(cmb_ok, 1)

            def take(k, p):
                moved(v, cmb_ok, k - 1)
                v.tensor_copy(wg[p][:, :], wts[:, bass.ds(k, 1), :].rearrange("p t k -> p (t k)"))
                v.tensor_copy(ig[p][:, :], gidx[:, bass.ds(k, 1), :].rearrange("p t k -> p (t k)")).then_inc(ig_ok, 1)

            v.wait_ge(idx_ok, 1)
            take(0, 0)
            take(1, 1)
            gated(0)
            x_low(1)
            g_low(0)
            with v.Fori(1, total + 1) as u:
                gated(u)
                x_low(u + 1)
                g_low(u)

            def shared(jj, p):
                k = 2 * jj + (2 - p)
                gated(total + k)
                x_low(total + k + 1)
                if not isinstance(k, int) or k >= 2:
                    take(k, p)
                g_low(total + k)
                combine(k - 1, 1 - p, jj)

            shared(0, 1)
            shared(0, 0)
            with v.Fori(1, (NST - 2) // 2) as jj:
                shared(jj, 1)
                shared(jj, 0)
            k = NST - 1
            gated(total + k)
            take(k, 1)
            g_low(total + k)
            combine(k - 1, 0, (k - 1) // 2)
            combine(k, 1, k // 2)

        @block.gpsimd
        def _(po):
            def load_w(k, i):
                moved(po, w_ok, (k - 1) * WP + i + 1)
                po.dma_start(wraw[:, part(i)], wall[k][:, part(i)]).then_inc(w_in[i], 16)

            def cut(k, p, tiles=None):
                for i in range(WP):
                    po.wait_ge(w_in[i], 16 * (k + 1))
                    if tiles is not None and i == 0:
                        po.wait_ge(w2_ps, tiles)
                    po.tensor_copy(w_h[p][:, part(i)], wraw[:, part(i)]).then_inc(w_used, 1)
                    po.wait_ge(w_used, k * WP + i + 1)
                    po.tensor_tensor(w_l[p][:, part(i)], wraw[:, part(i)], w_h[p][:, part(i)].bitcast(F32), ALU.subtract).then_inc(w_ok, 1)
                    if k < NX:
                        load_w(k + 1, i)

            def carry(n):
                po.wait_ge(spare_ok, n + 1)
                po.tensor_tensor(spare_p[:, 1:2], spare_p[:, 0:1], spare_p[:, 0:1], ALU.add).then_inc(spare_ok, 1)

            po.memset(spare_p[:, :], 0.0).then_inc(spare_ok, 1)
            po.wait_ge(spare_ok, 1)
            po.wait_ge(k_in, 16)

            def one(j, c):
                Eb, A, S, S2, S3 = (stage(j, c, k) for k in (3, 2, -1, -2, -3))

                def root(mv, rs, asked, b, done):
                    po.wait_ge(asked, b.n(1, 1))
                    po.tensor_tensor(rs[:, :], mv[:, :, 1], K[:, C_MH:C_MH + 1].to_broadcast([P, TC]), ALU.pow).then_inc(done, 1)

                def leave_low(side, high_ok, done):
                    po.wait_ge(high_ok, A.n(1, 1))
                    high, rest = (qk_s[:, 4 * side + 2 * half:4 * side + 2 * half + 2, :] for half in range(2))
                    po.tensor_tensor(rest, rest.bitcast(F32), high.bitcast(F32), ALU.subtract).then_inc(done, 1)

                if A:
                    leave_low(1, kh_ok, kl_ok)
                if S3:
                    po.wait_ge(slot_ok, S3.n(1, 1))
                    carry(S3.b)
                    for t in range(TC):
                        for k in range(2):
                            po.indirect_dma_start(
                                out=xs_d, out_offset=bass.IndirectOffsetOnAxis(ap=slot_i[:, t, k:k + 1].bitcast(U32), axis=0),
                                in_=xn2_s[S3.slot][:, t, :], in_offset=None).then_inc(sc_done, 16)
                if S2:
                    root(bmv2, rstd2, var2_ok, S2, rstd2_ok)
                if A:
                    leave_low(0, qh_ok, ql_ok)
                if Eb:
                    root(bmv, rstd, var1_ok, Eb, rstd1_ok)
                    moved(po, xnT_ps, Eb.n())
                    po.tensor_tensor(xn_s[:, :, :], x_s[:, :, :], bmv[:, :, 0:1].to_broadcast([P, TC, E]), ALU.subtract).then_inc(xc_ok, 1)
                    po.wait_ge(rstd1_ok, Eb.n(1, 1))
                    po.wait_ge(xc_ok, Eb.n(1, 1))
                    po.tensor_tensor(xn_s[:, :, :], xn_s[:, :, :], rstd[:, :].unsqueeze(2).to_broadcast([P, TC, E]), ALU.mult).then_inc(xn_ok, 1)
                if S:
                    if among_first(S, 1):
                        po.wait_ge(gbo_ok, 1)
                    po.wait_ge(xr_in, S.n(16, 16))
                    po.tensor_tensor(xr_s[:, :, :], xr_s[:, :, :], gbo[:, :].unsqueeze(1).to_broadcast([P, TC, E]), ALU.add).then_inc(xb_ok, 1)
                if Eb:
                    po.wait_ge(ch_ok, Eb.n(1, 1))
                    moved(po, v_ps, Eb.n(2))
                    po.tensor_tensor(c_l[:, :, :], c_s[:, :, :], c_h[:, :, :].bitcast(F32), ALU.subtract).then_inc(cl_ok, 1)
                if A:
                    if among_first(A, 1):
                        po.wait_ge(few_in, 80)
                    po.wait_ge(vr_ok, A.n(1, 1))
                    ring = v_s[A.slot][:, :, :, 0:D]
                    po.tensor_tensor(ring, ring, bv_s[:, :].rearrange("p (h d) -> p h d", h=H).unsqueeze(1).to_broadcast([P, TC, H, D]),
                                     ALU.add).then_inc(v_ok, 1)
                if Eb and among_first(Eb, 2) and Eb.b == 1:
                    for i in range(WP):
                        load_w(0, i)
                if S and among_first(S, NB) and S.b == NB - 1:
                    for i in range(WP):
                        load_w(1, i)

            iterations(po, one)

            po.wait_ge(tab_ok, 1)
            cut(1, 1)
            for k in range(2, NX + 1):
                te = po.value_load(tab[0:1, T_E + k - 2:T_E + k - 1], min_val=2, max_val=NT)
                cut(k, k % 2, te)
            total = po.value_load(tab[0:1, T_E + NX - 1:T_E + NX], min_val=2 * NX, max_val=NT)
            with po.Fori(0, NST // 2) as jj:
                for p in range(2):
                    po.wait_ge(y_st, total * 16)
                    po.wait_ge(ig_ok, 2 * jj + (1 + p))
                    carry(2 * jj + (NB + p))
                    for k, dst in enumerate((yga, ygb)):
                        po.indirect_dma_start(
                            out=dst[p][:, :], out_offset=None, in_=ys_d,
                            in_offset=bass.IndirectOffsetOnAxis(ap=ig[p][:, k:k + 1].bitcast(U32), axis=0)).then_inc(yg_in[p], 16)


LINKS_PER_LOOP = 3 * 17


def kernel(**inputs):
    import numpy as _np
    import concourse.bacc as _bacc
    from concourse import mybir as _mybir
    from concourse.bass_utils import run_bass_kernel_spmd as _run

    a = {k: _np.asarray(v) for k, v in inputs.items()}
    P_ = 128

    def chunks(w):
        return w.reshape(-1, P_, w.shape[-1]).transpose(1, 0, 2)

    def rows(v):
        return _np.broadcast_to(v[None, :], (P_, v.shape[0]))

    wT = _np.stack([chunks(a["L0_xattn_" + n].T) for n in ("Wq", "Wk", "Wv", "Wo")])
    experts = [(a["L0_ffn_w1"][e], a["L0_ffn_w3"][e], a["L0_ffn_w2"][e]) for e in range(8)]
    experts.append((a["L0_ffn_ws1"], a["L0_ffn_ws3"], a["L0_ffn_ws2"]))
    wall = _np.stack([_np.concatenate([chunks(m).reshape(P_, -1) for m in e], axis=1) for e in experts])
    arrays = {
        "x": a["x"],
        "ctxT": a["ctx_1024"].transpose(0, 2, 1),
        "gates": rows(_np.concatenate([a["g_xattn"], a["g_ffn"]])),
        "wT": wT,
        "bqk": _np.concatenate([a["L0_xattn_bq"].reshape(2, P_), a["L0_xattn_bk"].reshape(2, P_)]).T,
        "bvo": _np.stack([rows(a["L0_xattn_bv"]), rows(a["L0_xattn_bo"])]),
        "wr": chunks(a["L0_ffn_w_router"]),
        "wall": wall,
        "cst": constants(),
    }
    arrays = {k: _np.ascontiguousarray(v) for k, v in arrays.items()}
    nc = _bacc.Bacc("TRN2", target_bir_lowering=False, num_devices=1)
    args = [nc.dram_tensor(k, v.shape, _mybir.dt.from_np(v.dtype), kind="ExternalInput").ap() for k, v in arrays.items()]
    o = nc.dram_tensor("out", (NTOK, E), _mybir.dt.float32, kind="ExternalOutput").ap()
    build(nc, *args, o)
    r = _run(nc, [arrays], core_ids=[0])
    return r.results[0]["out"].reshape(16, 256, 256)
```

```python
from contextlib import ExitStack

import numpy as np
import concourse.bass as bass
from concourse import mybir

F32 = mybir.dt.float32
F32R = mybir.dt.float32r
I32 = mybir.dt.int32
U32 = mybir.dt.uint32
ALU = mybir.AluOpType
ACT = mybir.ActivationFunctionType
AX = mybir.AxisListType.X

P = 128
NB, L, E = 16, 256, 256
H, D = 16, 16
NX, HID = 8, 512
TC = L // P
EC = E // P
FC = HID // P
NTOK = NB * L
R = 3
LOOP0, TRIPS = 3, 3
W_ORDER = (1, 0, 2, 3)
LATE = 4
WP = 3
PVW = 32
TR = 256
TS = TR // P
REG = NTOK + 2 * TR
NT = (2 * NTOK) // TR + 2 * NX
WSZ = 2 * EC * HID + FC * E
W3O, W2O = EC * HID, 2 * EC * HID
NST = NTOK // P
NS = NTOK // TR

C_ID, C_UP, C_ONE, C_MROW = 0, P, 2 * P, 3 * P
C_EB = C_MROW + H
C_TRI = C_EB + NX
C_THR = C_TRI + NX * NX
NTHR = NTOK // TR + 1
C_TI = C_THR + NTHR
C_MH = C_TI + NT
CW = C_MH + 1

T_ROW, T_B, T_E, T_Z = 0, NT, NT + NX, NT + 2 * NX
T_L3, T_L1 = T_Z + NX, T_Z + NX + 1
TW = T_L1 + 1


def constants():
    c = np.zeros((P, CW), np.float32)
    c[:, C_ID:C_ID + P] = np.eye(P)
    c[:, C_UP:C_UP + P] = np.triu(np.ones((P, P)), 1)
    c[:, C_ONE:C_ONE + P] = 1.0
    c[P - 2, C_MROW:C_MROW + H:2] = 1.0
    c[P - 1, C_MROW + 1:C_MROW + H:2] = 1.0
    c[:, C_EB:C_EB + NX] = np.arange(NX) * REG
    c[:, C_TRI:C_TRI + NX * NX] = np.tril(np.ones((NX, NX)), -1).reshape(-1)
    c[:, C_THR:C_THR + NTHR] = np.arange(NTHR) * TR
    c[:, C_TI:C_TI + NT] = np.arange(NT)
    c[:, C_MH] = -0.5
    return c


def moved(e, sem, value):
    if isinstance(value, int) and value <= 0:
        return
    e.wait_ge(sem, value)


class Batch:

    def __init__(self, j, c):
        self.b = R * j + c
        self.slot = c % R
        self.turn = j + c // R

    def n(self, per=1, k=0):
        return self.b * per + k


def build(nc, x, ctxT, gates, wT, bqk, bvo, wr, wall, cst, out):
    with ExitStack() as keep:
        def sem(name):
            return keep.enter_context(nc.semaphore(name))

        def sb(stack, name, shape, dt=F32):
            return stack.enter_context(nc.sbuf_tensor(name, shape, dt))

        qk_d = nc.dram_tensor("qk_d", (R, 8, P, L), F32, kind="Internal").ap()
        xs_d = nc.dram_tensor("xs_d", (NX * REG, E), F32, kind="Internal").ap()
        ys_d = nc.dram_tensor("ys_d", (NT * TR, E), F32, kind="Internal").ap()
        xn2_d = nc.dram_tensor("xn2_d", (NTOK, E), F32, kind="Internal").ap()
        x2_d = nc.dram_tensor("x2_d", (NTOK, E), F32, kind="Internal").ap()

        K = sb(keep, "consts", [P, CW])
        ident = K[:, C_ID:C_ID + P]
        gt = sb(keep, "gates_sb", [P, 2])
        gate = sb(keep, "gate_tanh", [P, 2])
        gsc = sb(keep, "gate_scaled", [P, 2])
        acc = sb(keep, "mask_total", [P, TC, NX])
        wraw = sb(keep, "w_raw", [P, WSZ])
        w_h0 = sb(keep, "w_h0", [P, WSZ], F32R)
        w_l0 = sb(keep, "w_l0", [P, WSZ], F32R)
        tab = sb(keep, "table", [1, TW], I32)
        spare_v = sb(keep, "spare_v", [P, 1])
        spare_p = sb(keep, "spare_p", [P, 2])
        zero = sb(keep, "zero_rows", [P, E])
        slots = sb(keep, "slots_all", [P, NST, 2])
        wts = sb(keep, "router_wts", [P, NST, 2])

        with ExitStack() as a:
            wt_h = sb(a, "wt_h", [P, 4, EC, E], F32R)
            wt_l = sb(a, "wt_l", [P, 4, EC, E], F32R)
            bqk_s = sb(a, "bqk_s", [P, 4])
            bv_s = sb(a, "bv_s", [P, E])
            gbo = sb(a, "gated_bo", [P, E])
            wr_s = sb(a, "wr_s", [P, EC, NX])
            x_s = sb(a, "x_s", [P, TC, E])
            xr_s = sb(a, "x_residual", [P, TC, E])
            c_s = sb(a, "c_s", [P, EC, L])
            xn_s = sb(a, "xn_s", [P, TC, E])
            bst = sb(a, "bn_st", [P, TC, 6])
            bmv = sb(a, "bn_mv", [P, TC, 2])
            rstd = sb(a, "rstd", [P, TC])
            bst2 = sb(a, "bn_st2", [P, TC, 6])
            bmv2 = sb(a, "bn_mv2", [P, TC, 2])
            rstd2 = sb(a, "rstd2", [P, TC])
            xnT_h = sb(a, "xnT_h", [P, EC, L], F32R)
            xnT_l = sb(a, "xnT_l", [P, EC, L], F32R)
            c_h = sb(a, "c_h", [P, EC, L], F32R)
            c_l = sb(a, "c_l", [P, EC, L], F32R)
            qk_s = sb(a, "qk_s", [P, 8, L], F32R)
            q4 = [sb(a, f"q4_{i}", [P, H // 2, L], F32R) for i in range(R)]
            k4 = [sb(a, f"k4_{i}", [P, H, L], F32R) for i in range(R)]
            v_s = [sb(a, f"v_{i}", [P, TC, H, PVW]) for i in range(R)]
            mx = [sb(a, f"row_max_{i}", [P, TC, H]) for i in range(R)]
            mT = sb(a, "minus_max_T", [H, L], F32R)
            pT = sb(a, "probs_T", [P, 8, TC * L])
            wt_raw = pT[:, 0:4, :]
            oT_s = sb(a, "oT_s", [P, 4, L])
            rsum = sb(a, "rsum", [P, TC, H])
            o_s = sb(a, "o_s", [P, TC, E])
            oT_h = sb(a, "oT_h", [P, EC, L], F32R)
            oT_l = sb(a, "oT_l", [P, EC, L], F32R)
            x2_s = sb(a, "x2_s", [P, TC, E])
            xn2_s = [sb(a, f"xn2_{i}", [P, TC, E]) for i in range(R)]
            xn2T = sb(a, "xn2T", [P, EC, L])
            lg = sb(a, "logits", [P, TC, NX])
            lgd = sb(a, "logits_less_max", [P, TC, NX])
            lmx = sb(a, "logit_max", [P, TC])
            ex = sb(a, "router_exp", [P, TC, NX])
            gtm = sb(a, "count_greater", [P, TC, NX, NX])
            eqm = sb(a, "count_equal", [P, TC, NX, NX])
            rk = sb(a, "rank_in_row", [P, TC, NX])
            oh = sb(a, "one_hot", [P, 2, TC, NX])
            msk = sb(a, "mask", [P, TC, NX])
            pr = sb(a, "products", [P, 2, TC, NX])
            ssum = sb(a, "score_sum", [P, TC])
            rec = sb(a, "score_rec", [P, TC])
            s2 = sb(a, "score_second", [P, TC])
            ex2 = sb(a, "exp_second", [P, TC, NX])
            pos = sb(a, "list_pos", [P, TC, NX])
            slot = sb(a, "slot_f", [P, 2, TC])
            slot_i = sb(a, "slot_i", [P, TC, 2], I32)
        with ExitStack() as m:
            w_h = [w_h0, sb(m, "w_h1", [P, WSZ], F32R)]
            w_l = [w_l0, sb(m, "w_l1", [P, WSZ], F32R)]
            xg = sb(m, "xg", [P, TS, E])
            xg_h = sb(m, "xg_h", [P, EC, TR], F32R)
            xg_l = sb(m, "xg_l", [P, EC, TR], F32R)
            sg = sb(m, "sg", [P, FC, TR])
            gg = sb(m, "gg", [P, FC, TR])
            gT_h = sb(m, "gT_h", [P, FC, TR], F32R)
            gT_l = sb(m, "gT_l", [P, FC, TR], F32R)
            y_s = sb(m, "y_s", [P, TS, E])
            ysh = sb(m, "ysh", [P, TS, E])
            yga = [sb(m, f"yga_{i}", [P, E]) for i in range(2)]
            ygb = [sb(m, f"ygb_{i}", [P, E]) for i in range(2)]
            x2g = [sb(m, f"x2g_{i}", [P, E]) for i in range(2)]
            wg = [sb(m, f"wg_{i}", [P, 2]) for i in range(2)]
            ig = [sb(m, f"ig_{i}", [P, 2], I32) for i in range(2)]
            gidx = sb(m, "gather_rows", [P, NST, 2], I32)
            gf = sb(m, "gather_f", [P, NST * 2])
            gge = sb(m, "gather_ge", [P, NST * 2, NX])
            dlt = sb(m, "list_shift", [P, NX])
            mixed = [sb(m, f"mixed_{i}", [P, E]) for i in range(2)]
            o_o = [sb(m, f"oo_{i}", [P, E]) for i in range(2)]
            cnt = sb(m, "cnt", [P, NX])
            tge = sb(m, "tge", [P, NX, NTHR])
            ntl = sb(m, "ntl", [P, NX])
            tend = sb(m, "tend", [P, NX])
            tgt = sb(m, "tgt", [P, NT, NX])
            tpr = sb(m, "tpr", [P, NT, NX])
            tpe = sb(m, "tpe", [P, NX, NX])
            te_n = sb(m, "te_n", [P, NT])
            tb_n = sb(m, "tb_n", [P, NT])
            tabf = sb(m, "tabf", [P, TW])

        bank = [keep.enter_context(nc.psum_tensor(f"bank{i}", [P, 512], F32)) for i in range(8)]
        SS, SM, T2, T0, T1 = bank[0:2], bank[2:4], bank[5], bank[6], bank[7]
        OT = [bank[4][:, 0:L], bank[4][:, L:2 * L]]
        mT_p, lg_p, rk_p = bank[4][0:H, 0:L], T1[:, 0:TC * NX], T1[:, 0:TC * NX]
        psX, psY, psH1, psH3 = bank[0], bank[2], bank[3:5], bank[5:7]

        k_in = sem("k_in"); wt_in = [sem(f"wt_in{w}") for w in range(4)]; wth_ok = sem("wth_ok"); wtl_ok = sem("wtl_ok"); few_in = sem("few_in")
        zero_ok = sem("zero_ok"); q_zero = sem("q_zero"); k_init = sem("k_init"); gate_ok = sem("gate_ok"); gbo_ok = sem("gbo_ok")
        x_in = sem("x_in"); xr_in = sem("xr_in"); c_in = sem("c_in")
        var1_ok = sem("var1_ok"); rstd1_ok = sem("rstd1_ok"); var2_ok = sem("var2_ok"); rstd2_ok = sem("rstd2_ok")
        xn_ok = sem("xn_ok"); xc_ok = sem("xc_ok"); xnT_ps = sem("xnT_ps"); xnTh_ok = sem("xnTh_ok"); xnTl_ok = sem("xnTl_ok")
        ch_ok = sem("ch_ok"); cl_ok = sem("cl_ok")
        q_ps = sem("q_ps"); qh_ok = sem("qh_ok"); ql_ok = sem("ql_ok")
        k_ps = sem("k_ps"); kh_ok = sem("kh_ok"); kl_ok = sem("kl_ok")
        v_ps = sem("v_ps"); vr_ok = sem("vr_ok"); v_ok = sem("v_ok")
        qk_st = sem("qk_st"); stk = [sem(f"stk{i}") for i in range(R)]
        sm_ps = sem("sm_ps"); mx_ok = sem("mx_ok"); mT_ps = sem("mT_ps"); mT_ok = sem("mT_ok")
        mrow = sem("mrow")
        ss_ps = sem("ss_ps"); exp_ok = sem("exp_ok"); pv_ps = sem("pv_ps"); ot_ok = sem("ot_ok")
        oq_ps = sem("oq_ps"); o_ok = sem("o_ok"); oT_ps = sem("oT_ps"); oTh_ok = sem("oTh_ok")
        oTl_ok = sem("oTl_ok"); op_ps = sem("op_ps"); xb_ok = sem("xb_ok")
        x2_ok = sem("x2_ok"); xn2_ok = sem("xn2_ok"); x2_st = sem("x2_st"); xn2_st = sem("xn2_st")
        xn2T_ps = sem("xn2T_ps"); xn2T_ok = sem("xn2T_ok"); lg_ps = sem("lg_ps"); lgc_ok = sem("lgc_ok"); pos_ok = sem("pos_ok"); lgd_ok = sem("lgd_ok")
        ex_ok = sem("ex_ok"); oh_ok = sem("oh_ok"); rk_ps = sem("rk_ps"); slot_ok = sem("slot_ok")
        sc_done = sem("sc_done"); acc_ok = sem("acc_ok")
        chain = sem("chain")
        cnt_ps = sem("cnt_ps"); tab_ok = sem("tab_ok"); ends_ok = sem("ends_ok"); z_first = sem("z_first"); z_done = sem("z_done"); ys_zero = sem("ys_zero"); idx_ok = sem("idx_ok"); ig_ok = sem("ig_ok")
        w_in = [sem(f"w_in{i}") for i in range(WP)]; w_used = sem("w_used"); w_ok = sem("w_ok")
        xg_in = sem("xg_in"); xt_ps = sem("xt_ps"); xh_ok = sem("xh_ok"); xl_ok = sem("xl_ok")
        h1_ps = sem("h1_ps"); h3_ps = sem("h3_ps"); sg_ok = sem("sg_ok"); g_ok = sem("g_ok")
        gh_ok = sem("gh_ok"); gl_ok = sem("gl_ok"); w2_ps = sem("w2_ps")
        y_ok = sem("y_ok"); y_st = sem("y_st")
        mg_in = [sem(f"mg_in{i}") for i in range(2)]; yg_in = [sem(f"yg_in{i}") for i in range(2)]
        spare_ok = sem("spare_ok"); mix_ok = sem("mix_ok"); cmb_ok = sem("cmb_ok"); o_st = [sem(f"o_st{i}") for i in range(2)]

        block = keep.enter_context(nc.Block())

        def iterations(e, one):
            for i in range(-R, LOOP0):
                one(0, i)
            with e.Fori(0, TRIPS) as j:
                for c in range(LOOP0, LOOP0 + R):
                    one(j, c)
            for i in range(LOOP0 + R * TRIPS, NB + 3):
                one(0, i)

        def among_first(batch, n):
            return isinstance(batch.b, int) and batch.b < n

        def late_head(C, S, h):
            return (S, H - LATE + h) if h < LATE else (C, h - LATE)

        def parts(rows_d, first, n):
            return rows_d[bass.ds(first, n), :].rearrange("(t p) d -> p t d", p=P)

        def clear_behind(e, lists, done):
            for k in lists:
                z = e.value_load(tab[0:1, T_Z + k:T_Z + k + 1], min_val=0, max_val=NX * REG - 2 * TR)
                e.dma_start(xs_d[bass.ds(z, 2 * TR), :].rearrange("(t p) d -> p t d", p=P),
                            zero[:, :].unsqueeze(1).to_broadcast([P, 2 * TS, E])).then_inc(done, 16)

        def part(i):
            return slice(i * WSZ // WP, (i + 1) * WSZ // WP)

        def stage(j, c, ahead):
            if isinstance(j, int) and not 0 <= R * j + c + ahead < NB:
                return None
            return Batch(j, c + ahead)

        @block.sync
        def _(sp):
            def load_x(n):
                moved(sp, xn_ok, n.n())
                sp.dma_start(x_s[:, :, :], x[bass.ds(n.b, 1)].rearrange("b (t p) d -> p (b t) d", p=P)).then_inc(x_in, 16)

            def load_c(n):
                sp.dma_start(c_s[:, :, :], ctxT[bass.ds(n.b, 1)].rearrange("b (c p) t -> p (b c) t", p=P)).then_inc(c_in, 16)

            sp.sem_inc(xn2_st, R * 16)
            load_x(Batch(0, 0))
            sp.dma_start(K[:, :], cst).then_inc(k_in, 16)
            load_c(Batch(0, 0))
            for w in W_ORDER:
                sp.dma_start(wt_raw[:, w, :], wT[w].rearrange("p c n -> p (c n)")).then_inc(wt_in[w], 16)
            sp.dma_start(gt[:, :], gates).then_inc(few_in, 16)
            sp.dma_start(bqk_s[:, :], bqk).then_inc(few_in, 16)
            sp.dma_start(bv_s[:, :], bvo[0]).then_inc(few_in, 16)
            sp.dma_start(gbo[:, :], bvo[1]).then_inc(few_in, 16)
            sp.dma_start(wr_s[:, :, :], wr).then_inc(few_in, 16)

            def halves_out(A, side):
                if side == 1:
                    moved(sp, ss_ps, A.n(H, -(R - 1) * H))
                if among_first(A, R):
                    sp.wait_ge((q_zero, k_init)[side], A.b + 1)
                for s in ((qh_ok, ql_ok), (kh_ok, kl_ok))[side]:
                    sp.wait_ge(s, A.n(1, 1))
                sp.dma_start(qk_d[A.slot, 4 * side:4 * side + 4].rearrange("c p t -> p c t"),
                             qk_s[:, 4 * side:4 * side + 4, :].bitcast(F32)).then_inc(qk_st, 16)
                sp.wait_ge(qk_st, A.n(32, 32 - 16 * side))
                for par in range(2):
                    for first, terms, half in (((0, 1, 1), (1, 2, 0)), ((0, 2, 0), (2, 1, 1)))[side]:
                        c8 = 4 * side + 2 * half
                        rows = qk_d[A.slot, c8:c8 + 2].rearrange("c p t -> (c p) t")
                        rows = rows.rearrange("(s q d) t -> q d s t", q=2, d=D)[par]
                        for term in range(first, first + terms):
                            r0 = 64 * par + D * term
                            dst = (q4[A.slot][r0:r0 + D, :, :] if side == 0
                                   else k4[A.slot][r0:r0 + D, par:H:2, :])
                            sp.dma_start(dst.bitcast(F32), rows).then_inc(stk[A.slot], 16)

            def one(j, c):
                X, Eb, A, C, S, S2 = (stage(j, c, k) for k in (4, 3, 2, 0, -1, -2))
                if C:
                    sp.wait_ge(mT_ok, C.n(1, 1))
                    for par in range(2):
                        sp.dma_start(q4[C.slot][P - 2 + par:P - 1 + par, :, :].bitcast(F32), mT[8 * par:8 * par + 8, :].bitcast(F32)).then_inc(mrow, 16)
                if Eb:
                    moved(sp, ch_ok, Eb.n())
                    moved(sp, cl_ok, Eb.n())
                    if not among_first(Eb, 1):
                        load_c(Eb)
                if C:
                    sp.dma_start(ys_d[bass.ds(C.n(NT * TR // NB), NT * TR // NB), :].rearrange("(t p) d -> p t d", p=P), zero[:, :].unsqueeze(1).to_broadcast([P, NT * TS // NB, E])).then_inc(ys_zero, 16)
                if A:
                    halves_out(A, 1)
                if S2:
                    sp.wait_ge(x2_ok, S2.n(1, 1))
                    sp.dma_start(x2_d[bass.ds(S2.n(L), L), :].rearrange("(t p) d -> p t d", p=P), x2_s[:, :, :]).then_inc(x2_st, 16)
                if S:
                    sp.dma_start(xr_s[:, :, :], x[bass.ds(S.b, 1)].rearrange("b (t p) d -> p (b t) d", p=P)).then_inc(xr_in, 16)
                if S2:
                    sp.wait_ge(xn2_ok, S2.n(1, 1))
                    sp.dma_start(xn2_d[bass.ds(S2.n(L), L), :].rearrange("(t p) d -> p t d", p=P), xn2_s[S2.slot][:, :, :]).then_inc(xn2_st, 16)
                if A:
                    halves_out(A, 0)
                if X:
                    load_x(X)

            iterations(sp, one)

            sp.wait_ge(ends_ok, 1)
            clear_behind(sp, (0,), z_first)
            sp.wait_ge(sc_done, NB * 64)
            sp.wait_ge(z_first, 16)
            sp.dma_start(xg[:, :, :], parts(xs_d, 0, TR)).then_inc(xg_in, 16)
            clear_behind(sp, (2,), z_done)
            sp.wait_ge(xt_ps, 1)
            sp.dma_start(xg[:, :, :], parts(xs_d, TR, TR)).then_inc(xg_in, 16)
            clear_behind(sp, (4, 6), z_done)
            sp.wait_ge(tab_ok, 1)
            total = sp.value_load(tab[0:1, T_E + NX - 1:T_E + NX], min_val=2 * NX, max_val=NT)
            sp.wait_ge(z_done, 16 * (NX - 1))
            sp.wait_ge(ys_zero, NB * 16)

            def tile_row(u):
                return sp.value_load(tab[0:1, bass.ds(u, 1)], min_val=0, max_val=NX * REG - TR)

            def load_routed(u):
                r = tile_row(u)
                moved(sp, xt_ps, u)
                sp.dma_start(xg[:, :, :], parts(xs_d, r, TR)).then_inc(xg_in, 16)

            def load_shared(k):
                sp.wait_ge(xt_ps, total + k)
                sp.dma_start(xg[:, :, :], parts(xn2_d, k * TR, TR)).then_inc(xg_in, 16)

            def store_y(u):
                sp.wait_ge(y_ok, u + 2)
                sp.dma_start(parts(ys_d, u * TR, TR), y_s[:, :, :]).then_inc(y_st, 16)

            load_routed(2)
            with sp.Fori(3, total) as u:
                load_routed(u)
                store_y(u - 3)
            sp.wait_ge(xn2_st, (R + NB) * 16)
            sp.wait_ge(x2_st, NB * 16)
            last3 = sp.value_load(tab[0:1, T_L3:T_L3 + 1], min_val=2 * NX - 3, max_val=NT - 3)

            def load_x2(j):
                for p in range(TS):
                    moved(sp, mix_ok, TS * j + (p - 1))
                    sp.dma_start(x2g[p][:, :], x2_d[bass.ds(j * TR + p * P, P), :]).then_inc(mg_in[p], 16)

            def store_out(j):
                for p in range(TS):
                    sp.wait_ge(cmb_ok, TS * j + (p + 1))
                    sp.dma_start(out[bass.ds(j * TR + p * P, P), :], o_o[p][:, :]).then_inc(o_st[p], 16)

            for j in range(3):
                load_shared(j)
                store_y(last3 + j)
            load_x2(0)
            with sp.Fori(3, NS) as j:
                load_shared(j)
                load_x2(j - 2)
                store_out(j - 3)
            for j in range(NS, NS + 3):
                if j < NS + 2:
                    load_x2(j - 2)
                store_out(j - 3)
            sp.wait_ge(o_st[0], 16 * (NST // 2))
            sp.wait_ge(o_st[1], 16 * (NST // 2))

        @block.tensor
        def _(pe):
            def three(out, lhs, rhs, n, first=True, last=True):
                r = None
                for k in range(n):
                    (ah, al), (bh, bl) = lhs(k), rhs(k)
                    pe.matmul(out, ah, bh, start=first and k == 0, stop=False)
                    pe.matmul(out, al, bh, start=False, stop=False)
                    r = pe.matmul(out, ah, bl, start=False, stop=last and k == n - 1)
                return r

            pe.wait_ge(k_in, 16)
            pe.wait_ge(zero_ok, 1)

            def weights(batch, w):
                if among_first(batch, 1):
                    pe.wait_ge(wtl_ok, W_ORDER.index(w) + 1)

            def one(j, c):
                A, B, C, S, S2, S3 = (stage(j, c, k) for k in (2, 1, 0, -1, -2, -3))

                def scores(h):
                    V, hv = late_head(C, S, h)
                    if V:
                        if hv == 0:
                            pe.wait_ge(mrow, V.n(32, 32))
                        moved(pe, exp_ok, V.n(H, hv - 1))
                        for kc in range(TC):
                            r = pe.matmul(SS[hv % 2][:, kc * L:(kc + 1) * L],
                                          k4[V.slot][:, hv, kc * P:(kc + 1) * P], q4[V.slot][:, hv // 2, :],
                                          start=True, stop=True)
                        r.then_inc(ss_ps, 1)
                    if B:
                        if h == 0:
                            pe.wait_ge(stk[B.slot], B.turn * 192 + 192)
                        moved(pe, mx_ok, B.n(H, h - 1))
                        for qc in range(TC):
                            r = pe.matmul(SM[h % 2][:, qc * L:(qc + 1) * L],
                                          q4[B.slot][0:112, h // 2, qc * P:(qc + 1) * P], k4[B.slot][0:112, h, :],
                                          start=True, stop=True)
                        r.then_inc(sm_ps, 1)

                def values(V, g, kc):
                    if V:
                        if g == 0 and kc == 0:
                            if among_first(V, R):
                                pe.wait_ge(k_init, V.b + 1)
                            pe.wait_ge(v_ok, V.n(1, 1))
                        if kc == 0:
                            pe.wait_ge(exp_ok, V.n(H, 4 * g + 4))
                            moved(pe, ot_ok, V.n(4, g))
                        for i in range(4):
                            h = 4 * g + i
                            r = pe.matmul(OT[g % 2][PVW * i:PVW * (i + 1), :], v_s[V.slot][:, kc, h, :],
                                          pT[:, h % 8, kc * L:(kc + 1) * L], start=kc == 0, stop=kc == TC - 1)
                        if kc == TC - 1:
                            r.then_inc(pv_ps, 1)

                def transposes(bnk, src, done):
                    for ic in range(EC):
                        for t in range(TC):
                            r = pe.transpose(bnk[:, ic * L + t * P:ic * L + (t + 1) * P],
                                             src[:, t, ic * P:(ic + 1) * P], ident)
                    r.then_inc(done, 1)

                def attention_rows(qc):
                    for g in range(4):
                        r = pe.transpose((T0, T1)[qc][:, g * P:(g + 1) * P], oT_s[:, g, qc * P:(qc + 1) * P], ident)
                    r.then_inc(oq_ps, 1)

                def project(bnk, w, oc, src_h, src_l, done):
                    three(bnk[:, oc * L:(oc + 1) * L],
                          lambda k: (wt_h[:, w, k, oc * P:(oc + 1) * P], wt_l[:, w, k, oc * P:(oc + 1) * P]),
                          lambda k: (src_h[:, k, :], src_l[:, k, :]), EC).then_inc(done, 1)

                def project_rows(bnk, w, t, src_h, src_l, done):
                    three(bnk[:, t * E:(t + 1) * E],
                          lambda k: (src_h[:, k, t * P:(t + 1) * P], src_l[:, k, t * P:(t + 1) * P]),
                          lambda k: (wt_h[:, w, k, :], wt_l[:, w, k, :]), EC).then_inc(done, 1)

                for h in range(H):
                    scores(h)
                    if h == 0 and C:
                        pe.wait_ge(mx_ok, C.n(H, H))
                        if S:
                            pe.wait_ge(ot_ok, S.n(4, 2))
                        for qc in range(TC):
                            r = pe.transpose(mT_p[:, qc * P:(qc + 1) * P], mx[C.slot][:, qc, :], ident)
                        r.then_inc(mT_ps, 1)
                    if h == 0 and S3:
                        pe.wait_ge(oh_ok, S3.n(1, 1))
                        moved(pe, acc_ok, S3.n())
                        if S2:
                            pe.wait_ge(o_ok, S2.n(1, 1))
                        ones, up = K[:, C_ONE:C_ONE + P], K[:, C_UP:C_UP + P]
                        pe.matmul(rk_p, ones, acc[:, :, :].rearrange("p t e -> p (t e)"), start=True, stop=False)
                        r = pe.matmul(rk_p, up, msk[:, :, :].rearrange("p t e -> p (t e)"), start=False, stop=True)
                        r.then_inc(rk_ps, 1)
                    if h in (0, 1) and A:
                        if h == 0:
                            pe.wait_ge(cl_ok, A.n(1, 1))
                            moved(pe, qh_ok, A.n())
                            weights(A, 1)
                        project(T2, 1, h, c_h, c_l, k_ps)
                    if h in (2, 3):
                        if h == 2 and C:
                            pe.wait_ge(mT_ok, C.n(1, 1))
                        values(S, 2, h - 2)
                    if h in (2, 3) and S2:
                        if h == 2:
                            weights(S2, 3)
                            pe.wait_ge(oTl_ok, S2.n(1, 1))
                            if S3:
                                pe.wait_ge(pos_ok, S3.n(1, 1))
                        project_rows(T1, 3, h - 2, oT_h, oT_l, op_ps)
                    if h == 2 and A:
                        pe.wait_ge(xn_ok, A.n(1, 1))
                        if S2:
                            pe.wait_ge(oTl_ok, S2.n(1, 1))
                        else:
                            moved(pe, vr_ok, A.n())
                        transposes(T0, xn_s, xnT_ps)
                    if h in (5, 6):
                        values(S, 3, h - 5)
                    if h in (5, 6) and A:
                        if h == 5:
                            pe.wait_ge(xnTl_ok, A.n(1, 1))
                            pe.wait_ge(kh_ok, A.n(1, 1))
                            weights(A, 0)
                        project(T2, 0, h - 5, xnT_h, xnT_l, q_ps)
                    if h in (7, 8) and A:
                        if h == 7:
                            weights(A, 2)
                        project_rows(T0, 2, h - 7, c_h, c_l, v_ps)
                    if h == 9 and S2:
                        pe.wait_ge(xn2_ok, S2.n(1, 1))
                        pe.wait_ge(x2_ok, S2.n(1, 1))
                        transposes(T1, xn2_s[S2.slot], xn2T_ps)
                    if h in (9, 10):
                        values(C, 0, h - 9)
                    if h == 10 and S:
                        pe.wait_ge(ot_ok, S.n(4, 4))
                        if A:
                            pe.wait_ge(vr_ok, A.n(1, 1))
                        elif S2:
                            pe.wait_ge(oTl_ok, S2.n(1, 1))
                        attention_rows(0)
                    if h == 11 and S2:
                        if among_first(S2, 1):
                            pe.wait_ge(few_in, 80)
                        pe.wait_ge(xn2T_ok, S2.n(1, 1))
                        for t in range(TC):
                            for k in range(EC):
                                r = pe.matmul(lg_p[:, t * NX:(t + 1) * NX], xn2T[:, k, t * P:(t + 1) * P],
                                              wr_s[:, k, :], start=k == 0, stop=k == EC - 1)
                        r.then_inc(lg_ps, 1)
                    if h == 13 and S:
                        if S2:
                            pe.wait_ge(lgc_ok, S2.n(1, 1))
                        attention_rows(1)
                    if h in (13, 14):
                        values(C, 1, h - 13)
                    if h == 15 and S:
                        pe.wait_ge(o_ok, S.n(1, 1))
                        transposes(T0, o_s, oT_ps)

            iterations(pe, one)

            pe.wait_ge(acc_ok, NB)
            pe.matmul(T0[:, 0:NX], K[:, C_ONE:C_ONE + P], acc[:, 0, :], start=True, stop=True).then_inc(cnt_ps, 1)

            def transpose_x(u):
                pe.wait_ge(xg_in, u * 16 + 16)
                moved(pe, xl_ok, u)
                for t in range(TS):
                    for k in range(EC):
                        r = pe.transpose(psX[:, k * TR + t * P:k * TR + (t + 1) * P], xg[:, t, k * P:(k + 1) * P], ident)
                r.then_inc(xt_ps, 1)

            def up(u, p, after):
                pe.wait_ge(xl_ok, u + 1)
                moved(pe, sg_ok, u)
                for ps, off, done in ((psH1, 0, h1_ps), (psH3, W3O, h3_ps)):
                    for f in range(FC):
                        def weights(k):
                            at = slice(off + k * HID + f * P, off + k * HID + (f + 1) * P)
                            return w_h[p][:, at], w_l[p][:, at]
                        r = three(ps[f // 2][:, f % 2 * TR:(f % 2 + 1) * TR], weights,
                                  lambda k: (xg_h[:, k, :], xg_l[:, k, :]), EC)
                    r.then_inc(done, 1)
                    if done is h1_ps:
                        if after:
                            transpose_x(u + 1)
                        moved(pe, g_ok, u)

            def down(done, p):
                pe.wait_ge(gl_ok, done)
                pe.wait_ge(y_ok, done)
                for t in range(TS):
                    r = three(psY[:, t * E:(t + 1) * E], lambda k: (gT_h[:, k, t * P:(t + 1) * P], gT_l[:, k, t * P:(t + 1) * P]),
                              lambda k: (w_h[p][:, W2O + k * E:W2O + (k + 1) * E],
                                         w_l[p][:, W2O + k * E:W2O + (k + 1) * E]), FC)
                r.then_inc(w2_ps, 1)

            def tile(u, p, before, after=True):
                up(u, p, after)
                if before is not None:
                    down(u, before)

            def value(column, k, least, most):
                return pe.value_load(tab[0:1, bass.ds(k + column, 1)], min_val=least, max_val=most)

            def expert(k, p, before, tb, ends):
                pe.wait_ge(w_ok, k * WP + WP)
                tile(tb, p, before)
                te = ends if isinstance(ends, list) else [value(T_E, k + i, 2, NT) for i in range(ends)]
                with pe.Fori(tb + 1, te[0]) as u:
                    tile(u, p, p)
                return te

            transpose_x(0)
            pe.wait_ge(tab_ok, 1)
            expert(0, 0, None, 0, 1)
            with pe.Fori(0, (NX - 2) // 2) as kk:
                k = 2 * kk + 1
                ends = expert(k, 1, 0, value(T_B, k, 2, NT - 2), 2)
                expert(k + 1, 0, 1, ends[0], ends[1:])
            total, = expert(NX - 1, 1, 0, value(T_B, NX - 1, 2, NT - 2), 1)
            pe.wait_ge(w_ok, (NX + 1) * WP)
            tile(total, 0, 1)
            with pe.Fori(1, NS - 1) as k:
                tile(total + k, 0, 0)
            tile(total + (NS - 1), 0, 0, after=False)
            down(total + NS, 0)

        @block.scalar
        def _(act):
            act.sem_inc(y_ok, 1)

            def clear_q(i):
                act.activation(q4[i][:, :, :], zero[:, :].unsqueeze(1).to_broadcast([P, H // 2, L]), ACT.Copy).then_inc(q_zero, 1)

            act.wait_ge(zero_ok, 1)
            clear_q(0)
            for w in W_ORDER:
                act.wait_ge(wt_in[w], 16)
                act.activation(wt_h[:, w, :, :], wt_raw[:, w, :].rearrange("p (c n) -> p c n", c=EC), ACT.Copy).then_inc(wth_ok, 1)
            act.wait_ge(few_in, 80)
            act.activation(gate[:, :], gt[:, :], ACT.Tanh).then_inc(gate_ok, 1)

            def one(j, c):
                Eb, A, C, S, S2 = (stage(j, c, k) for k in (3, 2, 0, -1, -2))

                def probs(h):
                    V, hv = late_head(C, S, h)
                    if V:
                        if hv == 0 and among_first(V, 1):
                            act.wait_ge(wtl_ok, 4)
                        act.wait_ge(ss_ps, V.n(H, hv + 1))
                        moved(act, pv_ps, V.n(4, hv // 4 - 1))
                        act.activation(pT[:, hv % 8, :], SS[hv % 2][:, :], ACT.Exp, scale=D ** -0.5).then_inc(exp_ok, 1)

                def head_out(V, g):
                    if V:
                        act.wait_ge(pv_ps, V.n(4, g + 1))
                        moved(act, oq_ps, V.n(2))
                        act.activation(oT_s[:, g, :], OT[g % 2], ACT.Copy).then_inc(ot_ok, 1)

                def from_bank(dst, bnk, ps, b, used, count, done):
                    act.wait_ge(ps, b.n(1, 1))
                    moved(act, used, count)
                    act.activation(dst[:, :, :], bnk[:, :].rearrange("p (c t) -> p c t", c=EC), ACT.Copy).then_inc(done, 1)

                def q_or_k(side, bnk, ps, done):
                    act.wait_ge(ps, A.n(2, 2))
                    moved(act, qk_st, A.n(32, -16 * side))
                    for oc in range(EC):
                        for half in range(2):
                            dst = qk_s[:, 4 * side + 2 * half + oc, :]
                            r = act.activation(dst.bitcast(F32) if half else dst, bnk[:, oc * L:(oc + 1) * L], ACT.Identity,
                                               bias=bqk_s[:, 2 * side + oc:2 * side + oc + 1])
                    r.then_inc(done, 1)

                for h in range(H):
                    probs(h)
                    if h == 0 and S2:
                        from_bank(oT_h, T0, oT_ps, S2, op_ps, S2.n(2), oTh_ok)
                    if h == 0 and C:
                        act.wait_ge(mT_ps, C.n(1, 1))
                        moved(act, mrow, C.n(32))
                        act.activation(mT[:, :], mT_p, ACT.Copy, scale=-1.0).then_inc(mT_ok, 1)
                    if h == 2 and A:
                        q_or_k(1, T2, k_ps, kh_ok)
                    if h == 3 and A:
                        from_bank(xnT_h, T0, xnT_ps, A, q_ps, A.n(2), xnTh_ok)
                    if h == 4:
                        head_out(S, 2)
                    if h == 7:
                        head_out(S, 3)
                    if h == 7 and A:
                        q_or_k(0, T2, q_ps, qh_ok)
                    if h == 9 and A:
                        act.wait_ge(v_ps, A.n(2, 2))
                        moved(act, pv_ps, A.n(4, -4 * (R - 1)))
                        act.activation(v_s[A.slot][:, :, :, 0:D], T0[:, :].rearrange("p (t h d) -> p t h d", t=TC, h=H),
                                       ACT.Copy).then_inc(vr_ok, 1)
                    if h == 10 and Eb:
                        act.wait_ge(c_in, Eb.n(16, 16))
                        moved(act, v_ps, Eb.n(2))
                        act.activation(c_h[:, :, :], c_s[:, :, :], ACT.Copy).then_inc(ch_ok, 1)
                    if h == 10 and S2:
                        from_bank(xn2T, T1, xn2T_ps, S2, lg_ps, S2.n(), xn2T_ok)
                    if h == 11:
                        head_out(C, 0)
                    if h == 13 and S2:
                        act.wait_ge(lgd_ok, S2.n(1, 1))
                        act.activation(ex[:, :, :], lgd[:, :, :], ACT.Exp).then_inc(ex_ok, 1)
                    if h == 15:
                        head_out(C, 1)
                if Eb and among_first(Eb, R - 1):
                    clear_q(Eb.b + 1)
                if S and among_first(S, NB) and S.b == NB - 2:
                    for i in range(WP):
                        act.wait_ge(w_in[i], 16)
                        act.activation(w_h0[:, part(i)], wraw[:, part(i)], ACT.Copy).then_inc(w_used, 1)

            iterations(act, one)

            act.wait_ge(ends_ok, 1)
            act.wait_ge(sc_done, NB * 64)
            clear_behind(act, (1, 3), z_done)

            def x_high(u):
                act.wait_ge(xt_ps, u + 1)
                moved(act, h3_ps, u)
                act.activation(xg_h[:, :, :], psX[:, :].rearrange("p (c t) -> p c t", c=EC), ACT.Copy).then_inc(xh_ok, 1)

            def silu(u):
                act.wait_ge(h1_ps, u + 1)
                moved(act, g_ok, u)
                for i in range(2):
                    r = act.activation(sg[:, 2 * i:2 * i + 2, :].rearrange("p f t -> p (f t)"), psH1[i][:, :], ACT.Silu)
                r.then_inc(sg_ok, 1)

            def g_high(u):
                act.wait_ge(g_ok, u + 1)
                moved(act, w2_ps, u)
                act.activation(gT_h[:, :, :], gg[:, :, :], ACT.Copy).then_inc(gh_ok, 1)

            def y_routed(u):
                act.wait_ge(w2_ps, u + 1)
                moved(act, y_st, u * 16)
                act.activation(y_s[:, :, :].rearrange("p t d -> p (t d)"), psY[:, :], ACT.Copy).then_inc(y_ok, 1)

            def y_shared(j):
                act.wait_ge(w2_ps, total + j + 1)
                moved(act, cmb_ok, TS * j)
                act.activation(ysh[:, :, :].rearrange("p t d -> p (t d)"), psY[:, :], ACT.Copy).then_inc(y_ok, 1)

            x_high(0)
            act.wait_ge(tab_ok, 1)
            total = act.value_load(tab[0:1, T_E + NX - 1:T_E + NX], min_val=2 * NX, max_val=NT)
            clear_behind(act, (5, 7), z_done)
            silu(0)
            x_high(1)
            g_high(0)

            def routed(u):
                silu(u)
                x_high(u + 1)
                y_routed(u - 1)
                g_high(u)

            routed(1)
            with act.Fori(2, total) as u:
                routed(u)
            silu(total)
            x_high(total + 1)
            y_routed(act.value_load(tab[0:1, T_L1:T_L1 + 1], min_val=2 * NX - 1, max_val=NT - 1))
            g_high(total)

            def shared(j, after=True):
                u = total + j
                silu(u)
                if after:
                    x_high(u + 1)
                y_shared(j - 1)
                g_high(u)

            shared(1)
            with act.Fori(2, NS - 1) as j:
                shared(j)
            shared(NS - 1, after=False)
            y_shared(NS - 1)

        @block.vector
        def _(v):
            seen = {"base": 0, "k": 0, "j": None, "per": 0}

            def mark(ins):
                seen["k"] += 1
                ins.then_inc(chain, 1)

            def settle(apart=False):
                at = seen["base"] + seen["k"]
                v.wait_ge(chain, at if seen["j"] is None else seen["j"] * seen["per"] + at)
                if apart:
                    v.memset(spare_v[:, :], 0.0)

            def link(ins):
                mark(ins)
                settle()

            v.memset(zero[:, :], 0.0)
            link(v.memset(acc[:, :, :], 0.0))
            v.tensor_copy(spare_v[:, :], acc[:, 0, 0:1]).then_inc(zero_ok, 1)
            v.wait_ge(k_in, 16)

            def clear_k(i):
                link(v.memset(k4[i][:, :, :].bitcast(U32), 0))
                v.memset(v_s[i][:, :, :, D:D + 1], 1.0)
                v.memset(v_s[i][:, :, :, D + 1:PVW], 0.0)
                v.tensor_copy(k4[i][96:128, :, :], K[96:128, C_MROW:C_MROW + H].unsqueeze(2).to_broadcast([32, H, L])).then_inc(k_init, 1)

            def weights_low():
                for n, w in enumerate(W_ORDER):
                    v.wait_ge(wth_ok, n + 1)
                    v.tensor_tensor(wt_l[:, w, :, :], wt_raw[:, w, :].rearrange("p (c n) -> p c n", c=EC),
                                    wt_h[:, w, :, :].bitcast(F32), ALU.subtract).then_inc(wtl_ok, 1)

            def scale_gates():
                v.wait_ge(gate_ok, 1)
                link(v.tensor_scalar(gsc[:, 0:1], gate[:, 1:2], 1.0 / 3.0, None, ALU.mult))
                link(v.tensor_scalar(gsc[:, 1:2], gate[:, 1:2], 2.0 / 3.0, None, ALU.mult))
                v.tensor_scalar(gbo[:, :], gbo[:, :], gate[:, 0:1], None, ALU.mult).then_inc(gbo_ok, 1)

            def bank_chunks(bnk):
                return bnk[:, :].rearrange("p (c t) -> p c t", c=EC)

            def low(dst, ps, high):
                return v.tensor_tensor(dst, ps, high.bitcast(F32), ALU.subtract)

            def stats(src, st):
                for t in range(TC):
                    r = v.bn_stats(st[:, t, :], src[:, t, :])
                mark(r)

            def mean_and_variance(st, mv):
                settle(apart=True)
                for t in range(TC):
                    r = v.bn_aggr(mv[:, t, :], st[:, t, :])
                mark(r)

            def add_eps(mv, done):
                settle()
                v.tensor_scalar(mv[:, :, 1], mv[:, :, 1], 1e-5, None, ALU.add).then_inc(done, 1)

            def one(j, c):
                Eb, A, B, S, S2, S3 = (stage(j, c, k) for k in (3, 2, 1, -1, -2, -3))
                spread = [P, TC, NX]

                def early(h):
                    if h == 0 and S3:
                        settle()
                        v.reciprocal(rec[:, :], ssum[:, :])
                        mark(v.tensor_reduce(s2[:, :], ex2[:, :, :], AX, ALU.add))
                    if h == 1 and S3:
                        v.wait_ge(pos_ok, S3.n(1, 1))
                        mark(v.tensor_tensor(pr[:, :], oh[:, :], pos[:, :, :].unsqueeze(1).to_broadcast([P, 2, TC, NX]), ALU.mult))
                    if h == 1 and S2:
                        v.wait_ge(oTh_ok, S2.n(1, 1))
                        low(oT_l[:, :, :], bank_chunks(T0), oT_h[:, :, :]).then_inc(oTl_ok, 1)
                    if h == 2 and S3:
                        settle()
                        moved(v, sc_done, S3.n(64))
                        by_tile = slot[:, :, :].rearrange("p k t -> p t k")
                        v.tensor_copy(slots[:, bass.ds(S3.n(TC), TC), :], by_tile)
                        v.tensor_copy(slot_i[:, :, :], by_tile).then_inc(slot_ok, 1)
                        v.tensor_scalar(wts[:, bass.ds(S3.n(TC), TC), 0], rec[:, :], gsc[:, 1:2], None, ALU.mult)
                        v.tensor_scalar(wts[:, bass.ds(S3.n(TC), TC), 1], s2[:, :], gsc[:, 1:2], None, ALU.mult)
                        v.tensor_tensor(acc[:, 0, :], acc[:, 1, :], msk[:, 1, :], ALU.add).then_inc(acc_ok, 1)
                    if h == 4 and A:
                        v.wait_ge(xnTh_ok, A.n(1, 1))
                        low(xnT_l[:, :, :], bank_chunks(T0), xnT_h[:, :, :]).then_inc(xnTl_ok, 1)
                    if h == 5 and S2:
                        mean_and_variance(bst2, bmv2)
                    if h == 7 and S2:
                        v.wait_ge(rstd2_ok, S2.n(1, 1))
                        if not among_first(S2, 1):
                            v.wait_ge(xn2_st, S2.n(16, 16))
                        for t in range(TC):
                            r = v.tensor_scalar(xn2_s[S2.slot][:, t, :], x2_s[:, t, :], bmv2[:, t, 0:1], rstd2[:, t:t + 1], ALU.subtract, ALU.mult)
                        r.then_inc(xn2_ok, 1)
                    if h == 9 and Eb:
                        moved(v, xn_ok, Eb.n())
                        mean_and_variance(bst, bmv)
                    if h == 12 and S2:
                        v.wait_ge(lgc_ok, S2.n(1, 1))
                        mark(v.tensor_reduce(lmx[:, :], lg[:, :, :], AX, ALU.max))
                    if h == 13 and S2:
                        settle()
                        tri = K[:, C_TRI:C_TRI + NX * NX].rearrange("p (e j) -> p e j", e=NX)
                        mark(v.tensor_tensor(eqm[:, :], eqm[:, :], tri.unsqueeze(1).to_broadcast([P, TC, NX, NX]), ALU.mult))
                    if h == 14 and (S or S2):
                        settle()
                    if h == 14 and S2:
                        mark(v.tensor_reduce(rk[:, :, :], gtm[:, :], AX, ALU.add))
                    if h == 14 and S:
                        for qc, bnk in enumerate((T0, T1)):
                            r = v.tensor_tensor(o_s[:, qc, :].rearrange("p (h d) -> p h d", d=D),
                                                bnk[:, :].rearrange("p (h w) -> p h w", w=PVW)[:, :, 0:D],
                                                rsum[:, qc, :].unsqueeze(2).to_broadcast([P, H, D]), ALU.mult)
                        r.then_inc(o_ok, 1)
                    if h == 15 and S2:
                        settle()
                        link(v.tensor_tensor(msk[:, :, :], oh[:, 0], oh[:, 1], ALU.add))
                        v.tensor_tensor(acc[:, 1, :], acc[:, 0, :], msk[:, 0, :], ALU.add).then_inc(oh_ok, 1)

                def late(h):
                    if h == 0 and S3:
                        settle()
                        mark(v.tensor_tensor(s2[:, :], s2[:, :], rec[:, :], ALU.mult))
                        v.wait_ge(rk_ps, S3.n(1, 1))
                        v.tensor_tensor(pos[:, :, :], rk_p.rearrange("p (t e) -> p t e", t=TC),
                                        K[:, C_EB:C_EB + NX].unsqueeze(1).to_broadcast(spread), ALU.add).then_inc(pos_ok, 1)
                    if h == 1 and S3:
                        settle()
                        mark(v.tensor_reduce(slot[:, :, :], pr[:, :], AX, ALU.add))
                    if h == 3 and S2:
                        v.wait_ge(op_ps, S2.n(2, 2))
                        v.wait_ge(xb_ok, S2.n(1, 1))
                        moved(v, x2_st, S2.n(16))
                        v.scalar_tensor_tensor(x2_s[:, :, :], T1[:, :].rearrange("p (t d) -> p t d", t=TC), gate[:, 0:1],
                                               xr_s[:, :, :], ALU.mult, ALU.add).then_inc(x2_ok, 1)
                    if h == 4 and S2:
                        v.wait_ge(x2_ok, S2.n(1, 1))
                        stats(x2_s, bst2)
                    if h == 5 and S2:
                        add_eps(bmv2, var2_ok)
                    if h == 8 and Eb:
                        v.wait_ge(x_in, Eb.n(16, 16))
                        stats(x_s, bst)
                    if h == 9 and Eb:
                        add_eps(bmv, var1_ok)
                    if h == 11 and S2:
                        v.wait_ge(lg_ps, S2.n(1, 1))
                        v.tensor_copy(lg[:, :, :], lg_p.rearrange("p (t e) -> p t e", t=TC)).then_inc(lgc_ok, 1)
                    if h == 12 and S2:
                        settle()
                        v.tensor_tensor(lgd[:, :, :], lg[:, :, :], lmx[:, :].unsqueeze(2).to_broadcast(spread), ALU.subtract).then_inc(lgd_ok, 1)
                        for t in range(TC):
                            other = lg[:, t, :].unsqueeze(1).to_broadcast([P, NX, NX])
                            own = lg[:, t, :].unsqueeze(2).to_broadcast([P, NX, NX])
                            v.tensor_tensor(gtm[:, t], other, own, ALU.is_gt)
                            r = v.tensor_tensor(eqm[:, t], other, own, ALU.is_equal)
                        mark(r)
                    if h == 13 and S2:
                        settle()
                        mark(v.tensor_tensor(gtm[:, :], gtm[:, :], eqm[:, :], ALU.add))
                    if h == 13 and S:
                        v.wait_ge(oq_ps, S.n(2, 2))
                        moved(v, oT_ps, S.n())
                        for qc, bnk in enumerate((T0, T1)):
                            r = v.reciprocal(rsum[:, qc, :], bnk[:, :].rearrange("p (h w) -> p h w", w=PVW)[:, :, D])
                        mark(r)
                    if h == 14 and S2:
                        settle()
                        v.tensor_scalar(oh[:, 0], rk[:, :, :], 0.0, None, ALU.is_equal)
                        mark(v.tensor_scalar(oh[:, 1], rk[:, :, :], 1.0, None, ALU.is_equal))
                    if h == 15 and S2:
                        v.wait_ge(ex_ok, S2.n(1, 1))
                        v.tensor_reduce(ssum[:, :], ex[:, :, :], AX, ALU.add)
                        mark(v.tensor_tensor(ex2[:, :, :], ex[:, :, :], oh[:, 1], ALU.mult))

                for h in range(H):
                    early(h)
                    if B:
                        v.wait_ge(sm_ps, B.n(H, h + 1))
                        if h == 0:
                            moved(v, mT_ps, B.n(1, 1 - R))
                        v.tensor_reduce(mx[B.slot][:, :, 8 * (h % 2) + h // 2], SM[h % 2][:, :].rearrange("p (t k) -> p t k", t=TC),
                                        AX, ALU.max).then_inc(mx_ok, 1)
                    late(h)
                if S and among_first(S, NB) and S.b == NB - 2:
                    for i in range(WP):
                        v.wait_ge(w_used, i + 1)
                        v.tensor_tensor(w_l0[:, part(i)], wraw[:, part(i)], w_h0[:, part(i)].bitcast(F32), ALU.subtract).then_inc(w_ok, 1)
                if Eb and among_first(Eb, R):
                    if Eb.b == 0:
                        weights_low()
                    clear_k(Eb.b)
                    if Eb.b == 0:
                        scale_gates()

            for i in range(-R, LOOP0):
                one(0, i)
            seen.update(base=seen["base"] + seen["k"], k=0, per=LINKS_PER_LOOP)
            with v.Fori(0, TRIPS) as j:
                seen["j"] = j
                for c in range(LOOP0, LOOP0 + R):
                    one(j, c)
            assert seen["k"] == LINKS_PER_LOOP, seen["k"]
            seen.update(base=seen["base"] + TRIPS * LINKS_PER_LOOP, k=0, j=None)
            for i in range(LOOP0 + R * TRIPS, NB + 3):
                one(0, i)

            v.wait_ge(cnt_ps, 1)
            link(v.tensor_copy(cnt[:, :], T0[:, 0:NX]))
            link(v.tensor_tensor(tabf[:, T_Z:T_Z + NX], cnt[:, :], K[:, C_EB:C_EB + NX], ALU.add))
            v.tensor_copy(tab[0:1, T_Z:T_Z + NX], tabf[0:1, T_Z:T_Z + NX]).then_inc(ends_ok, 1)
            link(v.tensor_tensor(tge[:, :, :], cnt[:, :].unsqueeze(2).to_broadcast([P, NX, NTHR]),
                                 K[:, C_THR:C_THR + NTHR].unsqueeze(1).to_broadcast([P, NX, NTHR]), ALU.is_gt))
            link(v.tensor_reduce(ntl[:, :], tge[:, :, :], AX, ALU.add))
            link(v.tensor_scalar(ntl[:, :], ntl[:, :], 2.0, None, ALU.max))
            before = K[:, C_TRI:C_TRI + NX * NX].rearrange("p (e j) -> p e j", e=NX)
            link(v.tensor_tensor(tpe[:, :, :], before, ntl[:, :].unsqueeze(1).to_broadcast([P, NX, NX]), ALU.mult))
            link(v.tensor_reduce(tend[:, :], tpe[:, :, :], AX, ALU.add))
            link(v.tensor_tensor(tend[:, :], tend[:, :], ntl[:, :], ALU.add))
            v.tensor_copy(tabf[:, T_E:T_E + NX], tend[:, :])
            v.tensor_tensor(tabf[:, T_B:T_B + NX], tend[:, :], ntl[:, :], ALU.subtract)
            link(v.tensor_tensor(tgt[:, :, :], tend[:, :].unsqueeze(1).to_broadcast([P, NT, NX]),
                                 K[:, C_TI:C_TI + NT].unsqueeze(2).to_broadcast([P, NT, NX]), ALU.is_le))
            v.tensor_reduce(te_n[:, :], tgt[:, :, :], AX, ALU.add)
            link(v.tensor_tensor(tpr[:, :, :], tgt[:, :, :], ntl[:, :].unsqueeze(1).to_broadcast([P, NT, NX]), ALU.mult))
            link(v.tensor_reduce(tb_n[:, :], tpr[:, :, :], AX, ALU.add))
            link(v.tensor_scalar(te_n[:, :], te_n[:, :], float(NX - 1), float(REG), ALU.min, ALU.mult))
            link(v.tensor_tensor(tb_n[:, :], K[:, C_TI:C_TI + NT], tb_n[:, :], ALU.subtract))
            link(v.scalar_tensor_tensor(tabf[:, T_ROW:T_ROW + NT], tb_n[:, :], float(TR), te_n[:, :], ALU.mult, ALU.add))
            v.tensor_scalar(tabf[:, T_L3:T_L3 + 1], tend[:, NX - 1:NX], -3.0, None, ALU.add)
            link(v.tensor_scalar(tabf[:, T_L1:T_L1 + 1], tend[:, NX - 1:NX], -1.0, None, ALU.add))
            v.tensor_copy(tab[0:1, 0:T_Z], tabf[0:1, 0:T_Z])
            v.tensor_copy(tab[0:1, T_L3:TW], tabf[0:1, T_L3:TW]).then_inc(tab_ok, 1)
            v.wait_ge(tab_ok, 1)
            total = v.value_load(tab[0:1, T_E + NX - 1:T_E + NX], min_val=2 * NX, max_val=NT)

            def x_low(u):
                v.wait_ge(xh_ok, u + 1)
                low(xg_l[:, :, :], psX[:, :].rearrange("p (c t) -> p c t", c=EC), xg_h[:, :, :]).then_inc(xl_ok, 1)

            def gated(u):
                v.wait_ge(sg_ok, u + 1)
                v.wait_ge(h3_ps, u + 1)
                moved(v, gl_ok, u)
                for i in range(2):
                    r = v.tensor_tensor(gg[:, 2 * i:2 * i + 2, :].rearrange("p f t -> p (f t)"),
                                        sg[:, 2 * i:2 * i + 2, :].rearrange("p f t -> p (f t)"), psH3[i][:, :], ALU.mult)
                r.then_inc(g_ok, 1)

            def g_low(u):
                v.wait_ge(gh_ok, u + 1)
                low(gT_l[:, :, :], gg[:, :, :], gT_h[:, :, :]).then_inc(gl_ok, 1)

            x_low(0)
            link(v.scalar_tensor_tensor(dlt[:, :], tabf[:, T_B:T_B + NX], float(TR), K[:, C_EB:C_EB + NX], ALU.mult, ALU.subtract))
            link(v.tensor_copy(cnt[:, :], dlt[:, :]))
            link(v.tensor_tensor(dlt[:, 1:NX], cnt[:, 1:NX], cnt[:, 0:NX - 1], ALU.subtract))
            flat = slots[:, :, :].rearrange("p t k -> p (t k)")
            link(v.tensor_tensor(gge[:, :, :], flat.unsqueeze(2).to_broadcast([P, NST * 2, NX]),
                                 K[:, C_EB:C_EB + NX].unsqueeze(1).to_broadcast([P, NST * 2, NX]), ALU.is_ge))
            link(v.tensor_tensor(gge[:, :, :], gge[:, :, :], dlt[:, :].unsqueeze(1).to_broadcast([P, NST * 2, NX]), ALU.mult))
            link(v.tensor_reduce(gf[:, :], gge[:, :, :], AX, ALU.add))
            v.tensor_tensor(gidx[:, :, :].rearrange("p t k -> p (t k)"), gf[:, :], flat, ALU.add).then_inc(idx_ok, 1)
            base = seen["base"] + seen["k"]

            def mix(k, p, turn):
                v.wait_ge(mg_in[p], turn * 16 + 16)
                v.wait_ge(ig_ok, k + 1)
                v.wait_ge(yg_in[p], turn * 32 + 32)
                moved(v, cmb_ok, k - 1)
                v.scalar_tensor_tensor(yga[p][:, :], yga[p][:, :], wg[p][:, 0:1], x2g[p][:, :], ALU.mult, ALU.add).then_inc(chain, 1)
                v.wait_ge(chain, base + k + 1)
                v.scalar_tensor_tensor(mixed[p][:, :], ygb[p][:, :], wg[p][:, 1:2], yga[p][:, :], ALU.mult, ALU.add).then_inc(mix_ok, 1)

            def combine(k, p, turn):
                v.wait_ge(mix_ok, k + 1)
                v.wait_ge(y_ok, total + turn + 2)
                moved(v, o_st[p], turn * 16)
                v.scalar_tensor_tensor(o_o[p][:, :], ysh[:, p, :], gsc[:, 0:1], mixed[p][:, :], ALU.mult, ALU.add).then_inc(cmb_ok, 1)

            def take(k, p):
                moved(v, mix_ok, k - 1)
                v.tensor_copy(wg[p][:, :], wts[:, bass.ds(k, 1), :].rearrange("p t k -> p (t k)"))
                v.tensor_copy(ig[p][:, :], gidx[:, bass.ds(k, 1), :].rearrange("p t k -> p (t k)")).then_inc(ig_ok, 1)

            v.wait_ge(idx_ok, 1)
            take(0, 0)
            take(1, 1)
            x_low(1)
            gated(0)
            g_low(0)
            with v.Fori(1, total + 1) as u:
                x_low(u + 1)
                gated(u)
                g_low(u)

            def each(step, j):
                for p in range(TS):
                    step(TS * j + p, p, j)

            def take_tile(j):
                for p in range(TS):
                    take(TS * j + p, p)

            def shared(j):
                x_low(total + j + 1)
                gated(total + j)
                g_low(total + j)
                each(mix, j - 1)
                take_tile(j)
                each(combine, j - 1)

            shared(1)
            with v.Fori(2, NS - 1) as j:
                shared(j)
            gated(total + (NS - 1))
            g_low(total + (NS - 1))
            each(mix, NS - 2)
            take_tile(NS - 1)
            each(combine, NS - 2)
            each(mix, NS - 1)
            each(combine, NS - 1)

        @block.gpsimd
        def _(po):
            def load_w(k, i):
                moved(po, w_ok, (k - 1) * WP + i + 1)
                po.dma_start(wraw[:, part(i)], wall[k][:, part(i)]).then_inc(w_in[i], 16)

            def cut(k, p, tiles=None):
                for i in range(WP):
                    po.wait_ge(w_in[i], 16 * (k + 1))
                    if tiles is not None and i == 0:
                        po.wait_ge(w2_ps, tiles)
                    po.tensor_copy(w_h[p][:, part(i)], wraw[:, part(i)]).then_inc(w_used, 1)
                    po.wait_ge(w_used, k * WP + i + 1)
                    po.tensor_tensor(w_l[p][:, part(i)], wraw[:, part(i)], w_h[p][:, part(i)].bitcast(F32), ALU.subtract).then_inc(w_ok, 1)
                    if k < NX:
                        load_w(k + 1, i)

            def carry(n):
                po.wait_ge(spare_ok, n + 1)
                po.tensor_tensor(spare_p[:, 1:2], spare_p[:, 0:1], spare_p[:, 0:1], ALU.add).then_inc(spare_ok, 1)

            po.memset(spare_p[:, :], 0.0).then_inc(spare_ok, 1)
            po.wait_ge(spare_ok, 1)
            po.wait_ge(k_in, 16)

            def one(j, c):
                Eb, A, S, S2, S3 = (stage(j, c, k) for k in (3, 2, -1, -2, -3))

                def root(mv, rs, asked, b, done):
                    po.wait_ge(asked, b.n(1, 1))
                    po.tensor_tensor(rs[:, :], mv[:, :, 1], K[:, C_MH:C_MH + 1].to_broadcast([P, TC]), ALU.pow).then_inc(done, 1)

                def leave_low(side, high_ok, done):
                    po.wait_ge(high_ok, A.n(1, 1))
                    high, rest = (qk_s[:, 4 * side + 2 * half:4 * side + 2 * half + 2, :] for half in range(2))
                    po.tensor_tensor(rest, rest.bitcast(F32), high.bitcast(F32), ALU.subtract).then_inc(done, 1)

                if A:
                    leave_low(1, kh_ok, kl_ok)
                if S3:
                    po.wait_ge(slot_ok, S3.n(1, 1))
                    carry(S3.b)
                    for t in range(TC):
                        for k in range(2):
                            po.indirect_dma_start(
                                out=xs_d, out_offset=bass.IndirectOffsetOnAxis(ap=slot_i[:, t, k:k + 1].bitcast(U32), axis=0),
                                in_=xn2_s[S3.slot][:, t, :], in_offset=None).then_inc(sc_done, 16)
                if S2:
                    root(bmv2, rstd2, var2_ok, S2, rstd2_ok)
                if A:
                    leave_low(0, qh_ok, ql_ok)
                if Eb:
                    root(bmv, rstd, var1_ok, Eb, rstd1_ok)
                    moved(po, xnT_ps, Eb.n())
                    po.tensor_tensor(xn_s[:, :, :], x_s[:, :, :], bmv[:, :, 0:1].to_broadcast([P, TC, E]), ALU.subtract).then_inc(xc_ok, 1)
                    po.wait_ge(rstd1_ok, Eb.n(1, 1))
                    po.wait_ge(xc_ok, Eb.n(1, 1))
                    po.tensor_tensor(xn_s[:, :, :], xn_s[:, :, :], rstd[:, :].unsqueeze(2).to_broadcast([P, TC, E]), ALU.mult).then_inc(xn_ok, 1)
                if S:
                    if among_first(S, 1):
                        po.wait_ge(gbo_ok, 1)
                    po.wait_ge(xr_in, S.n(16, 16))
                    po.tensor_tensor(xr_s[:, :, :], xr_s[:, :, :], gbo[:, :].unsqueeze(1).to_broadcast([P, TC, E]), ALU.add).then_inc(xb_ok, 1)
                if Eb:
                    po.wait_ge(ch_ok, Eb.n(1, 1))
                    moved(po, v_ps, Eb.n(2))
                    po.tensor_tensor(c_l[:, :, :], c_s[:, :, :], c_h[:, :, :].bitcast(F32), ALU.subtract).then_inc(cl_ok, 1)
                if A:
                    if among_first(A, 1):
                        po.wait_ge(few_in, 80)
                    po.wait_ge(vr_ok, A.n(1, 1))
                    ring = v_s[A.slot][:, :, :, 0:D]
                    po.tensor_tensor(ring, ring, bv_s[:, :].rearrange("p (h d) -> p h d", h=H).unsqueeze(1).to_broadcast([P, TC, H, D]),
                                     ALU.add).then_inc(v_ok, 1)
                if Eb and among_first(Eb, 2) and Eb.b == 1:
                    for i in range(WP):
                        load_w(0, i)
                if S and among_first(S, NB) and S.b == NB - 1:
                    for i in range(WP):
                        load_w(1, i)

            iterations(po, one)

            po.wait_ge(tab_ok, 1)
            cut(1, 1)
            for k in range(2, NX + 1):
                te = po.value_load(tab[0:1, T_E + k - 2:T_E + k - 1], min_val=2, max_val=NT)
                cut(k, k % 2, te)
            total = po.value_load(tab[0:1, T_E + NX - 1:T_E + NX], min_val=2 * NX, max_val=NT)
            with po.Fori(0, NST // 2) as jj:
                for p in range(2):
                    po.wait_ge(y_st, total * 16)
                    po.wait_ge(ig_ok, 2 * jj + (1 + p))
                    carry(2 * jj + (NB + p))
                    for k, dst in enumerate((yga, ygb)):
                        po.indirect_dma_start(
                            out=dst[p][:, :], out_offset=None, in_=ys_d,
                            in_offset=bass.IndirectOffsetOnAxis(ap=ig[p][:, k:k + 1].bitcast(U32), axis=0)).then_inc(yg_in[p], 16)


LINKS_PER_LOOP = 3 * 17


def kernel(**inputs):
    import numpy as _np
    import concourse.bacc as _bacc
    from concourse import mybir as _mybir
    from concourse.bass_utils import run_bass_kernel_spmd as _run

    a = {k: _np.asarray(v) for k, v in inputs.items()}
    P_ = 128

    def chunks(w):
        return w.reshape(-1, P_, w.shape[-1]).transpose(1, 0, 2)

    def rows(v):
        return _np.broadcast_to(v[None, :], (P_, v.shape[0]))

    wT = _np.stack([chunks(a["L0_xattn_" + n].T) for n in ("Wq", "Wk", "Wv", "Wo")])
    experts = [(a["L0_ffn_w1"][e], a["L0_ffn_w3"][e], a["L0_ffn_w2"][e]) for e in range(8)]
    experts.append((a["L0_ffn_ws1"], a["L0_ffn_ws3"], a["L0_ffn_ws2"]))
    wall = _np.stack([_np.concatenate([chunks(m).reshape(P_, -1) for m in e], axis=1) for e in experts])
    arrays = {
        "x": a["x"],
        "ctxT": a["ctx_1024"].transpose(0, 2, 1),
        "gates": rows(_np.concatenate([a["g_xattn"], a["g_ffn"]])),
        "wT": wT,
        "bqk": _np.concatenate([a["L0_xattn_bq"].reshape(2, P_), a["L0_xattn_bk"].reshape(2, P_)]).T,
        "bvo": _np.stack([rows(a["L0_xattn_bv"]), rows(a["L0_xattn_bo"])]),
        "wr": chunks(a["L0_ffn_w_router"]),
        "wall": wall,
        "cst": constants(),
    }
    arrays = {k: _np.ascontiguousarray(v) for k, v in arrays.items()}
    nc = _bacc.Bacc("TRN2", target_bir_lowering=False, num_devices=1)
    args = [nc.dram_tensor(k, v.shape, _mybir.dt.from_np(v.dtype), kind="ExternalInput").ap() for k, v in arrays.items()]
    o = nc.dram_tensor("out", (NTOK, E), _mybir.dt.float32, kind="ExternalOutput").ap()
    build(nc, *args, o)
    r = _run(nc, [arrays], core_ids=[0])
    return r.results[0]["out"].reshape(16, 256, 256)
```
